# Optimizing a Trainium2 kernel written in Bass

```python
import numpy as np
import jax
import jax.numpy as jnp

def _softmax(x, axis=-1):
    return jax.nn.softmax(x, axis=axis)

def _gelu(x):
    return jax.nn.gelu(x, approximate=True)

def _silu(x):
    return jax.nn.silu(x)

def _sigmoid(x):
    return jax.nn.sigmoid(x)

def _layernorm(x, axis=-1, eps=1e-05):
    m = jnp.mean(x, axis=axis, keepdims=True)
    v = jnp.var(x, axis=axis, keepdims=True)
    return (x - m) / jnp.sqrt(v + eps)

def _scatter_add(tgt, idx, src, axis=0):
    return tgt.at[idx].add(src)

def _segment_sum(src, seg, n):
    return jax.ops.segment_sum(src, seg, n)
kernel_name = 'mk_prb_d1_jaxref_r8_c63ea5'

def setup_inputs(seed: int=0):
    np.random.seed(seed)
    _w = jnp.asarray

    def _L0_attn_setup():
        import jax, jax.numpy as jnp
        import numpy as np
        N_HEAD = 16
        POWER = 4
        key = jax.random.key(seed)
        k0, k1, k2 = jax.random.split(key, 3)
        B, T, C = (2, 256, 128)
        x = jax.random.normal(k0, (B, T, C), dtype=jnp.float32)
        W_attn = jax.random.normal(k1, (C, 3 * C), dtype=jnp.float32) * 0.02
        b_attn = jnp.zeros((3 * C,), dtype=jnp.float32)
        W_proj = jax.random.normal(k2, (C, C), dtype=jnp.float32) * 0.02
        b_proj = jnp.zeros((C,), dtype=jnp.float32)
        score_gain = jnp.asarray(4.0, dtype=jnp.float32)
        return {'x': x, 'W_attn': W_attn, 'b_attn': b_attn, 'W_proj': W_proj, 'b_proj': b_proj, 'score_gain': score_gain}
    _L0_attn_in = _L0_attn_setup()

    def _L0_ffn_setup():
        import jax, jax.numpy as jnp
        import numpy as np
        B, S, H = (2, 128, 128)
        DFF = 256
        E = 8
        TOPK = 2

        def _expert_ffn(x, w1, b1, w2, b2, wg, bg, w3, b3):
            x1 = jnp.einsum('bsh,hf->bsf', x, w1) + b1
            x2 = jnp.einsum('bsh,hf->bsf', x, w2) + b2
            z = x1 * x2
            s = jax.nn.silu(jnp.einsum('bsf,fg->bsg', z, wg) + bg)
            return jnp.einsum('bsg,gh->bsh', s, w3) + b3
        key = jax.random.key(seed)
        ks = jax.random.split(key, 12)
        sc = 0.02
        return {'x': jax.random.normal(ks[0], (B, S, H), jnp.float32), 'gate_w': jax.random.normal(ks[1], (H, E), jnp.float32) * sc, 'gate_b': jnp.zeros((E,), jnp.float32), 'w1': jax.random.normal(ks[2], (E, H, DFF), jnp.float32) * sc, 'b1': jnp.zeros((E, DFF), jnp.float32), 'w2': jax.random.normal(ks[3], (E, H, DFF), jnp.float32) * sc, 'b2': jnp.zeros((E, DFF), jnp.float32), 'wg': jax.random.normal(ks[4], (E, DFF, DFF), jnp.float32) * sc, 'bg': jnp.zeros((E, DFF), jnp.float32), 'w3': jax.random.normal(ks[5], (E, DFF, H), jnp.float32) * sc, 'b3': jnp.zeros((E, H), jnp.float32)}
    _L0_ffn_in = _L0_ffn_setup()
    _d = {'L0_attn_x': _L0_attn_in['x'], 'L0_attn_W_attn': _L0_attn_in['W_attn'], 'L0_attn_b_attn': _L0_attn_in['b_attn'], 'L0_attn_W_proj': _L0_attn_in['W_proj'], 'L0_attn_b_proj': _L0_attn_in['b_proj'], 'L0_attn_score_gain': _L0_attn_in['score_gain'], 'L0_ffn_gate_w': _L0_ffn_in['gate_w'], 'L0_ffn_gate_b': _L0_ffn_in['gate_b'], 'L0_ffn_w1': _L0_ffn_in['w1'], 'L0_ffn_b1': _L0_ffn_in['b1'], 'L0_ffn_w2': _L0_ffn_in['w2'], 'L0_ffn_b2': _L0_ffn_in['b2'], 'L0_ffn_wg': _L0_ffn_in['wg'], 'L0_ffn_bg': _L0_ffn_in['bg'], 'L0_ffn_w3': _L0_ffn_in['w3'], 'L0_ffn_b3': _L0_ffn_in['b3']}
    _x0 = _d['L0_attn_x']
    _d['L0_attn_x'] = jax.random.normal(jax.random.fold_in(jax.random.key(seed), 1), (4, 1024, 128), dtype=_x0.dtype)
    del _x0
    return _d

def reference(L0_attn_x, L0_attn_W_attn, L0_attn_b_attn, L0_attn_W_proj, L0_attn_b_proj, L0_attn_score_gain, L0_ffn_gate_w, L0_ffn_gate_b, L0_ffn_w1, L0_ffn_b1, L0_ffn_w2, L0_ffn_b2, L0_ffn_wg, L0_ffn_bg, L0_ffn_w3, L0_ffn_b3):

    def _L0_attn_ref(x, W_attn, b_attn, W_proj, b_proj, score_gain):
        import jax, jax.numpy as jnp
        import numpy as np
        N_HEAD = 16
        POWER = 4
        B, T, C = x.shape
        H = N_HEAD
        D = C // H
        qkv = x @ W_attn + b_attn
        q, k, v = jnp.split(qkv, 3, axis=-1)
        to_heads = lambda t: t.reshape(B, T, H, D).transpose(0, 2, 1, 3)
        q, k, v = (to_heads(q), to_heads(k), to_heads(v))
        s = jnp.einsum('bhtd,bhsd->bhts', q, k)
        s = s - s.mean(axis=-1, keepdims=True)
        mad = jnp.abs(s).mean(axis=-1, keepdims=True) + 1e-06
        s = s / mad * score_gain
        causal = jnp.tril(jnp.ones((T, T), dtype=bool))
        s = jnp.where(causal[None, None], s, jnp.asarray(-1000.0, s.dtype))
        r = jnp.maximum(s, 0.0) ** POWER
        att = r / (r.sum(axis=-1, keepdims=True) + 1e-06)
        y = jnp.einsum('bhts,bhsd->bhtd', att, v)
        y = y.transpose(0, 2, 1, 3).reshape(B, T, C)
        return y @ W_proj + b_proj

    def _L0_ffn_ref(x, gate_w, gate_b, w1, b1, w2, b2, wg, bg, w3, b3):
        import jax, jax.numpy as jnp
        import numpy as np
        B, S, H = (2, 128, 128)
        DFF = 256
        E = 8
        TOPK = 2

        def _expert_ffn(x, w1, b1, w2, b2, wg, bg, w3, b3):
            x1 = jnp.einsum('bsh,hf->bsf', x, w1) + b1
            x2 = jnp.einsum('bsh,hf->bsf', x, w2) + b2
            z = x1 * x2
            s = jax.nn.silu(jnp.einsum('bsf,fg->bsg', z, wg) + bg)
            return jnp.einsum('bsg,gh->bsh', s, w3) + b3
        logits = jnp.einsum('bsh,he->bse', x, gate_w) + gate_b
        topv, topi = jax.lax.top_k(logits, TOPK)
        probs = jax.nn.softmax(topv, axis=-1)
        out = jnp.zeros_like(x)
        for e in range(E):
            we = jnp.sum(probs * (topi == e), axis=-1)
            y = _expert_ffn(x, w1[e], b1[e], w2[e], b2[e], wg[e], bg[e], w3[e], b3[e])
            out = out + we[..., None] * y
        return out
    x = L0_attn_x
    xn = _layernorm(x, axis=-1)
    x = x + _L0_attn_ref(xn, L0_attn_W_attn, L0_attn_b_attn, L0_attn_W_proj, L0_attn_b_proj, L0_attn_score_gain) + _L0_ffn_ref(xn, L0_ffn_gate_w, L0_ffn_gate_b, L0_ffn_w1, L0_ffn_b1, L0_ffn_w2, L0_ffn_b2, L0_ffn_wg, L0_ffn_bg, L0_ffn_w3, L0_ffn_b3)
    return x

_drawn_inputs = setup_inputs


def setup_inputs(seed=0):
    import zlib

    import numpy as np

    out = dict(_drawn_inputs(seed))
    spreads = {'L0_attn_b_attn': (0.0, 2.0),
     'L0_attn_b_proj': (0.0, 0.592),
     'L0_ffn_gate_b': (0.0, 0.1),
     'L0_ffn_b1': (0.0, 0.8),
     'L0_ffn_b2': (0.0, 0.8),
     'L0_ffn_bg': (0.0, 0.703),
     'L0_ffn_b3': (0.0, 0.8)}
    factors = {'L0_attn_W_attn': 25.487,
     'L0_ffn_w1': 8.0,
     'L0_ffn_w2': 8.0,
     'L0_ffn_wg': 8.0,
     'L0_ffn_w3': 4.676,
     'L0_attn_W_proj': 4.838}
    for name, (base, spread) in spreads.items():
        noise = np.random.default_rng([zlib.crc32(name.encode()), seed]).standard_normal(out[name].shape)
        drawn = base * np.exp(spread * noise) if base else spread * noise
        out[name] = jnp.asarray(drawn.astype(out[name].dtype))
    for name, factor in factors.items():
        out[name] = (out[name] * factor).astype(out[name].dtype)
    return out
```

```python
from contextlib import ExitStack

import concourse.bass as bass
from concourse import mybir

F32 = mybir.dt.float32
BF16 = mybir.dt.bfloat16
I32 = mybir.dt.int32
ALU = mybir.AluOpType
ACT = mybir.ActivationFunctionType
AX = mybir.AxisListType.X

P = 128
LN_EPS = 1e-5
SMALL = 1e-6
HUGE = 1e30

HALF = 512
TERMS_Q = (0, 0, 1, 1, 0, 2)
TERMS_K = (0, 1, 0, 1, 2, 0)
VW = 10
SUM_R, SUM_U = 8, 9


def wait(engine, semaphore, value):
    if isinstance(value, int) and value <= 0:
        return
    engine.wait_ge(semaphore, value)


def layer_kernel(nc, x, w_attn, b_attn, w_proj, b_proj, score_gain, gate_w, gate_b,
                 w1, b1, w2, b2, wg, bg, w3, b3, out):
    B, T, C = x.shape
    E, _, F = w1.shape
    H = 16
    D = C // H
    N = B * T
    NT = N // P
    TB = T // P
    assert C == P and D == 8 and F == 2 * P
    TOPK = 2
    NX = -(-(N * TOPK + E * (P - 1)) // P)
    NX += NX % 2
    NQ = B * H // 4
    CH = T // HALF
    STEPS = [(c, j) for c in range(CH) for j in range(TB) if P * j < HALF * (c + 1)]
    NS = len(STEPS)
    NH = 2 * NS
    LOW = [max(0, P * j - HALF * c) for c, j in STEPS]
    DIAG = [P * j >= HALF * c for c, j in STEPS]
    ND = 2 * sum(DIAG)
    masks_to = lambda y: y // NH * ND + sum(DIAG[z // 2] for z in range(y % NH + 1))
    PIECES, MCOLS = [], TB - 1
    for g in range(4):
        short = []
        for n in range(TB - 1):
            k, w = P * (n + 1), T - P * (n + 1)
            if w < HALF:
                short.append((g, n, k, w, n))
                continue
            PIECES.append([(g, n, k, HALF, n)])
            if w > HALF:
                short.append((g, n, k + HALF, w - HALF, TB - 1 + n))
        while short:
            a = short.pop(0)
            fits = [b for b in short if a[3] + b[3] == HALF]
            short.remove(fits[0])
            PIECES.append([a, fits[0]])
    MCOLS += (TB - 1) // 2
    NP = len(PIECES)
    ENDS = [max(k for k in range(NS) if STEPS[k][0] == c) for c in range(CH)]
    LAST = [2 * max(k for k in range(NS) if STEPS[k][0] == c) + 1 for c in range(CH)]
    PIECE_AT = [m * 2 * NH // NP for m in range(NP)]
    PIECE_ACT = {4, 11, 18, 25}
    R_POOL = {6, 9, 12, 15, 17, 21, 23}
    RLAG, AVLAG = 2, 4
    NU, NR, NW, NSLOT = 8, 4, 4, 3
    LN_STEPS, ROUTE_M, ROUTE_EXP, ROUTE_STEPS = 9, 12, 13, 49
    NB, NW = 6, 4

    ctx = ExitStack()
    with ctx:
        def sb(name, shape, dt=F32):
            return ctx.enter_context(nc.sbuf_tensor(name, shape, dt))

        def sem(name):
            return ctx.enter_context(nc.semaphore(name))

        def dram(name, shape, dt=F32):
            return nc.dram_tensor(name, shape, dt, kind="Internal").ap()

        qk_d = dram("qk_parts", [2, B * P, 3, T], BF16)
        v_d = dram("v_stationary", [NQ, P, TB, 4 * VW])
        acc_d = dram("attention_sums", [B * H, VW, T])
        rec_d = dram("row_scale", [B * H, T])
        xs_d = dram("sorted_x", [NX * P, C])
        ys_d = dram("sorted_y", [NX * P, C])

        ident = sb("ident", [P, P])
        tri = sb("earlier", [P, P])
        ones = sb("ones", [P, P])
        causal = sb("causal", [P, P])
        usel = sb("usel", [P, VW])
        iota8 = sb("iota8", [P, E])
        iota_t = sb("iota_t", [P, NT])
        iota_x = sb("iota_x", [P, NX])
        wa = sb("wa", [P, 3 * C])
        wgate = sb("wgate", [P, E])
        wp = sb("wp", [P, C])
        bq = sb("bq", [P, 2])
        bq_s = sb("bq_s", [P, 1])
        bv = sb("bv", [P, TB, C])
        bgate = sb("bgate", [P, TB, E])
        bp = sb("bp", [P, C])
        gain = sb("gain", [P, 1])
        gsign = sb("gsign", [P, 3])
        w12 = sb("w12", [P, E, 2 * F])
        wgs = sb("wgs", [P, E, 2, F])
        w3s = sb("w3s", [P, E, 2, C])
        b12 = sb("b12", [P, E, 2 * F])
        bgs = sb("bgs", [P, E, F])
        b3s = sb("b3s", [P, E, C])
        xn = sb("xn", [P, NT, C])
        logit = sb("logit", [P, NT, E])
        prob = sb("prob", [P, NT, 2])
        pos = sb("pos", [P, 2, NT], I32)
        te = sb("te", [P, NX], I32)
        gate_v = sb("gate_v", [P, 1])
        msum = sb("msum", [P, NQ, 4, MCOLS])

        bank = [ctx.enter_context(nc.psum_tensor(f"bank{i}", [P, 2, HALF], F32)) for i in range(4)]

        c_pool, c_vec = sem("constants_pool"), sem("constants_vec")
        w_in, w_ffn = sem("small_weights_in"), sem("ffn_weights_in")
        x_in = sem("x_in")
        s_gain = sem("gain_sign")
        ln_v, ln_s = sem("ln_vector"), sem("ln_sqrt")
        xnb_ready, tr_done, xnT_ready = sem("xnb_ready"), sem("xn_transposed"), sem("xnT_ready")
        q_mm, k_mm, v_mm, g_mm = sem("q_mm"), sem("k_mm"), sem("v_mm"), sem("gate_mm")
        qk_f = sem("qk_float_ready")
        v_ev, k_c = sem("v_evacuated"), sem("k_centred")
        part_a, part_v = sem("part_rounded"), sem("part_rest")
        part_out, v_out = sem("parts_stored"), sem("v_stored")
        route, r_mm, r_exp = sem("route"), sem("route_mm"), sem("route_exp")
        z_out, xs_out = sem("xs_zeroed"), sem("xs_scattered")
        qk_in = [sem("quad_in0"), sem("quad_in1")]
        s_ready, u_ready, w_done, w_mask = sem("scores_ready"), sem("u_ready"), sem("w_done"), sem("w_masked")
        r_ready = [sem(f"r_ready{i}") for i in range(NR)]
        r_used, u_used = sem("r_used"), sem("u_used")
        acc_ev = sem("acc_evacuated")
        y_out = [sem("sums_stored0"), sem("sums_stored1")]
        p_ready, p_used = sem("piece_ready"), sem("piece_used")
        fx = [sem("ffn_x_in0"), sem("ffn_x_in1")]
        fy = [sem("ffn_y_out0"), sem("ffn_y_out1")]
        f = {n: sem("ffn_" + n) for n in
             ("tx", "cx", "mx", "bx", "z", "tz", "cz", "mg", "bg", "sl", "ts", "cs", "my", "by")}
        m_row = sem("piece_sums_by_row")
        fin_in, fin_v, ms_t, rec_out = sem("final_in"), sem("final_vec"), sem("ms_transposed"), sem("rec_stored")
        y_in, yn_ready, proj = [sem("y_in0"), sem("y_in1")], sem("yn_ready"), sem("proj")
        gathered, res_half, res_out = sem("gathered"), sem("result_half"), sem("result_out")

        phase = ExitStack()

        def tmp(name, shape, dt=F32):
            return phase.enter_context(nc.sbuf_tensor(name, shape, dt))

        x_t = tmp("x_t", [P, NT, C])
        st = tmp("st", [P, TB, 6])
        mv = tmp("mv", [P, TB, 2])
        lnw = tmp("lnw", [P, 5, TB])
        xnb = tmp("xnb", [P, TB, C])
        xnT = tmp("xnT", [P, T])
        qf = tmp("qf", [P, 2, T])
        ksum = tmp("ksum", [P, 4])
        rest = tmp("rest", [P, 2, T])
        parts = tmp("parts", [P, 2, 3, T], BF16)
        vb = tmp("vb", [P, 4, TB, 4, VW])
        rt = [tmp(f"rt{i}", [P, NT, E]) for i in range(6)]
        rs = tmp("rs", [P, 12, NT])
        rx = tmp("rx", [P, NX, E])
        rxs = tmp("rxs", [P, NX])
        rc = tmp("rc", [P, E, NT])
        rce = tmp("rce", [P, 4, E])
        phase.close()

        QS = [tmp(f"QS{i}", [P, 2, T], BF16) for i in range(2)]
        KS = [tmp(f"KS{i}", [P, 2, T], BF16) for i in range(2)]
        VS = [tmp(f"VS{i}", [P, TB, 4, VW]) for i in range(2)]
        U = [tmp(f"U{i}", [P, 2, HALF]) for i in range(NU)]
        R = [tmp(f"R{i}", [P, 2, HALF]) for i in range(NR)]
        W = [tmp(f"W{i}", [P, 2, HALF]) for i in range(NW)]
        yq = [tmp(f"yq{i}", [P, CH, HALF]) for i in range(2)]
        junk_a, junk_v = tmp("junk_a", [P, HALF], BF16), tmp("junk_v", [P, HALF], BF16)
        phase.close()

        xt = [tmp(f"xt{i}", [P, C]) for i in range(2)]
        xT = [tmp(f"xT{i}", [P, C]) for i in range(2)]
        xb = [tmp(f"xb{i}", [P, 2 * F]) for i in range(2)]
        zb = [tmp(f"zb{i}", [P, F]) for i in range(2)]
        zT = [tmp(f"zT{i}", [P, 2, P]) for i in range(2)]
        gb = [tmp(f"gb{i}", [P, F]) for i in range(2)]
        sg = [tmp(f"sg{i}", [P, F]) for i in range(2)]
        sT = [tmp(f"sT{i}", [P, 2, P]) for i in range(2)]
        yb = [tmp(f"yb{i}", [P, C]) for i in range(2)]
        mrow = tmp("mrow", [P, TB, B * H])
        sums = tmp("sums", [B * H, 2, T])
        fw = tmp("fw", [B * H, 3, T])
        yT = [tmp(f"yT{i}", [P, T]) for i in range(2)]
        rb = [tmp(f"rb{i}", [P, T]) for i in range(2)]
        xr = tmp("xr", [P, NT, C])
        gat = tmp("gat", [P, 2, NT, C])
        phase.close()

        x_v = x.rearrange("b (t p) c -> p (b t) c", p=P)
        out_v = out.rearrange("b (t p) c -> p (b t) c", p=P)
        row = lambda v: v.rearrange("(a n) -> a n", a=1)
        acc_q = acc_d.rearrange("(q g) r t -> q g r t", g=4)
        qk_q = qk_d.rearrange("s (q hh r d) part t -> s q r part d hh t", hh=2, r=2, d=D)

        def rows_of(ap, n):
            return ap.to_broadcast([P, n])

        block = ctx.enter_context(nc.Block())

        @block.sync
        def _(sp):
            for b in range(B):
                sp.dma_start(x_t[:, b * TB:(b + 1) * TB, :], x_v[:, b * TB:(b + 1) * TB, :]).then_inc(x_in, 16)
            sp.dma_start(wa[:, :], w_attn).then_inc(w_in, 16)
            sp.dma_start(wgate[:, :], gate_w).then_inc(w_in, 16)
            sp.dma_start(wp[:, :], w_proj).then_inc(w_in, 16)
            for s in range(2):
                sp.dma_start(bq[:, s:s + 1], b_attn[s * C:(s + 1) * C].rearrange("(p a) -> p a", a=1)).then_inc(w_in, 16)
            for t in range(TB):
                sp.dma_start(bv[:, t, :], rows_of(row(b_attn[2 * C:3 * C]), C)).then_inc(w_in, 16)
                sp.dma_start(bgate[:, t, :], rows_of(row(gate_b), E)).then_inc(w_in, 16)
            sp.dma_start(bp[:, :], rows_of(row(b_proj), C)).then_inc(w_in, 16)
            sp.dma_start(gain[:, :], rows_of(score_gain, 1)).then_inc(w_in, 16)
            sp.wait_ge(c_vec, 1)
            zero_rows = xs_d.rearrange("(k p) c -> p k c", p=P)
            for k in range(0, NX, NX // 8):
                sp.dma_start(zero_rows[:, k:k + NX // 8, :],
                             w12[:, 0:1, 0:C].to_broadcast([P, NX // 8, C])).then_inc(z_out, 16)
            with sp.Fori(0, B) as b:
                for s in range(2):
                    sp.wait_ge(part_a, 6 * b + (5 + s))
                    sp.dma_start(qk_d[s, bass.ts(b, P), :, :], parts[:, s, :, :]).then_inc(part_out, 16)
                sp.wait_ge(v_ev, b + 1)
                for hq in range(4):
                    sp.dma_start(v_d[b * 4 + hq].rearrange("p t n -> p (t n)"),
                                 vb[:, hq].rearrange("p t g n -> p (t g n)")).then_inc(v_out, 16)
            sp.wait_ge(z_out, 16 * 8)
            for e in range(E):
                sp.dma_start(w12[:, e, 0:F], w1[e]).then_inc(w_ffn, 16)
                sp.dma_start(w12[:, e, F:2 * F], w2[e]).then_inc(w_ffn, 16)
                sp.dma_start(wgs[:, e, :, :], wg[e].rearrange("(k p) n -> p k n", p=P)).then_inc(w_ffn, 16)
                sp.dma_start(w3s[:, e, :, :], w3[e].rearrange("(k p) n -> p k n", p=P)).then_inc(w_ffn, 16)
                sp.dma_start(b12[:, e, 0:F], rows_of(b1[e:e + 1], F)).then_inc(w_ffn, 16)
                sp.dma_start(b12[:, e, F:2 * F], rows_of(b2[e:e + 1], F)).then_inc(w_ffn, 16)
                sp.dma_start(bgs[:, e, :], rows_of(bg[e:e + 1], F)).then_inc(w_ffn, 16)
                sp.dma_start(b3s[:, e, :], rows_of(b3[e:e + 1], C)).then_inc(w_ffn, 16)

            def load_quad(q, par):
                for r in range(2):
                    for s, (dst, terms) in enumerate(((QS, TERMS_Q), (KS, TERMS_K))):
                        for k, part in enumerate(terms):
                            sp.dma_start(dst[par][64 * r + D * k:64 * r + D * (k + 1), :, :],
                                         qk_q[s, q, r, part]).then_inc(qk_in[par], 16)
                sp.dma_start(VS[par][:, :, :, :].rearrange("p t g n -> p t (g n)"), v_d[q]).then_inc(qk_in[par], 16)

            def store_quad(q, i, par):
                sp.wait_ge(acc_ev, (q + 1) * CH)
                for g in range(4):
                    sp.dma_start(acc_q[q, g], yq[par][32 * g:32 * g + VW, :, :].rearrange("p c n -> p (c n)"),
                                 ).then_inc(y_out[par], 16)

            sp.wait_ge(part_out, 16 * 2 * B)
            sp.wait_ge(v_out, 16 * 4 * B)
            sp.wait_ge(route, ROUTE_STEPS)
            load_quad(0, 0)
            load_quad(1, 1)
            with sp.Fori(0, NQ // 2 - 1) as i:
                for par in range(2):
                    store_quad(i * 2 + par, i, par)
                    sp.wait_ge(u_used, (i * 2 + (par + 1)) * NH)
                    load_quad(i * 2 + (par + 2), par)
            for par in range(2):
                store_quad(NQ - 2 + par, NQ // 2 - 1, par)
            for par in range(2):
                sp.wait_ge(y_out[par], 16 * 4 * NQ // 2)

            sp.wait_ge(xs_out, 16 * 2 * NT)
            sp.wait_ge(p_used, NP * NQ)
            xs_t = xs_d.rearrange("(k p) c -> k p c", p=P)

            def ffn_sp(i, par):
                wait(sp, f["tx"], i - 1)
                sp.dma_start(xt[par][:, :], xs_t[i]).then_inc(fx[par], 16)

            for i in range(2):
                ffn_sp(i, i)
            with sp.Fori(1, NX // 2) as t:
                for par in range(2):
                    ffn_sp(t * 2 + par, par)
            for par in range(2):
                sp.wait_ge(fy[par], 16 * NX // 2)

            sp.dma_start(xr[:, :, :], x_v).then_inc(fin_in, 16)
            sp.dma_start(sums[:, 0, :], acc_d[:, SUM_R, :]).then_inc(fin_in, 16)
            sp.dma_start(sums[:, 1, :], acc_d[:, SUM_U, :]).then_inc(fin_in, 16)
            sp.wait_ge(fin_v, 7)
            sp.dma_start(rec_d, fw[:, 0, :]).then_inc(rec_out, 16)
            sp.wait_ge(rec_out, 16)
            for b in range(B):
                if b >= 2:
                    sp.wait_ge(proj, 2 * (b - 1))
                for h in range(H):
                    sp.dma_start(yT[b % 2][D * h:D * (h + 1), :], acc_d[b * H + h, 0:D, :]).then_inc(y_in[b % 2], 16)
                    sp.dma_start(rb[b % 2][D * h:D * (h + 1), :],
                                 rec_d[b * H + h:b * H + h + 1, :].to_broadcast([D, T])).then_inc(y_in[b % 2], 16)
                if b >= 1:
                    sp.wait_ge(res_half, 2 * b)
                    sp.dma_start(out_v[:, (b - 1) * TB:b * TB, :], xr[:, (b - 1) * TB:b * TB, :]).then_inc(res_out, 16)
            sp.wait_ge(res_half, 2 * B)
            sp.dma_start(out_v[:, (B - 1) * TB:, :], xr[:, (B - 1) * TB:, :]).then_inc(res_out, 16)
            sp.wait_ge(res_out, 16 * B)

        @block.gpsimd
        def _(pool):
            pool.memset(ident[:, :], 0.0).then_inc(c_pool, 1)
            pool.memset(tri[:, :], 0.0).then_inc(c_pool, 1)
            pool.memset(ones[:, :], 1.0).then_inc(c_pool, 1)
            pool.wait_ge(c_pool, 3)
            pool.affine_select(out=ident[:, :], in_=ident[:, :], compare_op=ALU.not_equal, fill=1.0, base=0,
                               pattern=[[-1, P]], channel_multiplier=1).then_inc(c_pool, 1)
            pool.affine_select(out=tri[:, :], in_=ones[:, :], compare_op=ALU.is_gt, fill=0.0, base=0,
                               pattern=[[1, P]], channel_multiplier=-1).then_inc(c_pool, 1)
            pool.affine_select(out=causal[:, :], in_=ones[:, :], compare_op=ALU.is_ge, fill=0.0, base=0,
                               pattern=[[1, P]], channel_multiplier=-1).then_inc(c_pool, 1)
            pool.iota(iota8[:, :], [[1, E]], base=-E, channel_multiplier=0,
                      allow_small_or_imprecise_dtypes=True).then_inc(c_pool, 1)
            pool.iota(iota_t[:, :], [[P, NT]], base=0, channel_multiplier=0,
                      allow_small_or_imprecise_dtypes=True).then_inc(c_pool, 1)
            pool.iota(iota_x[:, :], [[1, NX]], base=0, channel_multiplier=0,
                      allow_small_or_imprecise_dtypes=True).then_inc(c_pool, 1)
            pool.wait_ge(c_pool, 9)
            pool.wait_ge(z_out, 16 * 8)
            pool.wait_ge(route, ROUTE_STEPS)
            for k in range(TOPK):
                for t in range(NT):
                    pool.indirect_dma_start(xs_d, bass.IndirectOffsetOnAxis(pos[:, k, t:t + 1], 0),
                                            xn[:, t, :], None).then_inc(xs_out, 16)

            def attention_pool(i, first, drain):
                for x in range(2 * NH):
                    if not drain and DIAG[x % NH // 2]:
                        pool.wait_ge(w_done, i * (2 * NH) + (x + 1))
                        pool.tensor_tensor(W[x % NW][:, :, 0:P], W[x % NW][:, :, 0:P],
                                           causal[:, :].unsqueeze(1).to_broadcast([P, 2, P]),
                                           ALU.mult).then_inc(w_mask, 1)
                    y = x - 1
                    if (y < 0 and first) or (y >= 0 and drain) or y % NH not in R_POOL:
                        continue
                    w = HALF - LOW[y % NH // 2]
                    if DIAG[y % NH // 2]:
                        pool.wait_ge(w_mask, i * (2 * ND) + masks_to(y))
                    else:
                        pool.wait_ge(w_done, i * (2 * NH) + (y + 1))
                    wait(pool, r_used, i * (2 * NH) + (y - NR + 1))
                    pool.tensor_tensor(R[y % NR][:, :, 0:w], W[y % NW][:, :, 0:w], W[y % NW][:, :, 0:w],
                                       ALU.mult).then_inc(r_ready[y % NR], 1)

            attention_pool(0, True, False)
            with pool.Fori(1, NQ // 2) as i:
                attention_pool(i, False, False)
            attention_pool(NQ // 2, False, True)

            for par in range(2):
                pool.wait_ge(fy[par], 16 * NX // 2)
            for t in range(NT):
                for k in range(TOPK):
                    pool.indirect_dma_start(gat[:, k, t, :], None, ys_d,
                                            bass.IndirectOffsetOnAxis(pos[:, k, t:t + 1], 0)).then_inc(gathered, 16)

        @block.scalar
        def _(act):
            act.wait_ge(w_in, 16 * (7 + 2 * TB))
            act.activation(gsign[:, 0:1], gain[:, :], ACT.Sign).then_inc(s_gain, 1)
            act.activation(gsign[:, 1:2], gain[:, :], ACT.Abs).then_inc(s_gain, 1)
            with act.Fori(0, B) as b:
                act.wait_ge(ln_v, b * LN_STEPS + 3)
                act.activation(lnw[:, 1, :], lnw[:, 0, :], ACT.Sqrt).then_inc(ln_s, 1)
            act.wait_ge(s_gain, 3)
            with act.Fori(0, B) as b:
                act.wait_ge(ln_v, (b + 1) * LN_STEPS)
                wait(act, tr_done, b)
                act.copy(xnb[:, :, :], xn[:, bass.ts(b, TB), :]).then_inc(xnb_ready, 1)
                act.wait_ge(tr_done, b + 1)
                act.copy(xnT[:, :], bank[0][:, :, :].rearrange("p a n -> p (a n)")).then_inc(xnT_ready, 1)
                act.wait_ge(q_mm, b + 1)
                act.activation(qf[:, 0, :], bank[1][:, :, :].rearrange("p a n -> p (a n)"), ACT.Identity,
                               scale=gsign[:, 0:1], bias=bq_s[:, 0:1]).then_inc(qk_f, 1)
                act.wait_ge(k_mm, b + 1)
                act.activation(qf[:, 1, :], bank[2][:, :, :].rearrange("p a n -> p (a n)"), ACT.Identity,
                               bias=bq[:, 1:2], accum_out=ksum[:, 0:1]).then_inc(qk_f, 1)
                for n in range(3):
                    for s in range(2):
                        if n == 0 and s == 0:
                            act.wait_ge(qk_f, b * 2 + 1)
                            wait(act, part_out, b * 32)
                        if n == 0 and s == 1:
                            act.wait_ge(k_c, b * 2 + 2)
                        if n:
                            act.wait_ge(part_v, b * 4 + (2 * n - 1 + s))
                        act.copy(parts[:, s, n, :], rest[:, s, :] if n else qf[:, s, :]).then_inc(part_a, 1)
            act.wait_ge(route, ROUTE_EXP)
            act.activation(rs[:, 5, :], rs[:, 4, :], ACT.Exp).then_inc(r_exp, 1)

            def attention_act(i, first, drain):
                for x in range(2 * NH):
                    par, h = divmod(x, NH)
                    if not drain:
                        w = HALF - LOW[h // 2]
                        act.wait_ge(s_ready, i * (2 * NH) + (x + 1))
                        wait(act, u_used, i * (2 * NH) + (x - NU + 1))
                        act.activation(U[x % NU][:, :, 0:w], bank[x % NSLOT][:, :, 0:w], ACT.Relu).then_inc(u_ready, 1)
                    z = x - AVLAG - 1
                    if z % NH in LAST and not ((z < 0 and first) or (z >= 0 and drain)):
                        q = i * 2 + z // NH
                        act.wait_ge(u_used, i * (2 * NH) + (z + 1))
                        if not (isinstance(q, int) and q < 2):
                            act.wait_ge(y_out[z // NH % 2], 64 * (i + z // NH // 2))
                        act.copy(yq[z // NH % 2][:, STEPS[z % NH // 2][0], :], bank[3][:, 0, :]).then_inc(acc_ev, 1)
                    y = x - RLAG
                    if not ((y < 0 and first) or (y >= 0 and drain)) and y % NH not in R_POOL:
                        w = HALF - LOW[y % NH // 2]
                        if DIAG[y % NH // 2]:
                            act.wait_ge(w_mask, i * (2 * ND) + masks_to(y))
                        else:
                            act.wait_ge(w_done, i * (2 * NH) + (y + 1))
                        wait(act, r_used, i * (2 * NH) + (y - NR + 1))
                        act.activation(R[y % NR][:, :, 0:w], W[y % NW][:, :, 0:w], ACT.Square,
                                       ).then_inc(r_ready[y % NR], 1)
                    for m in range(NP):
                        if not drain and (PIECE_AT[m] + 1) // 2 == h and m in PIECE_ACT:
                            q = i * 2 + par
                            act.wait_ge(p_ready, q * NP + (m + 1))
                            at = 0
                            for g, n, k, w, col in PIECES[m]:
                                last = act.activation(junk_a[:, at:at + w], bank[3][:, 1, at:at + w], ACT.Relu,
                                                      accum_out=msum_at(q, g, col))
                                at += w
                            last.then_inc(p_used, 1)

            def msum_at(q, g, col):
                return msum[:, q, g, col:col + 1] if isinstance(q, int) else msum[:, bass.ds(q, 1), g, col]

            attention_act(0, True, False)
            with act.Fori(1, NQ // 2) as i:
                attention_act(i, False, False)
            attention_act(NQ // 2, False, True)

            act.wait_ge(p_used, NP * NQ)
            for par in range(2):
                act.wait_ge(y_out[par], 16 * 4 * NQ // 2)

            ys_t = ys_d.rearrange("(k p) c -> k p c", p=P)

            def ffn_act(i, par, lo, hi):
                o = 1 - par
                if lo >= 6:
                    act.wait_ge(f["by"], i - 5)
                    act.dma_start(ys_t[i - 6], yb[par][:, :]).then_inc(fy[par], 16)
                if lo >= 0 and hi > 0:
                    act.wait_ge(f["tx"], i + 1)
                    wait(act, f["mx"], i - 1)
                    act.copy(xT[par][:, :], bank[0][:, 0, 0:P]).then_inc(f["cx"], 1)
                if lo >= 2 and hi > -2:
                    act.wait_ge(f["tz"], i - 1)
                    wait(act, f["mg"], i - 3)
                    act.copy(zT[par][:, :, :].rearrange("p a n -> p (a n)"), bank[1][:, 0, 0:F]).then_inc(f["cz"], 1)
                if lo >= 3 and hi > -3:
                    act.wait_ge(f["bg"], i - 2)
                    wait(act, f["ts"], i - 4)
                    act.activation(sg[o][:, :], gb[o][:, :], ACT.Silu).then_inc(f["sl"], 1)
                if lo >= 4 and hi > -4:
                    act.wait_ge(f["ts"], i - 3)
                    wait(act, f["my"], i - 5)
                    act.copy(sT[par][:, :, :].rearrange("p a n -> p (a n)"), bank[2][:, 0, 0:F]).then_inc(f["cs"], 1)

            for i in range(6):
                ffn_act(i, i % 2, i, 1)
            with act.Fori(3, NX // 2) as t:
                for par in range(2):
                    ffn_act(t * 2 + par, par, 9, 1)
            for i in range(NX, NX + 6):
                ffn_act(i, i % 2, 9, NX - i)

        @block.tensor
        def _(pe):
            pe.wait_ge(c_pool, 9)
            pe.wait_ge(w_in, 16 * (7 + 2 * TB))
            flat = [bk[:, :, :].rearrange("p a n -> p (a n)") for bk in bank]
            with pe.Fori(0, B) as b:
                pe.wait_ge(xnb_ready, b + 1)
                wait(pe, v_ev, b * 1)
                for t in range(TB):
                    last = pe.transpose(flat[0][:, t * P:(t + 1) * P], xnb[:, t, :], ident[:, :])
                last.then_inc(tr_done, 1)
                pe.wait_ge(xnT_ready, b + 1)
                for s, done in ((0, q_mm), (1, k_mm)):
                    for c in range(CH):
                        last = pe.matmul(bank[1 + s][:, c, :], wa[:, s * C:(s + 1) * C],
                                         xnT[:, c * HALF:(c + 1) * HALF], start=True, stop=True)
                    last.then_inc(done, 1)
                for t in range(TB):
                    last = pe.matmul(flat[3][:, t * P:(t + 1) * P], xnT[:, t * P:(t + 1) * P],
                                     wa[:, 2 * C:3 * C], start=True, stop=True)
                last.then_inc(v_mm, 1)
                for t in range(TB):
                    last = pe.matmul(flat[0][:, t * E:(t + 1) * E], xnT[:, t * P:(t + 1) * P], wgate[:, :],
                                     start=True, stop=True)
                last.then_inc(g_mm, 1)
            pe.wait_ge(route, ROUTE_M)
            m_all = rt[4][:, :, :].rearrange("p t e -> p (t e)")
            pe.matmul(bank[3][:, 0, 0:NT * E], tri[:, :], m_all, start=True, stop=True).then_inc(r_mm, 1)
            pe.matmul(bank[3][:, 1, 0:NT * E], ones[:, :], m_all, start=True, stop=True).then_inc(r_mm, 1)

            def attention_pe(i, first, drain):
                for x in range(2 * NH):
                    par, h = divmod(x, NH)

                    def pieces(at_half):
                        for m in range(NP):
                            if not drain and PIECE_AT[m] == 2 * h + at_half:
                                wait(pe, p_used, (i * 2 + par) * NP + m)
                                at = 0
                                for g, n, k, w, _ in PIECES[m]:
                                    rows = slice(64 * (g % 2), 64 * (g % 2) + 6 * D)
                                    last = pe.matmul(bank[3][:, 1, at:at + w], QS[par][rows, g // 2, P * n:P * (n + 1)],
                                                     KS[par][rows, g // 2, k:k + w], start=True, stop=True)
                                    at += w
                                last.then_inc(p_ready, 1)

                    if not drain:
                        c, j = STEPS[h // 2]
                        lo, p = LOW[h // 2], h % 2
                        if h == 0:
                            pe.wait_ge(qk_in[par], (i + 1) * (16 * 25))
                        wait(pe, w_done, i * (2 * NH) + (x - NSLOT + 1))
                        for r in range(2):
                            rows = slice(64 * r, 64 * r + 6 * D)
                            last = pe.matmul(bank[x % NSLOT][:, r, 0:HALF - lo], KS[par][rows, p, P * j:P * (j + 1)],
                                             QS[par][rows, p, HALF * c + lo:HALF * (c + 1)], start=True, stop=True)
                        last.then_inc(s_ready, 1)
                    pieces(0)
                    y, z = x - AVLAG, x - AVLAG - 1
                    has_r = not ((y < 0 and first) or (y >= 0 and drain))
                    has_u = not ((z < 0 and first) or (z >= 0 and drain))
                    if has_r:
                        pe.wait_ge(r_ready[y % NR], i * (2 * NH // NR) + (y // NR + 1))
                    if has_u:
                        average(z, U[z % NU], True).then_inc(u_used, 1)
                    if has_r:
                        if STEPS[y % NH // 2][1] == 0 and y % 2 == 0:
                            wait(pe, acc_ev, i * (2 * CH) + (y // NH * CH + STEPS[y % NH // 2][0]))
                        average(y, R[y % NR], False).then_inc(r_used, 1)
                    pieces(1)

            def average(y, src, of_u):
                c, j = STEPS[y % NH // 2]
                lo = LOW[y % NH // 2]
                for r in range(2):
                    g = y % 2 * 2 + r
                    last = pe.matmul(bank[3][32 * g:32 * g + VW, 0, lo:HALF],
                                     usel[:, :] if of_u else VS[y // NH % 2][:, j, g, :], src[:, r, 0:HALF - lo],
                                     start=(j == 0 and not of_u), stop=(y % NH // 2 in ENDS and of_u),
                                     skip_group_check=True)
                return last

            pe.wait_ge(part_a, 6 * B)
            pe.wait_ge(route, ROUTE_STEPS)
            attention_pe(0, True, False)
            with pe.Fori(1, NQ // 2) as i:
                attention_pe(i, False, False)
            attention_pe(NQ // 2, False, True)

            pe.wait_ge(p_used, NP * NQ)
            pe.wait_ge(w_ffn, 16 * 8 * E)

            def expert(k):
                return pe.value_load(te[0:1, k:k + 1] if isinstance(k, int) else te[0:1, bass.ds(k, 1)],
                                     min_val=0, max_val=E - 1)

            def ffn_pe(i, t, par, lo, hi):
                o = 1 - par
                if hi > 0:
                    pe.wait_ge(fx[par], (t + 1) * 16)
                    wait(pe, f["cx"], i)
                    pe.transpose(bank[0][:, 0, 0:P], xt[par][:, :], ident[:, :]).then_inc(f["tx"], 1)
                if lo >= 1 and hi > -1:
                    e = expert(i - 1)
                    pe.wait_ge(f["cx"], i)
                    wait(pe, f["bx"], i - 1)
                    pe.matmul(bank[0][:, 1, :], xT[o][:, :], w12[:, bass.ds(e, 1), :].rearrange("p a n -> p (a n)"),
                              start=True, stop=True).then_inc(f["mx"], 1)
                if lo >= 2 and hi > -2:
                    pe.wait_ge(f["z"], i - 1)
                    wait(pe, f["cz"], i - 2)
                    for k in range(2):
                        last = pe.transpose(bank[1][:, 0, k * P:(k + 1) * P], zb[par][:, k * P:(k + 1) * P], ident[:, :])
                    last.then_inc(f["tz"], 1)
                if lo >= 3 and hi > -3:
                    e = expert(i - 3)
                    pe.wait_ge(f["cz"], i - 2)
                    wait(pe, f["bg"], i - 3)
                    for k in range(2):
                        last = pe.matmul(bank[1][:, 1, 0:F], zT[o][:, k, :],
                                         wgs[:, bass.ds(e, 1), k, :].rearrange("p a n -> p (a n)"),
                                         start=(k == 0), stop=(k == 1))
                    last.then_inc(f["mg"], 1)
                if lo >= 4 and hi > -4:
                    pe.wait_ge(f["sl"], i - 3)
                    wait(pe, f["cs"], i - 4)
                    for k in range(2):
                        last = pe.transpose(bank[2][:, 0, k * P:(k + 1) * P], sg[par][:, k * P:(k + 1) * P], ident[:, :])
                    last.then_inc(f["ts"], 1)
                if lo >= 5:
                    e = expert(i - 5)
                    pe.wait_ge(f["cs"], i - 4)
                    wait(pe, f["by"], i - 5)
                    for k in range(2):
                        last = pe.matmul(bank[2][:, 1, 0:C], sT[o][:, k, :],
                                         w3s[:, bass.ds(e, 1), k, :].rearrange("p a n -> p (a n)"),
                                         start=(k == 0), stop=(k == 1))
                    last.then_inc(f["my"], 1)

            for i in range(6):
                ffn_pe(i, i // 2, i % 2, i, 1)
            with pe.Fori(3, NX // 2) as t:
                for par in range(2):
                    ffn_pe(t * 2 + par, t, par, 9, 1)
            for i in range(NX, NX + 5):
                ffn_pe(i, i // 2, i % 2, 9, NX - i)

            pe.wait_ge(acc_ev, CH * NQ)
            pe.wait_ge(m_row, 1)
            for n in range(TB):
                last = pe.transpose(bank[3][0:B * H, n // 4, n % 4 * P:(n % 4 + 1) * P], mrow[:, n, :], ident[:, :])
            last.then_inc(ms_t, 1)
            for b in range(B):
                pe.wait_ge(yn_ready, b + 1)
                for hb in range(2):
                    n = 2 * b + hb
                    if n >= 2:
                        pe.wait_ge(res_half, n - 1)
                    for t in range(4):
                        k = hb * 4 + t
                        last = pe.matmul(bank[1 + hb][:, 0, t * C:(t + 1) * C], yT[b % 2][:, k * P:(k + 1) * P],
                                         wp[:, :], start=True, stop=True)
                    last.then_inc(proj, 1)


        @block.vector
        def _(vec):
            vec.memset(w12[:, 0, 0:C], 0.0).then_inc(c_vec, 1)
            vec.memset(usel[:, :], 0.0).then_inc(c_vec, 1)
            vec.memset(vb[:, :, :, :, :], 0.0).then_inc(c_vec, 1)
            vec.memset(msum[:, :, :, :], 0.0).then_inc(c_vec, 1)
            vec.memset(bank[3][:, :, :], 0.0).then_inc(c_vec, 1)
            vec.wait_ge(c_vec, 5)
            vec.memset(usel[:, SUM_U:SUM_U + 1], 1.0).then_inc(c_vec, 1)
            vec.memset(vb[:, :, :, :, SUM_R], 1.0).then_inc(c_vec, 1)
            vec.wait_ge(c_vec, 7)

            vec.wait_ge(x_in, 16 * B)
            with vec.Fori(0, B) as b:
                tile = lambda t: bass.ds(b * TB + t, 1)
                for t in range(TB):
                    last = vec.bn_stats(st[:, t, :], x_t[:, tile(t), :].rearrange("p a c -> p (a c)"))
                last.then_inc(ln_v, 1)
                vec.wait_ge(ln_v, b * LN_STEPS + 1)
                vec.memset(gate_v[:, :], 0.0)
                for t in range(TB):
                    last = vec.bn_aggr(mv[:, t, :], st[:, t, :])
                last.then_inc(ln_v, 1)
                vec.wait_ge(ln_v, b * LN_STEPS + 2)
                vec.tensor_scalar(lnw[:, 0, :], mv[:, :, 1], LN_EPS, None, ALU.add).then_inc(ln_v, 1)
                vec.wait_ge(ln_s, b + 1)
                vec.reciprocal(lnw[:, 2, :], lnw[:, 1, :]).then_inc(ln_v, 1)
                vec.wait_ge(ln_v, b * LN_STEPS + 4)
                vec.tensor_tensor(lnw[:, 3, :], lnw[:, 0, :], lnw[:, 2, :], ALU.mult).then_inc(ln_v, 1)
                vec.wait_ge(ln_v, b * LN_STEPS + 5)
                vec.tensor_tensor(lnw[:, 4, :], lnw[:, 3, :], lnw[:, 1, :], ALU.add).then_inc(ln_v, 1)
                vec.wait_ge(ln_v, b * LN_STEPS + 6)
                vec.reciprocal(lnw[:, 2, :], lnw[:, 4, :]).then_inc(ln_v, 1)
                vec.wait_ge(ln_v, b * LN_STEPS + 7)
                vec.tensor_scalar(lnw[:, 3, :], lnw[:, 2, :], 2.0, None, ALU.mult).then_inc(ln_v, 1)
                vec.wait_ge(ln_v, b * LN_STEPS + 8)
                for t in range(TB):
                    last = vec.tensor_scalar(xn[:, tile(t), :].rearrange("p a c -> p (a c)"),
                                             x_t[:, tile(t), :].rearrange("p a c -> p (a c)"),
                                             mv[:, t, 0:1], lnw[:, 3, t:t + 1], ALU.subtract, ALU.mult)
                last.then_inc(ln_v, 1)
            vec.wait_ge(s_gain, 2)
            vec.wait_ge(w_in, 16 * (7 + 2 * TB))
            vec.tensor_tensor(bq_s[:, :], bq[:, 0:1], gsign[:, 0:1], ALU.mult).then_inc(s_gain, 1)
            vec.reciprocal(gsign[:, 2:3], gsign[:, 1:2]).then_inc(s_gain, 1)
            flat3 = bank[3][:, :, :].rearrange("p a n -> p (a n)")
            with vec.Fori(0, B) as b:
                vec.wait_ge(v_mm, b + 1)
                wait(vec, v_out, b * 64)
                for hq in range(4):
                    four = slice(hq * 4 * D, (hq + 1) * 4 * D)
                    heads = lambda ap: ap[:, :, four].rearrange("p t (g d) -> p t g d", d=D)
                    vec.tensor_tensor(vb[:, hq, :, :, 0:D], heads(flat3.rearrange("p (t c) -> p t c", c=C)),
                                      heads(bv[:, :, :]), ALU.add)
                vec.wait_ge(g_mm, b + 1)
                vec.tensor_tensor(logit[:, bass.ts(b, TB), :].rearrange("p t e -> p (t e)"), bank[0][:, 0, 0:TB * E],
                                  bgate[:, :, :].rearrange("p t e -> p (t e)"), ALU.add).then_inc(v_ev, 1)
                vec.wait_ge(qk_f, b * 2 + 2)
                vec.tensor_scalar(ksum[:, 1:2], ksum[:, 0:1], 1.0 / T, None, ALU.mult).then_inc(k_c, 1)
                vec.wait_ge(k_c, b * 2 + 1)
                vec.tensor_scalar(qf[:, 1, :], qf[:, 1, :], ksum[:, 1:2], None, ALU.subtract).then_inc(k_c, 1)
                for n in range(2):
                    for s in range(2):
                        vec.wait_ge(part_a, b * 6 + (2 * n + s + 1))
                        if n:
                            vec.wait_ge(part_v, b * 4 + (s + 1))
                        vec.tensor_tensor(rest[:, s, :], (rest if n else qf)[:, s, :], parts[:, s, n, :],
                                          ALU.subtract).then_inc(part_v, 1)

            steps = [0]

            def chain(instruction):
                steps[0] += 1
                instruction.then_inc(route, 1)
                vec.wait_ge(route, steps[0])

            by_e = lambda v: v.unsqueeze(2).to_broadcast([P, NT, E])
            e_of = iota8[:, :].unsqueeze(1).to_broadcast([P, NT, E])
            vec.wait_ge(c_pool, 9)
            vec.wait_ge(v_ev, B)
            chain(vec.tensor_reduce(rs[:, 0, :], logit[:, :, :], AX, ALU.max))
            chain(vec.tensor_tensor(rt[0][:, :, :], logit[:, :, :], by_e(rs[:, 0, :]), ALU.is_equal))
            chain(vec.tensor_tensor(rt[1][:, :, :], rt[0][:, :, :], e_of, ALU.mult))
            chain(vec.tensor_reduce(rs[:, 1, :], rt[1][:, :, :], AX, ALU.min))
            chain(vec.tensor_tensor(rt[2][:, :, :], e_of, by_e(rs[:, 1, :]), ALU.is_equal))
            chain(vec.scalar_tensor_tensor(rt[0][:, :, :], rt[2][:, :, :], -HUGE, logit[:, :, :], ALU.mult, ALU.add))
            chain(vec.tensor_reduce(rs[:, 2, :], rt[0][:, :, :], AX, ALU.max))
            chain(vec.tensor_tensor(rt[1][:, :, :], rt[0][:, :, :], by_e(rs[:, 2, :]), ALU.is_equal))
            chain(vec.tensor_tensor(rt[3][:, :, :], rt[1][:, :, :], e_of, ALU.mult))
            chain(vec.tensor_reduce(rs[:, 3, :], rt[3][:, :, :], AX, ALU.min))
            chain(vec.tensor_tensor(rt[5][:, :, :], e_of, by_e(rs[:, 3, :]), ALU.is_equal))
            chain(vec.tensor_tensor(rt[4][:, :, :], rt[2][:, :, :], rt[5][:, :, :], ALU.add))
            chain(vec.tensor_tensor(rs[:, 4, :], rs[:, 2, :], rs[:, 0, :], ALU.subtract))
            vec.wait_ge(r_exp, 1)
            chain(vec.tensor_scalar(rs[:, 6, :], rs[:, 5, :], 1.0, None, ALU.add))
            chain(vec.reciprocal(prob[:, :, 0], rs[:, 6, :]))
            chain(vec.tensor_tensor(prob[:, :, 1], rs[:, 5, :], prob[:, :, 0], ALU.mult))
            vec.wait_ge(r_mm, 2)
            total = bank[3][:, 1, 0:NT * E].rearrange("p (t e) -> p t e", e=E)
            chain(vec.tensor_copy(rt[0][:, :, :], total))
            a, b_ = rt[0], rt[1]
            k = 1
            while k < NT:
                chain(vec.tensor_copy(b_[:, 0:k, :], a[:, 0:k, :]))
                chain(vec.tensor_tensor(b_[:, k:, :], a[:, k:, :], a[:, 0:NT - k, :], ALU.add))
                a, b_, k = b_, a, 2 * k
            upto, free = a, b_
            chain(vec.tensor_tensor(rc[:, :, :], upto[:, NT - 1, :].unsqueeze(2).to_broadcast([P, E, NT]),
                                    iota_t[:, :].unsqueeze(1).to_broadcast([P, E, NT]), ALU.is_gt))
            chain(vec.tensor_reduce(rce[:, 0, :], rc[:, :, :], AX, ALU.add))
            a, k = 0, 1
            for b_ in (1, 2, 3):
                chain(vec.tensor_copy(rce[:, b_, 0:k], rce[:, a, 0:k]))
                chain(vec.tensor_tensor(rce[:, b_, k:], rce[:, a, k:], rce[:, a, 0:E - k], ALU.add))
                a, k = b_, 2 * k
            chain(vec.tensor_tensor(rce[:, 1, :], rce[:, 3, :], rce[:, 0, :], ALU.subtract))
            chain(vec.tensor_scalar(rce[:, 2, :], rce[:, 1, :], float(P), None, ALU.mult))
            rank = bank[3][:, 0, 0:NT * E].rearrange("p (t e) -> p t e", e=E)
            chain(vec.tensor_tensor(rt[3][:, :, :], rank, upto[:, :, :], ALU.add))
            chain(vec.tensor_tensor(free[:, :, :], rt[3][:, :, :], total, ALU.subtract))
            chain(vec.tensor_tensor(rt[3][:, :, :], free[:, :, :],
                                    rce[:, 2, :].unsqueeze(1).to_broadcast([P, NT, E]), ALU.add))
            for k, chosen in enumerate((rt[2], rt[5])):
                chain(vec.tensor_tensor(free[:, :, :], rt[3][:, :, :], chosen[:, :, :], ALU.mult))
                chain(vec.tensor_reduce(rs[:, 7 + k, :], free[:, :, :], AX, ALU.add))
                chain(vec.tensor_copy(pos[:, k, :], rs[:, 7 + k, :]))
            chain(vec.tensor_tensor(rx[:, :, :], iota_x[:, :].unsqueeze(2).to_broadcast([P, NX, E]),
                                    rce[:, 3, :].unsqueeze(1).to_broadcast([P, NX, E]), ALU.is_ge))
            chain(vec.tensor_reduce(rxs[:, :], rx[:, :, :], AX, ALU.add))
            chain(vec.tensor_scalar(te[:, :], rxs[:, :], float(E - 1), None, ALU.min))
            assert steps[0] == ROUTE_STEPS, steps

            def attention_vec(i):
                for x in range(2 * NH):
                    par, h = divmod(x, NH)
                    for m in range(NP):
                        if (PIECE_AT[m] + 1) // 2 == h and m not in PIECE_ACT:
                            q = i * 2 + par
                            vec.wait_ge(p_ready, q * NP + (m + 1))
                            at = 0
                            for g, n, k, w, col in PIECES[m]:
                                to = msum[:, q, g, col:col + 1] if isinstance(q, int) else msum[:, bass.ds(q, 1), g, col]
                                last = vec.tensor_scalar(junk_v[:, at:at + w], bank[3][:, 1, at:at + w], 0.0, None,
                                                         ALU.max, ALU.add, accum_out=to)
                                at += w
                            last.then_inc(p_used, 1)
                    w = HALF - LOW[h // 2]
                    vec.wait_ge(u_ready, i * (2 * NH) + (x + 1))
                    y = x - NW
                    wait(vec, r_ready[y % NR], i * (2 * NH // NR) + (y // NR + 1))
                    vec.scalar_tensor_tensor(W[x % NW][:, :, 0:w], bank[x % NSLOT][:, :, 0:w], 0.0,
                                             U[x % NU][:, :, 0:w], ALU.max, ALU.mult).then_inc(w_done, 1)

            attention_vec(0)
            with vec.Fori(1, NQ // 2) as i:
                attention_vec(i)

            vec.wait_ge(p_used, NP * NQ)
            for par in range(2):
                vec.wait_ge(y_out[par], 16 * 4 * NQ // 2)
            vec.wait_ge(w_ffn, 16 * 8 * E)

            def expert(k):
                return vec.value_load(te[0:1, k:k + 1] if isinstance(k, int) else te[0:1, bass.ds(k, 1)],
                                      min_val=0, max_val=E - 1)

            def ffn_vec(i, t, par, lo, hi):
                o = 1 - par
                if lo >= 1 and hi > -1:
                    e = expert(i - 1)
                    vec.wait_ge(f["mx"], i)
                    vec.tensor_tensor(xb[o][:, :], bank[0][:, 1, :], b12[:, bass.ds(e, 1), :].rearrange("p a n -> p (a n)"),
                                      ALU.add).then_inc(f["bx"], 1)
                    vec.wait_ge(f["bx"], i)
                    wait(vec, f["tz"], i - 2)
                    vec.tensor_tensor(zb[o][:, :], xb[o][:, 0:F], xb[o][:, F:2 * F], ALU.mult).then_inc(f["z"], 1)
                if lo >= 3 and hi > -3:
                    e = expert(i - 3)
                    vec.wait_ge(f["mg"], i - 2)
                    wait(vec, f["sl"], i - 4)
                    vec.tensor_tensor(gb[o][:, :], bank[1][:, 1, 0:F], bgs[:, bass.ds(e, 1), :].rearrange("p a n -> p (a n)"),
                                      ALU.add).then_inc(f["bg"], 1)
                if lo >= 5:
                    e = expert(i - 5)
                    vec.wait_ge(f["my"], i - 4)
                    wait(vec, fy[o], (t + (par - 7) // 2 + 1) * 16)
                    vec.tensor_tensor(yb[o][:, :], bank[2][:, 1, 0:C], b3s[:, bass.ds(e, 1), :].rearrange("p a n -> p (a n)"),
                                      ALU.add).then_inc(f["by"], 1)

            for i in range(6):
                ffn_vec(i, i // 2, i % 2, i, 1)
            with vec.Fori(3, NX // 2) as t:
                for par in range(2):
                    ffn_vec(t * 2 + par, t, par, 9, 1)
            for i in range(NX, NX + 5):
                ffn_vec(i, i // 2, i % 2, 9, NX - i)

            by_n = msum[:, :, :, :].rearrange("p q g n -> p n (q g)")
            cut = MCOLS - (TB - 1)
            vec.memset(mrow[:, TB - 1, :], 0.0)
            vec.tensor_copy(mrow[:, cut:TB - 1, :], by_n[:, cut:TB - 1, :])
            vec.tensor_tensor(mrow[:, 0:cut, :], by_n[:, 0:cut, :], by_n[:, TB - 1:, :], ALU.add).then_inc(m_row, 1)
            vec.wait_ge(fin_in, 48)
            vec.wait_ge(ms_t, 1)
            n64 = B * H
            vec.tensor_tensor(fw[:, 1, :], sums[:, 1, :], flat3[0:n64, :], ALU.add).then_inc(fin_v, 1)
            vec.wait_ge(fin_v, 1)
            vec.tensor_scalar(fw[:, 2, :], fw[:, 1, :], 2.0 / T, SMALL, ALU.mult, ALU.add).then_inc(fin_v, 1)
            vec.wait_ge(fin_v, 2)
            vec.tensor_scalar(fw[:, 1, :], fw[:, 2, :], gsign[0:n64, 2:3], None, ALU.mult).then_inc(fin_v, 1)
            vec.wait_ge(fin_v, 3)
            vec.tensor_tensor(fw[:, 2, :], fw[:, 1, :], fw[:, 1, :], ALU.mult).then_inc(fin_v, 1)
            vec.wait_ge(fin_v, 4)
            vec.tensor_tensor(fw[:, 1, :], fw[:, 2, :], fw[:, 2, :], ALU.mult).then_inc(fin_v, 1)
            vec.wait_ge(fin_v, 5)
            vec.scalar_tensor_tensor(fw[:, 2, :], fw[:, 1, :], SMALL, sums[:, 0, :], ALU.mult, ALU.add).then_inc(fin_v, 1)
            vec.wait_ge(fin_v, 6)
            vec.reciprocal(fw[:, 0, :], fw[:, 2, :]).then_inc(fin_v, 1)
            vec.tensor_tensor(xr[:, :, :], xr[:, :, :], bp[:, :].unsqueeze(1).to_broadcast([P, NT, C]),
                              ALU.add).then_inc(fin_v, 1)
            vec.wait_ge(gathered, 16 * 2 * NT)
            for k in range(TOPK):
                vec.wait_ge(fin_v, 8 + k)
                for t in range(NT):
                    last = vec.scalar_tensor_tensor(xr[:, t, :], gat[:, k, t, :], prob[:, t, k:k + 1], xr[:, t, :],
                                                    ALU.mult, ALU.add)
                last.then_inc(fin_v, 1)
            vec.wait_ge(fin_v, 8 + TOPK)
            for b in range(B):
                vec.wait_ge(y_in[b % 2], 16 * 2 * H * (b // 2 + 1))
                vec.tensor_tensor(yT[b % 2][:, :], yT[b % 2][:, :], rb[b % 2][:, :], ALU.mult).then_inc(yn_ready, 1)
                for hb in range(2):
                    vec.wait_ge(proj, 2 * b + hb + 1)
                    half = xr[:, b * TB + 4 * hb:b * TB + 4 * hb + 4, :].rearrange("p t c -> p (t c)")
                    vec.tensor_tensor(half, bank[1 + hb][:, 0, :], half, ALU.add).then_inc(res_half, 1)


_INS = ["L0_attn_x", "L0_attn_W_attn", "L0_attn_b_attn", "L0_attn_W_proj", "L0_attn_b_proj", "L0_attn_score_gain",
        "L0_ffn_gate_w", "L0_ffn_gate_b", "L0_ffn_w1", "L0_ffn_b1", "L0_ffn_w2", "L0_ffn_b2", "L0_ffn_wg",
        "L0_ffn_bg", "L0_ffn_w3", "L0_ffn_b3"]


def kernel(**inputs):
    import numpy as np
    import concourse.bacc as bacc
    from concourse.bass_utils import run_bass_kernel_spmd

    nc = bacc.Bacc("TRN2", target_bir_lowering=False, num_devices=1)
    arrays, args = {}, []
    for name in _INS:
        a = np.ascontiguousarray(inputs[name])
        if a.size == 1:
            a = a.reshape(1, 1)
        arrays["in_" + name] = a
        args.append(nc.dram_tensor("in_" + name, a.shape, mybir.dt.from_np(a.dtype), kind="ExternalInput").ap())
    shape = np.asarray(inputs["L0_attn_x"]).shape
    args.append(nc.dram_tensor("out", shape, F32, kind="ExternalOutput").ap())
    layer_kernel(nc, *args)
    r = run_bass_kernel_spmd(nc, [arrays], core_ids=[0])
    return r.results[0]["out"]
```

```python
from contextlib import ExitStack

import concourse.bass as bass
from concourse import mybir

F32 = mybir.dt.float32
BF16 = mybir.dt.bfloat16
I32 = mybir.dt.int32
ALU = mybir.AluOpType
ACT = mybir.ActivationFunctionType
AX = mybir.AxisListType.X

P = 128
LN_EPS = 1e-5
SMALL = 1e-6
HUGE = 1e30
TINY = 1e-37

HALF = 512
TERMS_Q = (0, 0, 1, 1, 0, 2)
TERMS_K = (0, 1, 0, 1, 2, 0)
VW = 10
SUM_R, SUM_U = 8, 9


def wait(engine, semaphore, value):
    if isinstance(value, int) and value <= 0:
        return
    engine.wait_ge(semaphore, value)


def layer_kernel(nc, x, w_attn, b_attn, w_proj, b_proj, score_gain, gate_w, gate_b,
                 w1, b1, w2, b2, wg, bg, w3, b3, out):
    B, T, C = x.shape
    E, _, F = w1.shape
    H = 16
    D = C // H
    N = B * T
    NT = N // P
    TB = T // P
    assert C == P and D == 8 and F == 2 * P
    TOPK = 2
    NX = -(-(N * TOPK + E * (P - 1)) // P)
    NX += -NX % 4
    NQ = B * H // 4
    CH = T // HALF
    STEPS = [(c, j) for c in range(CH) for j in range(TB) if P * j < HALF * (c + 1)]
    NS = len(STEPS)
    NH = 2 * NS
    LOW = [max(0, P * j - HALF * c) for c, j in STEPS]
    DIAG = [P * j >= HALF * c for c, j in STEPS]
    ND = 2 * sum(DIAG)
    masks_to = lambda y: y // NH * ND + sum(DIAG[z // 2] for z in range(y % NH + 1))
    PIECES, MCOLS = [], TB - 1
    for g in range(4):
        short = []
        for n in range(TB - 1):
            k, w = P * (n + 1), T - P * (n + 1)
            if w < HALF:
                short.append((g, n, k, w, n))
                continue
            PIECES.append([(g, n, k, HALF, n)])
            if w > HALF:
                short.append((g, n, k + HALF, w - HALF, TB - 1 + n))
        while short:
            a = short.pop(0)
            fits = [b for b in short if a[3] + b[3] == HALF]
            short.remove(fits[0])
            PIECES.append([a, fits[0]])
    MCOLS += (TB - 1) // 2
    NP = len(PIECES)
    ENDS = [max(k for k in range(NS) if STEPS[k][0] == c) for c in range(CH)]
    LAST = [2 * max(k for k in range(NS) if STEPS[k][0] == c) + 1 for c in range(CH)]
    PLAN = ["V", "VA", "V", "V", "V", "VA", "V", "VA", "V", "A", "V", "", "A", "", "V", "",
            "V", "VA", "V", "VA", "V", "VA", "V", "VA"]
    PIECE_OF = [(h, e) for h in range(NH) for e in PLAN[h]]
    assert len(PIECE_OF) == NP
    R_POOL = {1, 3, 5, 7, 8, 10, 12, 14, 17, 19, 21, 23}
    RLAG, AVLAG = 2, 5
    NU, NW = 8, 8
    NSLOT, NPB = 5, 2
    QUAD_SLOTS = -(-4 * NS // NSLOT) * NSLOT
    slot_of = lambda n: n % (4 * NS) % NSLOT

    def slot_free(n):
        q, k = divmod(n, 4 * NS)
        v = q * QUAD_SLOTS + k - NSLOT
        return v // QUAD_SLOTS * 4 * NS + min(v % QUAD_SLOTS + 1, 4 * NS)

    def pieces_done(m, engine):
        q, k = divmod(m, NP)
        return q * sum(e == engine for _, e in PIECE_OF) + sum(e == engine for _, e in PIECE_OF[:k + 1])

    MID = NQ // 2 - 1

    def by_pool(i, y):
        at = i if y >= 0 or not isinstance(i, int) else i - 1
        if isinstance(at, int) and (at == MID or at == 0 and y % (2 * NH) < 2 * NH - RLAG):
            return False
        return y % NH in R_POOL

    ROUTE_M, ROUTE_PLACES, ROUTE_STEPS = 13, 30, 33

    ctx = ExitStack()
    with ctx:
        def sb(name, shape, dt=F32):
            return ctx.enter_context(nc.sbuf_tensor(name, shape, dt))

        def sem(name):
            return ctx.enter_context(nc.semaphore(name))

        def dram(name, shape, dt=F32):
            return nc.dram_tensor(name, shape, dt, kind="Internal").ap()

        qk_d = dram("qk_parts", [2, B * P, 3, T], BF16)
        v_d = dram("v_stationary", [NQ, P, TB, 4 * VW])
        y_d = dram("attention_of_v", [B * H, D, T])
        s_d = dram("sums_of_r_and_u", [2, CH, B * H, HALF])
        xs_d = dram("sorted_x", [NX * P, C])
        ys_d = dram("sorted_y", [NX * P, C])

        ident = sb("ident", [P, P])
        tri = sb("earlier", [P, P])
        ones = sb("ones", [P, P])
        causal = sb("causal", [P, P])
        usel = sb("usel", [P, VW])
        iota8 = sb("iota8", [P, E])
        iota_t = sb("iota_t", [P, NT])
        iota_x = sb("iota_x", [P, NX + 4])
        wa = sb("wa", [P, 3 * C])
        wgate = sb("wgate", [P, E])
        wp = sb("wp", [P, C])
        bq = sb("bq", [P, 1])
        bq_s = sb("bq_s", [P, 1])
        bv = sb("bv", [P, C])
        sel = sb("sel", [P, CH * B, C])
        bgate = sb("bgate", [P, E])
        bp = sb("bp", [P, C])
        gain = sb("gain", [P, 1])
        gsign = sb("gsign", [P, 4])
        xn = sb("xn", [P, NT, C])
        logit = sb("logit", [P, NT, E])
        prob = sb("prob", [P, NT, 2])
        pos = sb("pos", [P, 2, NT], I32)
        te = sb("te", [P, NX + 4], I32)
        gate_v = sb("gate_v", [P, 1])
        msum = sb("msum", [P, NQ, 4, MCOLS])

        weights = ExitStack()
        w12, wgs, w3s, b12, bgs, b3s = [weights.enter_context(nc.sbuf_tensor(name, shape, F32)) for name, shape in (
            ("w12", [P, E, 2 * F]), ("wgs", [P, E, 2, F]), ("w3s", [P, E, 2, C]),
            ("b12", [P, E, 2 * F]), ("bgs", [P, E, F]), ("b3s", [P, E, C]))]
        weights.close()
        x_t, xnT_all = [weights.enter_context(nc.sbuf_tensor(name, shape, F32)) for name, shape in (
            ("x_t", [P, NT, C]), ("xnT_all", [P, B, T]))]
        xnb = [weights.enter_context(nc.sbuf_tensor(f"xnb{i}", [P, TB, C], F32)) for i in range(2)]
        xnT = [weights.enter_context(nc.sbuf_tensor(f"xnT{i}", [P, T], F32)) for i in range(2)]
        vb = [weights.enter_context(nc.sbuf_tensor(f"vb{i}", [P, 4, TB, 4, VW], F32)) for i in range(2)]
        rest = weights.enter_context(nc.sbuf_tensor("rest", [P, 2, T], F32))
        weights.close()
        xr = sb("xr", [P, NT, C])
        gat = sb("gat", [P, 2, NT, C])
        sb("rest_of_weights", [P, E * (7 * F + 3 * C) - 3 * NT * C])

        xt = [sb(f"xt{i}", [P, C]) for i in range(2)]

        bank = [ctx.enter_context(nc.psum_tensor(f"bank{i}", [P, 2, HALF], F32)) for i in range(4)]

        c_pool, c_vec = sem("constants_pool"), sem("constants_vec")
        w_in, w_ffn = sem("small_weights_in"), sem("ffn_weights_in")
        x_in, w_late = sem("x_in"), sem("late_weights_in")
        s_gain = sem("gain_sign")
        ln_v, ln_s = sem("ln_vector"), sem("ln_sqrt")
        xnb_ready, tr_done, xnT_ready = sem("xnb_ready"), sem("xn_transposed"), sem("xnT_ready")
        xnT_kept = sem("xnT_kept")
        q_mm, k_mm, v_mm, g_mm = sem("q_mm"), sem("k_mm"), sem("v_mm"), sem("gate_mm")
        qk_f = sem("qk_float_ready")
        v_ev, lg_ev, k_mean, m_mm = sem("v_evacuated"), sem("logits_evacuated"), sem("k_mean"), sem("k_mean_mm")
        part_a, part_v, part_p = sem("part_rounded"), sem("part_rest"), sem("last_part_rounded")
        part_out = [sem("parts_stored0"), sem("parts_stored1")]
        v_out = [sem("v_stored0"), sem("v_stored1")]
        route, r_mm, r_exp = sem("route"), sem("route_mm"), sem("route_exp")
        z_out, xs_out = sem("xs_zeroed"), sem("xs_scattered")
        qk_in = [sem("quad_in0"), sem("quad_in1")]
        s_ready, u_ready, w_done, w_mask = sem("scores_ready"), sem("u_ready"), sem("w_done"), sem("w_masked")
        r_ready = [sem(f"r_ready{i}") for i in range(NW)]
        r_used, u_used = sem("r_used"), sem("u_used")
        acc_ev = sem("acc_evacuated")
        y_out = [sem("sums_stored0"), sem("sums_stored1")]
        p_ready, p_used = sem("piece_ready"), {"V": sem("piece_used_vec"), "A": sem("piece_used_act")}
        fx = [sem("ffn_x_in0"), sem("ffn_x_in1")]
        fy = [sem("ffn_y_out0"), sem("ffn_y_out1")]
        f = {n: sem("ffn_" + n) for n in
             ("tx", "cx", "mx", "bx", "z", "tz", "cz", "mg", "bg", "sl", "ts", "cs", "my", "by")}
        m_row = sem("piece_sums_by_row")
        fin_in, fin_v, ms_t, rb_mm = sem("final_in"), sem("final_vec"), sem("ms_transposed"), sem("scales_by_row")
        y_in, yn_ready, proj = [sem(f"y_in{b}") for b in range(B)], sem("yn_ready"), sem("proj")
        x_again, res_x = sem("x_in_again"), sem("result_without_attention")
        gathered, res_half, res_out = sem("gathered"), sem("result_half"), sem("result_out")

        phase = ExitStack()

        def tmp(name, shape, dt=F32):
            return phase.enter_context(nc.sbuf_tensor(name, shape, dt))

        st = tmp("st", [P, TB, 6])
        mvb = tmp("mvb", [P, TB, 2])
        mv = tmp("mv", [P, NT, 2])
        lnw = tmp("lnw", [P, 5, NT])
        qkf = tmp("qkf", [P, 2, 2, T])
        ksum = tmp("ksum", [P, B])
        k_off = tmp("k_off", [P, 2])
        parts = [tmp(f"parts{i}", [P, 2, 3, T], BF16) for i in range(2)]
        rt = [tmp(f"rt{i}", [P, NT, E]) for i in range(6)]
        rs = tmp("rs", [P, 12, NT])
        rx = tmp("rx", [P, NX + 4, E])
        rxs = tmp("rxs", [P, NX + 4])
        rc = tmp("rc", [P, E, NT])
        rce = tmp("rce", [P, 4, E])
        phase.close()

        U = [tmp(f"U{i}", [P, 2, HALF]) for i in range(NU)]
        W = [tmp(f"W{i}", [P, 2, HALF]) for i in range(NW)]
        yq = [tmp(f"yq{i}", [P, CH, HALF]) for i in range(2)]
        junk = [tmp(f"junk{i}", [P, HALF], BF16) for i in range(NPB)]
        QS = [tmp(f"QS{i}", [P, 2, T], BF16) for i in range(2)]
        KS = [tmp(f"KS{i}", [P, 4, T], BF16) for i in range(2)]
        VS = [tmp(f"VS{i}", [P, TB, 4, VW]) for i in range(2)]
        phase.close()

        xT = [tmp(f"xT{i}", [P, C]) for i in range(2)]
        xb = [tmp(f"xb{i}", [P, 2 * F]) for i in range(2)]
        zb = [tmp(f"zb{i}", [P, F]) for i in range(2)]
        zT = [tmp(f"zT{i}", [P, 2, P]) for i in range(2)]
        gb = [tmp(f"gb{i}", [P, F]) for i in range(2)]
        sg = [tmp(f"sg{i}", [P, F]) for i in range(2)]
        sT = [tmp(f"sT{i}", [P, 2, P]) for i in range(2)]
        yb = [tmp(f"yb{i}", [P, C]) for i in range(2)]
        phase.close()
        mrow = tmp("mrow", [P, TB // CH, CH * B * H])
        sums = tmp("sums", [P, 2, HALF])
        fw = tmp("fw", [P, 3, HALF])
        yT = [tmp(f"yT{i}", [P, T]) for i in range(B)]
        phase.close()

        x_v = x.rearrange("b (t p) c -> p (b t) c", p=P)
        out_v = out.rearrange("b (t p) c -> p (b t) c", p=P)
        flat = [bk[:, :, :].rearrange("p a n -> p (a n)") for bk in bank]
        row = lambda v: v.rearrange("(a n) -> a n", a=1)
        s_q = s_d.rearrange("k c (q g) n -> q g k c n", g=4)
        v_bias = bv[:, :].unsqueeze(1).to_broadcast([P, TB, C])
        qk_q = qk_d.rearrange("s (q hh r d) part t -> s q r part d hh t", hh=2, r=2, d=D)

        def rows_of(ap, n):
            return ap.to_broadcast([P, n])

        score = lambda n: bank[slot_of(n) // 2][:, slot_of(n) % 2, :]
        piece = lambda m: bank[2 + m % NPB][:, 1, :]

        def wait_pieces(engine):
            for e in "VA":
                engine.wait_ge(p_used[e], pieces_done(NP * NQ - 1, e))

        def rest_of(engine, b):
            for n in range(2):
                for s in (1, 0):
                    engine.wait_ge(part_a, 4 * b + 2 * n + 2 - s)
                    if n == 0:
                        wait(engine, part_p, 2 * b - s)
                    else:
                        engine.wait_ge(part_v, 4 * b + 2 - s)
                    engine.tensor_tensor(rest[:, s, :], rest[:, s, :] if n else qkf[:, b % 2, s, :],
                                         parts[b % 2][:, s, n, :], ALU.subtract).then_inc(part_v, 1)

        def experts(engine, t):
            at = 4 * (t - 1) if not isinstance(t, int) or t else 0
            return nc.values_load_multi_w_load_instructions(
                te[0:1, at:at + 8] if isinstance(at, int) else te[0:1, bass.ds(at, 8)], engines=[engine],
                min_val=0, max_val=E - 1, skip_runtime_bounds_check_because="te is a minimum with E - 1")[1]

        block = ctx.enter_context(nc.Block())

        @block.sync
        def _(sp):
            for b in range(B):
                wait(sp, x_in, 16 * b)
                sp.dma_start(x_t[:, b * TB:(b + 1) * TB, :], x_v[:, b * TB:(b + 1) * TB, :]).then_inc(x_in, 16)
            sp.wait_ge(c_vec, 2)
            zero_rows = xs_d.rearrange("(k p) c -> p k c", p=P)
            zeros = msum[:, :, :, :].rearrange("p q g n -> p (q g n)")[:, 0:C]
            for k in range(0, NX, NX // 4):
                sp.dma_start(zero_rows[:, k:k + NX // 4, :],
                             zeros.unsqueeze(1).to_broadcast([P, NX // 4, C])).then_inc(z_out, 16)
            with sp.Fori(0, B // 2) as i:
                for par in range(2):
                    sp.wait_ge(v_ev, i * 2 + par + 3)
                    for hq in range(4):
                        sp.dma_start(v_d[i * 8 + par * 4 + hq].rearrange("p t n -> p (t n)"),
                                     vb[par][:, hq].rearrange("p t g n -> p (t g n)")).then_inc(v_out[par], 16)

            def load_quad(q, par):
                for r in range(2):
                    for k in range(len(TERMS_Q)):
                        rows = slice(64 * r + D * k, 64 * r + D * (k + 1))
                        sp.dma_start(QS[par][rows, :, :], qk_q[0, q, r, TERMS_Q[k]]).then_inc(qk_in[par], 16)
                        sp.dma_start(KS[par][rows, r::2, :], qk_q[1, q, r, TERMS_K[k]]).then_inc(qk_in[par], 16)
                sp.dma_start(VS[par][:, :, :, :].rearrange("p t g n -> p t (g n)"), v_d[q]).then_inc(qk_in[par], 16)

            def store_quad(q, i, par):
                sp.wait_ge(acc_ev, (q + 1) * CH)
                for g in range(4):
                    sp.dma_start(y_d[q * 4 + g], yq[par][32 * g:32 * g + D, :, :].rearrange("p c n -> p (c n)"),
                                 ).then_inc(y_out[par], 16)
                    sp.dma_start(s_q[q, g], yq[par][32 * g + D:32 * g + VW, :, :]).then_inc(y_out[par], 16)

            for b in range(B):
                for s in (1, 0):
                    sp.wait_ge(part_p, 2 * b + 2 - s)
                    sp.dma_start(qk_d[s, b * P:(b + 1) * P, :, :], parts[b % 2][:, s, :, :]).then_inc(part_out[b % 2], 16)
                if b == 0:
                    for par in range(2):
                        sp.wait_ge(v_out[par], 64 * (B // 2) + 1)
                    sp.wait_ge(part_out[0], 33)
                    sp.wait_ge(c_vec, 10)
                    load_quad(0, 0)
            load_quad(1, 1)
            for par in range(2):
                sp.wait_ge(part_out[par], 32 * (B // 2) + 1)
            for to, w in ((w12[:, :, 0:F], w1), (w12[:, :, F:2 * F], w2)):
                sp.dma_start(to, w.rearrange("e c n -> c e n")).then_inc(w_ffn, 16)
            for e in range(E):
                sp.dma_start(wgs[:, e, :, :], wg[e].rearrange("(k p) n -> p k n", p=P)).then_inc(w_ffn, 16)
                sp.dma_start(w3s[:, e, :, :], w3[e].rearrange("(k p) n -> p k n", p=P)).then_inc(w_ffn, 16)
            for to, v, n in ((b12[:, :, 0:F], b1, F), (b12[:, :, F:2 * F], b2, F), (bgs[:, :, :], bg, F), (b3s[:, :, :], b3, C)):
                sp.dma_start(to, v.rearrange("(a e) n -> a e n", a=1).to_broadcast([P, E, n])).then_inc(w_ffn, 16)

            def next_quad(i, par):
                store_quad(i * 2 + par, i, par)
                sp.wait_ge(u_used, i * (2 * NH) + (par + 1) * NH)
                load_quad(i * 2 + (par + 2), par)

            with sp.Fori(0, MID - 1) as i:
                for par in range(2):
                    next_quad(i, par)
            next_quad(MID - 1, 0)

            sp.wait_ge(xs_out, 16 * 2 * NT)
            xs_t = xs_d.rearrange("(k p) c -> k p c", p=P)

            def ffn_sp(i, par):
                wait(sp, f["tx"], i - 1)
                sp.dma_start(xt[par][:, :], xs_t[i]).then_inc(fx[par], 16)

            for i in range(2):
                ffn_sp(i, i)
            store_quad(2 * MID - 1, MID - 1, 1)
            with sp.Fori(1, NX // 2) as t:
                for par in range(2):
                    ffn_sp(t * 2 + par, par)

            load_quad(NQ - 1, 1)
            for par in range(2):
                sp.wait_ge(fy[par], 16 * NX // 2)
            sp.dma_start(xr[:, :, :], x_v).then_inc(x_again, 16)
            for par in range(2):
                store_quad(NQ - 2 + par, NQ // 2 - 1, par)
            for par in range(2):
                sp.wait_ge(y_out[par], 16 * 8 * NQ // 2)

            sp.wait_ge(u_used, NQ * NH)
            for k in range(2):
                sp.dma_start(sums[:, k, :], s_d[k].rearrange("c h n -> (c h) n")).then_inc(fin_in, 16)
            for b in range(B):
                sp.dma_start(yT[b][:, :], y_d[b * H:(b + 1) * H].rearrange("h d t -> (h d) t")).then_inc(y_in[b], 16)
            for b in range(B):
                sp.wait_ge(res_half, 2 * (b + 1))
                sp.dma_start(out_v[:, b * TB:(b + 1) * TB, :], xr[:, b * TB:(b + 1) * TB, :]).then_inc(res_out, 16)
            sp.wait_ge(res_out, 16 * B)

        @block.gpsimd
        def _(pool):
            pool.memset(ident[:, :], 0.0).then_inc(c_pool, 1)
            pool.memset(tri[:, :], 0.0).then_inc(c_pool, 1)
            pool.memset(ones[:, :], 1.0).then_inc(c_pool, 1)
            pool.memset(sel[:, :, :], 0.0).then_inc(c_pool, 1)
            pool.wait_ge(c_pool, 4)
            pool.affine_select(out=ident[:, :], in_=ident[:, :], compare_op=ALU.not_equal, fill=1.0, base=0,
                               pattern=[[-1, P]], channel_multiplier=1).then_inc(c_pool, 1)
            pool.affine_select(out=tri[:, :], in_=ones[:, :], compare_op=ALU.is_gt, fill=0.0, base=0,
                               pattern=[[1, P]], channel_multiplier=-1).then_inc(c_pool, 1)
            pool.affine_select(out=causal[:, :], in_=ones[:, :], compare_op=ALU.is_ge, fill=0.0, base=0,
                               pattern=[[1, P]], channel_multiplier=-1).then_inc(c_pool, 1)
            pool.affine_select(out=sel[:, :, :].rearrange("p a (m d) -> p a m d", d=D),
                               in_=sel[:, :, :].rearrange("p a (m d) -> p a m d", d=D), compare_op=ALU.not_equal, fill=1.0,
                               base=0, pattern=[[-H, CH * B], [-1, H], [0, D]], channel_multiplier=1).then_inc(c_pool, 1)
            pool.iota(iota8[:, :], [[1, E]], base=-E, channel_multiplier=0,
                      allow_small_or_imprecise_dtypes=True).then_inc(c_pool, 1)
            pool.iota(iota_t[:, :], [[P, NT]], base=0, channel_multiplier=0,
                      allow_small_or_imprecise_dtypes=True).then_inc(c_pool, 1)
            pool.iota(iota_x[:, :], [[1, NX + 4]], base=-1, channel_multiplier=0,
                      allow_small_or_imprecise_dtypes=True).then_inc(c_pool, 1)
            pool.wait_ge(c_pool, 11)
            rest_of(pool, 0)
            for b in range(B):
                for s in (1, 0):
                    pool.wait_ge(part_v, 4 * b + 4 - s)
                    pool.tensor_copy(parts[b % 2][:, s, 2, :], rest[:, s, :]).then_inc(part_p, 1)

            places = [(k, t) for t in range(NT) for k in range(TOPK)]

            def scatter(x):
                if x == 0:
                    pool.wait_ge(z_out, 16 * 4)
                    pool.wait_ge(route, ROUTE_STEPS)
                for k, t in places[x * len(places) // (2 * NH):(x + 1) * len(places) // (2 * NH)]:
                    pool.indirect_dma_start(xs_d, bass.IndirectOffsetOnAxis(pos[:, k, t:t + 1], 0),
                                            xn[:, t, :], None).then_inc(xs_out, 16)

            def gather(x):
                if x == 0:
                    for par in range(2):
                        pool.wait_ge(fy[par], 16 * NX // 2)
                for k, t in places[x * len(places) // (2 * NH):(x + 1) * len(places) // (2 * NH)]:
                    pool.indirect_dma_start(gat[:, k, t, :], None, ys_d,
                                            bass.IndirectOffsetOnAxis(pos[:, k, t:t + 1], 0)).then_inc(gathered, 16)

            def attention_pool(i, first, drain, move=None):
                for x in range(2 * NH):
                    if move:
                        move(x)
                    if not drain and not move and DIAG[x % NH // 2]:
                        pool.wait_ge(w_done, i * (4 * NH) + 2 * (x + 1))
                        pool.tensor_tensor(W[x % NW][:, :, 0:P], W[x % NW][:, :, 0:P],
                                           causal[:, :].unsqueeze(1).to_broadcast([P, 2, P]),
                                           ALU.mult).then_inc(w_mask, 1)
                    y = x - 1
                    if (y < 0 and first) or (y >= 0 and drain) or not by_pool(i, y):
                        continue
                    w = HALF - LOW[y % NH // 2]
                    if DIAG[y % NH // 2]:
                        pool.wait_ge(w_mask, i * (2 * ND) + masks_to(y))
                    else:
                        pool.wait_ge(w_done, i * (4 * NH) + 2 * (y + 1))
                    pool.tensor_tensor(W[y % NW][:, :, 0:w], W[y % NW][:, :, 0:w], W[y % NW][:, :, 0:w],
                                       ALU.mult).then_inc(r_ready[y % NW], 1)

            attention_pool(0, True, False, scatter)
            with pool.Fori(1, MID) as i:
                attention_pool(i, False, False)
            attention_pool(MID, False, True)
            attention_pool(MID, True, False, gather)
            attention_pool(MID + 1, False, True)

        @block.scalar
        def _(act):
            act.dma_start(wa[:, :], w_attn).then_inc(w_in, 16)
            act.dma_start(gain[:, :], rows_of(score_gain, 1)).then_inc(w_in, 16)
            act.dma_start(bq[:, :], b_attn[0:C].rearrange("(p a) -> p a", a=1)).then_inc(w_in, 16)
            act.dma_start(bv[:, :], rows_of(row(b_attn[2 * C:3 * C]), C)).then_inc(w_in, 16)
            act.dma_start(wgate[:, :], gate_w).then_inc(w_in, 16)
            act.dma_start(bgate[:, :], rows_of(row(gate_b), E)).then_inc(w_late, 16)
            act.dma_start(wp[:, :], w_proj).then_inc(w_late, 16)
            act.dma_start(bp[:, :], rows_of(row(b_proj), C)).then_inc(w_late, 16)
            act.wait_ge(ln_v, 3 * B + 1)
            act.activation(lnw[:, 1, :], lnw[:, 0, :], ACT.Sqrt).then_inc(ln_s, 1)
            act.wait_ge(w_in, 16 * 5)
            act.activation(gsign[:, 0:1], gain[:, :], ACT.Sign).then_inc(s_gain, 1)
            act.activation(gsign[:, 1:2], gain[:, :], ACT.Abs).then_inc(s_gain, 1)
            act.wait_ge(s_gain, 1)
            act.activation(bq_s[:, :], bq[:, :], ACT.Copy, scale=gsign[:, 0:1]).then_inc(s_gain, 1)
            act.wait_ge(s_gain, 3)
            with act.Fori(0, B // 2) as i:
                for par in range(2):
                    act.wait_ge(ln_v, i * 2 + (3 * B + 8 + par))
                    act.copy(xnb[par][:, :, :], xn[:, bass.ds(i * 2 * TB + par * TB, TB), :]).then_inc(xnb_ready, 1)
                for par in range(2):
                    act.wait_ge(tr_done, i * 2 + par + 1)
                    act.activation(xnT[par][:, :], flat[par], ACT.Identity,
                                   accum_out=ksum[:, bass.ds(i * 2 + par, 1)]).then_inc(xnT_ready, 1)
                for par in range(2):
                    act.wait_ge(g_mm, i * 2 + par + 1)
                    act.copy(logit[:, bass.ds(i * 2 * TB + par * TB, TB), :].rearrange("p t e -> p (t e)"),
                             bank[par][:, 0, 0:TB * E]).then_inc(lg_ev, 1)
                for par in range(2):
                    act.wait_ge(xnT_ready, i * 2 + par + 1)
                    act.copy(xnT_all[:, bass.ds(i * 2 + par, 1), :].rearrange("p a t -> p (a t)"),
                             xnT[par][:, :]).then_inc(xnT_kept, 1)
            with act.Fori(0, B // 2) as i:
                for par in range(2):
                    act.wait_ge(m_mm, i * 2 + par + 1)
                    act.activation(k_off[:, par:par + 1], bank[2][:, 0, 0:1], ACT.Copy, scale=-1.0 / T).then_inc(k_mean, 1)
                    act.wait_ge(k_mm, i * 2 + par + 1)
                    act.wait_ge(k_mean, i * 2 + par + 1)
                    act.activation(qkf[:, par, 1, :], flat[0], ACT.Identity, bias=k_off[:, par:par + 1]).then_inc(qk_f, 1)
                    act.wait_ge(q_mm, i * 2 + par + 1)
                    act.activation(qkf[:, par, 0, :], flat[1], ACT.Identity,
                                   scale=gsign[:, 0:1], bias=bq_s[:, 0:1]).then_inc(qk_f, 1)
                    act.wait_ge(part_out[par], i * 32 + 1)
                    for s in (1, 0):
                        act.wait_ge(qk_f, i * 4 + 2 * par + 4 - s)
                        act.copy(parts[par][:, s, 0, :], qkf[:, par, s, :]).then_inc(part_a, 1)
                    for s in (1, 0):
                        act.wait_ge(part_v, i * 8 + 4 * par + 2 - s)
                        act.copy(parts[par][:, s, 1, :], rest[:, s, :]).then_inc(part_a, 1)
            act.wait_ge(route, ROUTE_PLACES)
            act.activation(rs[:, 5, :], rs[:, 4, :], ACT.Exp).then_inc(r_exp, 1)

            act.wait_ge(route, ROUTE_STEPS)
            for par in range(2):
                act.wait_ge(part_out[par], 32 * (B // 2) + 1)

            def attention_act(i, first, drain):
                for x in range(2 * NH):
                    par, h = divmod(x, NH)
                    if not drain:
                        w = HALF - LOW[h // 2]
                        wait(act, u_used, i * (2 * NH) + (x - NU + 1))
                        for r in range(2):
                            act.wait_ge(s_ready, i * (4 * NH) + (2 * x + r + 1))
                            act.activation(U[x % NU][:, r, 0:w], score(2 * x + r)[:, 0:w], ACT.Relu).then_inc(u_ready, 1)
                    for m, (at_h, e) in enumerate(PIECE_OF):
                        if not drain and at_h == h and e == "A":
                            q = i * 2 + par
                            act.wait_ge(p_ready, q * NP + (m + 1))
                            at = 0
                            for g, n, k, w, col in PIECES[m]:
                                last = act.activation(junk[m % NPB][:, at:at + w], piece(m)[:, at:at + w], ACT.Relu,
                                                      accum_out=msum_at(q, g, col))
                                at += w
                            last.then_inc(p_used["A"], 1)
                    y = x - RLAG
                    if not ((y < 0 and first) or (y >= 0 and drain)) and not by_pool(i, y):
                        w = HALF - LOW[y % NH // 2]
                        if DIAG[y % NH // 2]:
                            act.wait_ge(w_mask, i * (2 * ND) + masks_to(y))
                        else:
                            act.wait_ge(w_done, i * (4 * NH) + 2 * (y + 1))
                        act.activation(W[y % NW][:, :, 0:w], W[y % NW][:, :, 0:w], ACT.Square,
                                       ).then_inc(r_ready[y % NW], 1)
                    z = x - AVLAG
                    if z % NH in LAST and not ((z < 0 and first) or (z >= 0 and drain)):
                        q = i * 2 + z // NH
                        act.wait_ge(u_used, i * (2 * NH) + (z + 1))
                        if not (isinstance(q, int) and q < 2):
                            act.wait_ge(y_out[z // NH % 2], 128 * (i + z // NH // 2))
                        act.copy(yq[z // NH % 2][:, STEPS[z % NH // 2][0], :], bank[3][:, 0, :]).then_inc(acc_ev, 1)

            def msum_at(q, g, col):
                return msum[:, q, g, col:col + 1] if isinstance(q, int) else msum[:, bass.ds(q, 1), g, col]

            attention_act(0, True, False)
            with act.Fori(1, MID) as i:
                attention_act(i, False, False)
            attention_act(MID, False, True)

            ys_t = ys_d.rearrange("(k p) c -> k p c", p=P)

            def ffn_act(i, par, lo, hi):
                o = 1 - par
                if lo >= 6:
                    act.wait_ge(f["by"], i - 5)
                    act.dma_start(ys_t[i - 6], yb[par][:, :]).then_inc(fy[par], 16)
                if lo >= 0 and hi > 0:
                    act.wait_ge(f["tx"], i + 1)
                    wait(act, f["mx"], i - 1)
                    act.copy(xT[par][:, :], bank[0][:, 0, 0:P]).then_inc(f["cx"], 1)
                if lo >= 2 and hi > -2:
                    act.wait_ge(f["tz"], i - 1)
                    wait(act, f["mg"], i - 3)
                    act.copy(zT[par][:, :, :].rearrange("p a n -> p (a n)"), bank[1][:, 0, 0:F]).then_inc(f["cz"], 1)
                if lo >= 3 and hi > -3:
                    act.wait_ge(f["bg"], i - 2)
                    wait(act, f["ts"], i - 4)
                    act.activation(sg[o][:, :], gb[o][:, :], ACT.Silu).then_inc(f["sl"], 1)
                if lo >= 4 and hi > -4:
                    act.wait_ge(f["ts"], i - 3)
                    wait(act, f["my"], i - 5)
                    act.copy(sT[par][:, :, :].rearrange("p a n -> p (a n)"), bank[2][:, 0, 0:F]).then_inc(f["cs"], 1)

            for i in range(8):
                ffn_act(i, i % 2, i, 1)
            with act.Fori(2, NX // 4) as t:
                for k in range(4):
                    ffn_act(t * 4 + k, k % 2, 9, 1)
            for i in range(NX, NX + 6):
                ffn_act(i, i % 2, 9, NX - i)
            for par in range(2):
                act.wait_ge(fy[par], 16 * NX // 2)
            attention_act(MID, True, False)
            attention_act(MID + 1, False, True)

        @block.tensor
        def _(pe):
            pe.wait_ge(c_pool, 11)
            pe.wait_ge(w_in, 16 * 5)
            with pe.Fori(0, B // 2) as i:
                for par in range(2):
                    pe.wait_ge(xnb_ready, i * 2 + par + 1)
                    for t in range(TB):
                        last = pe.transpose(flat[par][:, t * P:(t + 1) * P], xnb[par][:, t, :], ident[:, :])
                    last.then_inc(tr_done, 1)
                for par in range(2):
                    pe.wait_ge(xnT_ready, i * 2 + par + 1)
                    for t in range(TB):
                        last = pe.matmul(bank[par][:, 0, t * E:(t + 1) * E], xnT[par][:, t * P:(t + 1) * P], wgate[:, :],
                                         start=True, stop=True)
                    last.then_inc(g_mm, 1)
                for par in range(2):
                    pe.wait_ge(v_ev, i * 2 + par + 1)
                    for t in range(TB):
                        last = pe.matmul(flat[2 + par][:, t * P:(t + 1) * P], xnT[par][:, t * P:(t + 1) * P],
                                         wa[:, 2 * C:3 * C], start=True, stop=True)
                    last.then_inc(v_mm, 1)
            pe.wait_ge(v_ev, B + 2)
            pe.wait_ge(lg_ev, B)
            pe.wait_ge(route, ROUTE_M)
            m_all = rt[4][:, :, :].rearrange("p t e -> p (t e)")
            pe.matmul(bank[3][:, 0, 0:NT * E], tri[:, :], m_all, start=True, stop=True).then_inc(r_mm, 1)
            pe.matmul(bank[3][:, 1, 0:NT * E], ones[:, :], m_all, start=True, stop=True).then_inc(r_mm, 1)
            with pe.Fori(0, B) as b:
                pe.wait_ge(xnT_kept, b + 1)
                for s, done in ((1, k_mm), (0, q_mm)):
                    pe.wait_ge(qk_f, b * 2 + 2 - s)
                    if s == 1:
                        pe.matmul(bank[2][:, 0, 0:1], wa[:, C:2 * C], ksum[:, bass.ds(b, 1)],
                                  start=True, stop=True).then_inc(m_mm, 1)
                    for c in range(CH):
                        last = pe.matmul(bank[1 - s][:, c, :], wa[:, s * C:(s + 1) * C],
                                         xnT_all[:, bass.ds(b, 1), c * HALF:(c + 1) * HALF].rearrange("p a t -> p (a t)"),
                                         start=True, stop=True)
                    last.then_inc(done, 1)

            def attention_pe(i, first, drain):
                for x in range(2 * NH):
                    par, h = divmod(x, NH)

                    if not drain:
                        c, j = STEPS[h // 2]
                        lo, p = LOW[h // 2], h % 2
                        if h == 0:
                            pe.wait_ge(qk_in[par], (i + 1) * (16 * 25))
                        for r in range(2):
                            wait(pe, w_done, i * (4 * NH) + slot_free(2 * x + r))
                            pe.matmul(score(2 * x + r)[:, 0:HALF - lo], KS[par][:, 2 * p + r, P * j:P * (j + 1)],
                                      QS[par][:, p, HALF * c + lo:HALF * (c + 1)], start=True, stop=True).then_inc(s_ready, 1)
                    for m, (at_h, e) in enumerate(PIECE_OF):
                        if not drain and at_h == h:
                            before = PIECE_OF[m - NPB][1]
                            wait(pe, p_used[before], i * pieces_done(2 * NP - 1, before)
                                 + pieces_done(par * NP + m - NPB, before))
                            at = 0
                            for g, n, k, w, _ in PIECES[m]:
                                last = pe.matmul(piece(m)[:, at:at + w], QS[par][:, g // 2, P * n:P * (n + 1)],
                                                 KS[par][:, g, k:k + w], start=True, stop=True)
                                at += w
                            last.then_inc(p_ready, 1)
                    y, z = x - AVLAG, x - AVLAG - 1
                    has_r = not ((y < 0 and first) or (y >= 0 and drain))
                    has_u = not ((z < 0 and first) or (z >= 0 and drain))
                    if has_r:
                        pe.wait_ge(r_ready[y % NW], i * (2 * NH // NW) + (y // NW + 1))
                    if has_u and z % NH not in LAST:
                        average(z, U[z % NU], True).then_inc(u_used, 1)
                    if has_r:
                        if STEPS[y % NH // 2][1] == 0 and y % 2 == 0:
                            wait(pe, acc_ev, i * (2 * CH) + (y // NH * CH + STEPS[y % NH // 2][0]))
                        average(y, W[y % NW], False).then_inc(r_used, 1)
                        if y % NH in LAST:
                            average(y, U[y % NU], True).then_inc(u_used, 1)

            def average(y, src, of_u):
                c, j = STEPS[y % NH // 2]
                lo = LOW[y % NH // 2]
                for r in range(2):
                    g = y % 2 * 2 + r
                    last = pe.matmul(bank[3][32 * g:32 * g + VW, 0, lo:HALF],
                                     usel[:, :] if of_u else VS[y // NH % 2][:, j, g, :], src[:, r, 0:HALF - lo],
                                     start=(j == 0 and not of_u), stop=(y % NH // 2 in ENDS and of_u),
                                     skip_group_check=True)
                return last

            pe.wait_ge(route, ROUTE_STEPS)
            pe.wait_ge(qk_f, 2 * B + 2)
            attention_pe(0, True, False)
            with pe.Fori(1, MID) as i:
                attention_pe(i, False, False)
            attention_pe(MID, False, True)

            for e in "VA":
                pe.wait_ge(p_used[e], MID * pieces_done(2 * NP - 1, e))
            pe.wait_ge(w_done, MID * 4 * NH)
            pe.wait_ge(w_ffn, 16 * (2 * E + 6))

            def ffn_pe(i, t, par, lo, hi, expert):
                o = 1 - par
                if hi > 0:
                    pe.wait_ge(fx[par], (t + 1) * 16)
                    wait(pe, f["cx"], i)
                    pe.transpose(bank[0][:, 0, 0:P], xt[par][:, :], ident[:, :]).then_inc(f["tx"], 1)
                if lo >= 1 and hi > -1:
                    e = expert(1)
                    pe.wait_ge(f["cx"], i)
                    wait(pe, f["bx"], i - 1)
                    pe.matmul(bank[0][:, 1, :], xT[o][:, :], w12[:, bass.ds(e, 1), :].rearrange("p a n -> p (a n)"),
                              start=True, stop=True).then_inc(f["mx"], 1)
                if lo >= 2 and hi > -2:
                    pe.wait_ge(f["z"], i - 1)
                    wait(pe, f["cz"], i - 2)
                    for k in range(2):
                        last = pe.transpose(bank[1][:, 0, k * P:(k + 1) * P], zb[par][:, k * P:(k + 1) * P], ident[:, :])
                    last.then_inc(f["tz"], 1)
                if lo >= 3 and hi > -3:
                    e = expert(3)
                    pe.wait_ge(f["cz"], i - 2)
                    wait(pe, f["bg"], i - 3)
                    for k in range(2):
                        last = pe.matmul(bank[1][:, 1, 0:F], zT[o][:, k, :],
                                         wgs[:, bass.ds(e, 1), k, :].rearrange("p a n -> p (a n)"),
                                         start=(k == 0), stop=(k == 1))
                    last.then_inc(f["mg"], 1)
                if lo >= 4 and hi > -4:
                    pe.wait_ge(f["sl"], i - 3)
                    wait(pe, f["cs"], i - 4)
                    for k in range(2):
                        last = pe.transpose(bank[2][:, 0, k * P:(k + 1) * P], sg[par][:, k * P:(k + 1) * P], ident[:, :])
                    last.then_inc(f["ts"], 1)
                if lo >= 5:
                    e = expert(5)
                    pe.wait_ge(f["cs"], i - 4)
                    wait(pe, f["by"], i - 5)
                    for k in range(2):
                        last = pe.matmul(bank[2][:, 1, 0:C], sT[o][:, k, :],
                                         w3s[:, bass.ds(e, 1), k, :].rearrange("p a n -> p (a n)"),
                                         start=(k == 0), stop=(k == 1))
                    last.then_inc(f["my"], 1)

            es = experts(mybir.EngineType.PE, 0)
            for i in range(8):
                ffn_pe(i, i // 2, i % 2, i, 1, lambda back: es[i - back + 1])
            with pe.Fori(2, NX // 4) as t:
                es = experts(mybir.EngineType.PE, t)
                for k in range(4):
                    ffn_pe(t * 4 + k, t * 2 + k // 2, k % 2, 9, 1, lambda back: es[k - back + 5])
            es = experts(mybir.EngineType.PE, NX // 4)
            for i in range(NX, NX + 5):
                ffn_pe(i, i // 2, i % 2, 9, NX - i, lambda back: es[min(i - NX - back + 5, 7)])

            pe.wait_ge(f["by"], NX)
            attention_pe(MID, True, False)
            attention_pe(MID + 1, False, True)

            wait_pieces(pe)
            pe.wait_ge(acc_ev, CH * NQ)
            pe.wait_ge(w_late, 48)
            pe.wait_ge(m_row, 1)
            for n in range(TB // CH):
                last = pe.transpose(bank[0][:, 0, n * P:(n + 1) * P], mrow[:, n, :], ident[:, :])
            last.then_inc(ms_t, 1)
            pe.wait_ge(fin_v, 7)

            def scales(b):
                for c in range(CH):
                    last = pe.matmul(bank[b % 2][:, c, :], sel[:, c * B + b, :], fw[:, 0, :], start=True, stop=True)
                last.then_inc(rb_mm, 1)

            scales(0)
            scales(1)
            for b in range(B):
                pe.wait_ge(yn_ready, b + 1)
                for hb in range(2):
                    wait(pe, res_half, 2 * (b - 1) + hb + 1)
                    for t in range(4):
                        k = hb * 4 + t
                        last = pe.matmul(bank[2 + hb][:, 0, t * C:(t + 1) * C], yT[b][:, k * P:(k + 1) * P],
                                         wp[:, :], start=True, stop=True)
                    last.then_inc(proj, 1)
                if b + 2 < B:
                    scales(b + 2)

        @block.vector
        def _(vec):
            vec.memset(usel[:, :], 0.0).then_inc(c_vec, 1)
            vec.memset(msum[:, :, :, :], 0.0).then_inc(c_vec, 1)
            for par in range(2):
                vec.memset(vb[par][:, :, :, :, :], 0.0).then_inc(c_vec, 1)
            vec.wait_ge(c_vec, 4)
            vec.memset(usel[:, SUM_U:SUM_U + 1], 1.0).then_inc(c_vec, 1)
            for par in range(2):
                vec.memset(vb[par][:, :, :, :, SUM_R], 1.0).then_inc(v_out[par], 1)
                vec.memset(gate_v[:, :], 0.0).then_inc(v_ev, 1)
                vec.wait_ge(v_ev, par + 1)
                vec.memset(parts[par][:, 0, 0, 0:1], 0.0).then_inc(part_out[par], 1)
                vec.memset(rest[:, par, 0:1], 0.0).then_inc(qk_f, 1)

            with vec.Fori(0, B) as b:
                tile = lambda t: bass.ds(b * TB + t, 1)
                vec.wait_ge(x_in, b * 16 + 16)
                for t in range(TB):
                    last = vec.bn_stats(st[:, t, :], x_t[:, tile(t), :].rearrange("p a c -> p (a c)"))
                last.then_inc(ln_v, 1)
                vec.wait_ge(ln_v, b * 3 + 1)
                vec.memset(gate_v[:, :], 0.0)
                for t in range(TB):
                    last = vec.bn_aggr(mvb[:, t, :], st[:, t, :])
                last.then_inc(ln_v, 1)
                vec.wait_ge(ln_v, b * 3 + 2)
                vec.tensor_copy(mv[:, bass.ts(b, TB), :], mvb[:, :, :]).then_inc(ln_v, 1)
            vec.wait_ge(ln_v, 3 * B)
            vec.tensor_scalar(lnw[:, 0, :], mv[:, :, 1], LN_EPS, None, ALU.add).then_inc(ln_v, 1)
            vec.wait_ge(ln_s, 1)
            vec.reciprocal(lnw[:, 2, :], lnw[:, 1, :]).then_inc(ln_v, 1)
            vec.wait_ge(ln_v, 3 * B + 2)
            vec.tensor_tensor(lnw[:, 3, :], lnw[:, 0, :], lnw[:, 2, :], ALU.mult).then_inc(ln_v, 1)
            vec.wait_ge(ln_v, 3 * B + 3)
            vec.tensor_tensor(lnw[:, 4, :], lnw[:, 3, :], lnw[:, 1, :], ALU.add).then_inc(ln_v, 1)
            vec.wait_ge(ln_v, 3 * B + 4)
            vec.reciprocal(lnw[:, 2, :], lnw[:, 4, :]).then_inc(ln_v, 1)
            vec.wait_ge(ln_v, 3 * B + 5)
            vec.tensor_scalar(lnw[:, 3, :], lnw[:, 2, :], 2.0, None, ALU.mult).then_inc(ln_v, 1)
            vec.wait_ge(ln_v, 3 * B + 6)
            vec.tensor_scalar(lnw[:, 4, :], mv[:, :, 0], 1.0, None, ALU.mult).then_inc(ln_v, 1)
            vec.wait_ge(ln_v, 3 * B + 7)
            with vec.Fori(0, B) as b:
                for t in range(TB):
                    at = bass.ds(b * TB + t, 1)
                    last = vec.tensor_scalar(xn[:, at, :].rearrange("p a c -> p (a c)"),
                                             x_t[:, at, :].rearrange("p a c -> p (a c)"),
                                             lnw[:, 4, at], lnw[:, 3, at], ALU.subtract, ALU.mult)
                last.then_inc(ln_v, 1)

            for par in range(2):
                vec.memset(QS[par][:, :, :], 0.0).then_inc(c_vec, 1)
                vec.memset(KS[par][:, :, :], 0.0).then_inc(c_vec, 1)
            vec.memset(gate_v[:, :], 0.0).then_inc(c_vec, 1)
            vec.wait_ge(w_in, 16 * 5)
            with vec.Fori(0, B // 2) as i:
                for par in range(2):
                    vec.wait_ge(v_mm, i * 2 + par + 1)
                    vec.wait_ge(v_out[par], i * 64 + 1)
                    for hq in range(4):
                        heads = lambda ap: ap[:, :, hq * 4 * D:(hq + 1) * 4 * D].rearrange("p t (g d) -> p t g d", d=D)
                        last = vec.tensor_tensor(vb[par][:, hq, :, :, 0:D], heads(flat[2 + par].rearrange("p (t c) -> p t c", c=C)),
                                                 heads(v_bias), ALU.add)
                    last.then_inc(v_ev, 1)

            steps = [0]

            def chain(*instructions):
                steps[0] += 1
                instructions[-1].then_inc(route, 1)
                vec.wait_ge(route, steps[0])

            by_e = lambda v: v.unsqueeze(2).to_broadcast([P, NT, E])
            e_of = iota8[:, :].unsqueeze(1).to_broadcast([P, NT, E])
            vec.wait_ge(c_pool, 11)
            vec.wait_ge(lg_ev, B)
            vec.wait_ge(w_late, 48)
            chain(vec.tensor_tensor(logit[:, :, :], logit[:, :, :], bgate[:, :].unsqueeze(1).to_broadcast([P, NT, E]), ALU.add))
            chain(vec.tensor_reduce(rs[:, 0, :], logit[:, :, :], AX, ALU.max))
            chain(vec.tensor_tensor(rt[0][:, :, :], logit[:, :, :], by_e(rs[:, 0, :]), ALU.is_equal))
            chain(vec.tensor_tensor(rt[1][:, :, :], rt[0][:, :, :], e_of, ALU.mult))
            chain(vec.tensor_reduce(rs[:, 1, :], rt[1][:, :, :], AX, ALU.min))
            chain(vec.tensor_tensor(rt[2][:, :, :], e_of, by_e(rs[:, 1, :]), ALU.is_equal))
            chain(vec.scalar_tensor_tensor(rt[0][:, :, :], rt[2][:, :, :], -HUGE, logit[:, :, :], ALU.mult, ALU.add))
            chain(vec.tensor_reduce(rs[:, 2, :], rt[0][:, :, :], AX, ALU.max))
            chain(vec.tensor_tensor(rt[1][:, :, :], rt[0][:, :, :], by_e(rs[:, 2, :]), ALU.is_equal))
            chain(vec.tensor_tensor(rt[3][:, :, :], rt[1][:, :, :], e_of, ALU.mult))
            chain(vec.tensor_reduce(rs[:, 3, :], rt[3][:, :, :], AX, ALU.min))
            chain(vec.tensor_tensor(rt[5][:, :, :], e_of, by_e(rs[:, 3, :]), ALU.is_equal),
                  vec.tensor_tensor(rs[:, 4, :], rs[:, 2, :], rs[:, 0, :], ALU.subtract))
            chain(vec.tensor_tensor(rt[4][:, :, :], rt[2][:, :, :], rt[5][:, :, :], ALU.add))
            assert steps[0] == ROUTE_M, steps
            vec.wait_ge(r_mm, 2)
            total = bank[3][:, 1, 0:NT * E].rearrange("p (t e) -> p t e", e=E)
            chain(vec.tensor_copy(rt[0][:, :, :], total))
            a, b_ = rt[0], rt[1]
            k = 1
            while k < NT:
                chain(vec.tensor_copy(b_[:, 0:k, :], a[:, 0:k, :]),
                      vec.tensor_tensor(b_[:, k:, :], a[:, k:, :], a[:, 0:NT - k, :], ALU.add))
                a, b_, k = b_, a, 2 * k
            upto, free = a, b_
            rank = bank[3][:, 0, 0:NT * E].rearrange("p (t e) -> p t e", e=E)
            chain(vec.tensor_tensor(rc[:, :, :], upto[:, NT - 1, :].unsqueeze(2).to_broadcast([P, E, NT]),
                                    iota_t[:, :].unsqueeze(1).to_broadcast([P, E, NT]), ALU.is_gt),
                  vec.tensor_tensor(rt[3][:, :, :], rank, upto[:, :, :], ALU.add))
            chain(vec.tensor_reduce(rce[:, 0, :], rc[:, :, :], AX, ALU.add),
                  vec.tensor_tensor(free[:, :, :], rt[3][:, :, :], total, ALU.subtract))
            a, k = 0, 1
            for b_ in (1, 2, 3):
                chain(vec.tensor_copy(rce[:, b_, 0:k], rce[:, a, 0:k]),
                      vec.tensor_tensor(rce[:, b_, k:], rce[:, a, k:], rce[:, a, 0:E - k], ALU.add))
                a, k = b_, 2 * k
            chain(vec.tensor_tensor(rce[:, 1, :], rce[:, 3, :], rce[:, 0, :], ALU.subtract),
                  vec.tensor_tensor(rx[:, :, :], iota_x[:, :].unsqueeze(2).to_broadcast([P, NX + 4, E]),
                                    rce[:, 3, :].unsqueeze(1).to_broadcast([P, NX + 4, E]), ALU.is_ge))
            chain(vec.tensor_scalar(rce[:, 2, :], rce[:, 1, :], float(P), None, ALU.mult),
                  vec.tensor_reduce(rxs[:, :], rx[:, :, :], AX, ALU.add))
            chain(vec.tensor_tensor(rt[3][:, :, :], free[:, :, :],
                                    rce[:, 2, :].unsqueeze(1).to_broadcast([P, NT, E]), ALU.add),
                  vec.tensor_scalar(te[:, :], rxs[:, :], float(E - 1), None, ALU.min))
            chain(*[vec.tensor_tensor(to, rt[3][:, :, :], chosen[:, :, :], ALU.mult)
                    for to, chosen in ((rt[0][:, :, :], rt[2]), (rt[1][:, :, :], rt[5]))])
            chain(*[vec.tensor_reduce(rs[:, 7 + k, :], rt[k][:, :, :], AX, ALU.add) for k in range(TOPK)])
            chain(vec.tensor_copy(pos[:, :, :], rs[:, 7:9, :]))
            assert steps[0] == ROUTE_PLACES, steps
            for b in range(1, B):
                rest_of(vec, b)

            vec.wait_ge(r_exp, 1)
            chain(vec.tensor_scalar(rs[:, 6, :], rs[:, 5, :], 1.0, None, ALU.add))
            chain(vec.reciprocal(prob[:, :, 0], rs[:, 6, :]))
            chain(vec.tensor_tensor(prob[:, :, 1], rs[:, 5, :], prob[:, :, 0], ALU.mult))
            assert steps[0] == ROUTE_STEPS, steps

            def attention_vec(i, masks=False):
                def mask(x):
                    if masks and x >= 0 and DIAG[x % NH // 2]:
                        vec.wait_ge(w_done, i * (4 * NH) + 2 * (x + 1))
                        vec.tensor_tensor(W[x % NW][:, :, 0:P], W[x % NW][:, :, 0:P],
                                          causal[:, :].unsqueeze(1).to_broadcast([P, 2, P]), ALU.mult).then_inc(w_mask, 1)

                for x in range(2 * NH):
                    par, h = divmod(x, NH)
                    for m, (at_h, e) in enumerate(PIECE_OF):
                        if at_h == h and e == "V":
                            q = i * 2 + par
                            vec.wait_ge(p_ready, q * NP + (m + 1))
                            at = 0
                            for g, n, k, w, col in PIECES[m]:
                                to = msum[:, q, g, col:col + 1] if isinstance(q, int) else msum[:, bass.ds(q, 1), g, col]
                                last = vec.tensor_scalar(junk[m % NPB][:, at:at + w], piece(m)[:, at:at + w], 0.0, None,
                                                         ALU.max, ALU.add, accum_out=to)
                                at += w
                            last.then_inc(p_used["V"], 1)
                    w = HALF - LOW[h // 2]
                    wait(vec, r_used, i * (2 * NH) + (x - NW + 1))
                    for r in range(2):
                        vec.wait_ge(u_ready, i * (4 * NH) + (2 * x + r + 1))
                        vec.scalar_tensor_tensor(W[x % NW][:, r, 0:w], score(2 * x + r)[:, 0:w], 0.0,
                                                 U[x % NU][:, r, 0:w], ALU.max, ALU.mult).then_inc(w_done, 1)
                    mask(x - 1)
                mask(2 * NH - 1)

            for par in range(2):
                vec.wait_ge(part_out[par], 32 * (B // 2) + 1)
            attention_vec(0, True)
            with vec.Fori(1, MID) as i:
                attention_vec(i)

            vec.wait_ge(w_ffn, 16 * (2 * E + 6))

            def ffn_vec(i, t, par, lo, hi, expert):
                o = 1 - par
                if lo >= 1 and hi > -1:
                    e = expert(1)
                    vec.wait_ge(f["mx"], i)
                    vec.tensor_tensor(xb[o][:, :], bank[0][:, 1, :], b12[:, bass.ds(e, 1), :].rearrange("p a n -> p (a n)"),
                                      ALU.add).then_inc(f["bx"], 1)
                    vec.wait_ge(f["bx"], i)
                    wait(vec, f["tz"], i - 2)
                    vec.tensor_tensor(zb[o][:, :], xb[o][:, 0:F], xb[o][:, F:2 * F], ALU.mult).then_inc(f["z"], 1)
                if lo >= 3 and hi > -3:
                    e = expert(3)
                    vec.wait_ge(f["mg"], i - 2)
                    wait(vec, f["sl"], i - 4)
                    vec.tensor_tensor(gb[o][:, :], bank[1][:, 1, 0:F], bgs[:, bass.ds(e, 1), :].rearrange("p a n -> p (a n)"),
                                      ALU.add).then_inc(f["bg"], 1)
                if lo >= 5:
                    e = expert(5)
                    vec.wait_ge(f["my"], i - 4)
                    wait(vec, fy[o], (t + (par - 7) // 2 + 1) * 16)
                    vec.tensor_tensor(yb[o][:, :], bank[2][:, 1, 0:C], b3s[:, bass.ds(e, 1), :].rearrange("p a n -> p (a n)"),
                                      ALU.add).then_inc(f["by"], 1)

            es = experts(mybir.EngineType.DVE, 0)
            for i in range(8):
                ffn_vec(i, i // 2, i % 2, i, 1, lambda back: es[i - back + 1])
            with vec.Fori(2, NX // 4) as t:
                es = experts(mybir.EngineType.DVE, t)
                for k in range(4):
                    ffn_vec(t * 4 + k, t * 2 + k // 2, k % 2, 9, 1, lambda back: es[k - back + 5])
            es = experts(mybir.EngineType.DVE, NX // 4)
            for i in range(NX, NX + 5):
                ffn_vec(i, i // 2, i % 2, 9, NX - i, lambda back: es[min(i - NX - back + 5, 7)])

            for par in range(2):
                vec.wait_ge(fy[par], 16 * NX // 2)
            attention_vec(MID, True)

            vec.wait_ge(s_gain, 2)
            vec.reciprocal(gsign[:, 2:3], gsign[:, 1:2]).then_inc(s_gain, 1)
            wait_pieces(vec)
            vec.wait_ge(u_used, NQ * NH)
            by_n = msum[:, :, :, :].rearrange("p q g n -> p n (q g)")
            for n in range(TB):
                to = mrow[:, n % (TB // CH), n // (TB // CH) * B * H:(n // (TB // CH) + 1) * B * H]
                if n == TB - 1:
                    last = vec.memset(to, 0.0)
                elif TB - 1 + n < MCOLS:
                    vec.tensor_tensor(to, by_n[:, n, :], by_n[:, TB - 1 + n, :], ALU.add)
                else:
                    vec.tensor_copy(to, by_n[:, n, :])
            last.then_inc(m_row, 1)
            vec.wait_ge(s_gain, 4)
            vec.tensor_tensor(gsign[:, 3:4], gsign[:, 2:3], gsign[:, 2:3], ALU.mult).then_inc(s_gain, 1)
            vec.wait_ge(x_again, 16)
            vec.tensor_tensor(xr[:, :, :], xr[:, :, :], bp[:, :].unsqueeze(1).to_broadcast([P, NT, C]),
                              ALU.add).then_inc(res_x, 1)
            vec.wait_ge(gathered, 16 * 2 * NT)
            for k in range(TOPK):
                vec.wait_ge(res_x, 1 + k)
                for t in range(NT):
                    last = vec.scalar_tensor_tensor(xr[:, t, :], gat[:, k, t, :], prob[:, t, k:k + 1], xr[:, t, :],
                                                    ALU.mult, ALU.add)
                last.then_inc(res_x, 1)
            vec.wait_ge(fin_in, 32)
            vec.wait_ge(ms_t, 1)
            vec.tensor_tensor(fw[:, 1, :], sums[:, 1, :], bank[0][:, 0, :], ALU.add).then_inc(fin_v, 1)
            vec.wait_ge(fin_v, 1)
            vec.tensor_scalar(fw[:, 2, :], fw[:, 1, :], 2.0 / T, SMALL, ALU.mult, ALU.add).then_inc(fin_v, 1)
            vec.wait_ge(fin_v, 2)
            vec.wait_ge(s_gain, 5)
            vec.scalar_tensor_tensor(fw[:, 1, :], fw[:, 2, :], gsign[:, 3:4], fw[:, 2, :], ALU.mult, ALU.mult).then_inc(fin_v, 1)
            vec.wait_ge(fin_v, 3)
            vec.tensor_tensor(fw[:, 2, :], fw[:, 1, :], fw[:, 1, :], ALU.mult).then_inc(fin_v, 1)
            vec.wait_ge(fin_v, 4)
            vec.scalar_tensor_tensor(fw[:, 1, :], fw[:, 2, :], SMALL, sums[:, 0, :], ALU.mult, ALU.add).then_inc(fin_v, 1)
            vec.wait_ge(fin_v, 5)
            vec.tensor_scalar(fw[:, 2, :], fw[:, 1, :], TINY, None, ALU.max).then_inc(fin_v, 1)
            vec.wait_ge(fin_v, 6)
            vec.reciprocal(fw[:, 0, :], fw[:, 2, :]).then_inc(fin_v, 1)

            def scaled(b):
                vec.wait_ge(y_in[b], 16)
                vec.wait_ge(rb_mm, b + 1)
                vec.tensor_tensor(yT[b][:, :], yT[b][:, :], flat[b % 2], ALU.mult).then_inc(yn_ready, 1)

            scaled(0)
            vec.wait_ge(res_x, 1 + TOPK)
            for b in range(B):
                if b + 1 < B:
                    scaled(b + 1)
                for hb in range(2):
                    vec.wait_ge(proj, 2 * b + hb + 1)
                    half = xr[:, b * TB + 4 * hb:b * TB + 4 * hb + 4, :].rearrange("p t c -> p (t c)")
                    vec.tensor_tensor(half, bank[2 + hb][:, 0, :], half, ALU.add).then_inc(res_half, 1)


_INS = ["L0_attn_x", "L0_attn_W_attn", "L0_attn_b_attn", "L0_attn_W_proj", "L0_attn_b_proj", "L0_attn_score_gain",
        "L0_ffn_gate_w", "L0_ffn_gate_b", "L0_ffn_w1", "L0_ffn_b1", "L0_ffn_w2", "L0_ffn_b2", "L0_ffn_wg",
        "L0_ffn_bg", "L0_ffn_w3", "L0_ffn_b3"]


def kernel(**inputs):
    import numpy as np
    import concourse.bacc as bacc
    from concourse.bass_utils import run_bass_kernel_spmd

    nc = bacc.Bacc("TRN2", target_bir_lowering=False, num_devices=1)
    arrays, args = {}, []
    for name in _INS:
        a = np.ascontiguousarray(inputs[name])
        if a.size == 1:
            a = a.reshape(1, 1)
        arrays["in_" + name] = a
        args.append(nc.dram_tensor("in_" + name, a.shape, mybir.dt.from_np(a.dtype), kind="ExternalInput").ap())
    shape = np.asarray(inputs["L0_attn_x"]).shape
    args.append(nc.dram_tensor("out", shape, F32, kind="ExternalOutput").ap())
    layer_kernel(nc, *args)
    r = run_bass_kernel_spmd(nc, [arrays], core_ids=[0])
    return r.results[0]["out"]
```

```python
from contextlib import ExitStack

import concourse.bass as bass
from concourse import mybir

F32 = mybir.dt.float32
BF16 = mybir.dt.bfloat16
I32 = mybir.dt.int32
ALU = mybir.AluOpType
ACT = mybir.ActivationFunctionType
AX = mybir.AxisListType.X

P = 128
LN_EPS = 1e-5
SMALL = 1e-6
HUGE = 1e30
TINY = 1e-37

HALF = 512
TERMS = ((0, 3, 0), (3, 5, 1), (5, 6, 2))
NK = 6
VW = 10
SUM_R, SUM_U = 8, 9


def wait(engine, semaphore, value):
    if isinstance(value, int) and value <= 0:
        return
    engine.wait_ge(semaphore, value)


def layer_kernel(nc, x, w_attn, b_attn, w_proj, b_proj, score_gain, gate_w, gate_b,
                 w1, b1, w2, b2, wg, bg, w3, b3, out):
    B, T, C = x.shape
    E, _, F = w1.shape
    H = 16
    D = C // H
    N = B * T
    NT = N // P
    TB = T // P
    assert C == P and D == 8 and F == 2 * P
    TOPK = 2
    NX = -(-(N * TOPK + E * (P - 1)) // P)
    NX += -NX % 4
    XW = C + 2
    NQ = B * H // 4
    CH = T // HALF
    STEPS = [(c, j) for c in range(CH) for j in range(TB) if P * j < HALF * (c + 1)]
    NS = len(STEPS)
    NH = 2 * NS
    LOW = [max(0, P * j - HALF * c) for c, j in STEPS]
    DIAG = [P * j >= HALF * c for c, j in STEPS]
    ND = 2 * sum(DIAG)
    masks_to = lambda y: y // NH * ND + sum(DIAG[z // 2] for z in range(y % NH + 1))
    PIECES, MCOLS = [], TB - 1
    for g in range(4):
        short = []
        for n in range(TB - 1):
            k, w = P * (n + 1), T - P * (n + 1)
            if w < HALF:
                short.append((g, n, k, w, n))
                continue
            PIECES.append([(g, n, k, HALF, n)])
            if w > HALF:
                short.append((g, n, k + HALF, w - HALF, TB - 1 + n))
        while short:
            a = short.pop(0)
            fits = [b for b in short if a[3] + b[3] == HALF]
            short.remove(fits[0])
            PIECES.append([a, fits[0]])
    MCOLS += (TB - 1) // 2
    NP = len(PIECES)
    ENDS = [max(k for k in range(NS) if STEPS[k][0] == c) for c in range(CH)]
    LAST = [2 * max(k for k in range(NS) if STEPS[k][0] == c) + 1 for c in range(CH)]
    PLAN = ["A", "V", "VA", "VA", "V", "VA", "VA", "VA", "", "V", "", "", "V", "", "", "",
            "V", "VA", "V", "VA", "VA", "VA", "V", "VA"]
    PIECE_OF = [(h, e) for h in range(NH) for e in PLAN[h]]
    assert len(PIECE_OF) == NP
    R_POOL = {1, 3, 5, 7, 8, 10, 12, 14, 15, 19, 21, 23}
    RLAG, AVLAG = 2, 5
    NU, NW = 8, 8
    NSLOT, NPB = 5, 2
    QUAD_SLOTS = -(-4 * NS // NSLOT) * NSLOT
    slot_of = lambda n: n % (4 * NS) % NSLOT

    def slot_free(n):
        q, k = divmod(n, 4 * NS)
        v = q * QUAD_SLOTS + k - NSLOT
        return v // QUAD_SLOTS * 4 * NS + min(v % QUAD_SLOTS + 1, 4 * NS)

    def pieces_done(m, engine):
        q, k = divmod(m, NP)
        return q * sum(e == engine for _, e in PIECE_OF) + sum(e == engine for _, e in PIECE_OF[:k + 1])

    NE = B - 1
    MID = NQ // 2 - 1

    def by_pool(i, y):
        if isinstance(i, int) and (i == 0 and y < POOL_FROM or i > 0 and y < 0):
            return False
        return y % NH in R_POOL

    POOL_FROM = 2 * NH - 16
    DRAIN = ((0, 1), (2, 3), (4, 5))
    ROUTE_M, ROUTE_PLACES, ROUTE_STEPS = 12, 29, 32

    ctx = ExitStack()
    with ctx:
        def sb(name, shape, dt=F32):
            return ctx.enter_context(nc.sbuf_tensor(name, shape, dt))

        def sem(name):
            return ctx.enter_context(nc.semaphore(name))

        def dram(name, shape, dt=F32):
            return nc.dram_tensor(name, shape, dt, kind="Internal").ap()

        qk_d = dram("qk_stacked", [2, B * P, NK, T], BF16)
        v_d = dram("v_stationary", [NQ, P, TB, 4 * VW])
        y_d = dram("attention_of_v", [B * H, D, T])
        s_d = dram("sums_of_r_and_u", [2, B * H, T])
        r_d = dram("scales", [NE, H, TB, P])
        xs_d = dram("sorted_x", [NX * P, XW])
        ys_d = dram("weighted_y", [N * TOPK + 4 * P, C])

        ident = sb("ident", [P, P])
        tri = sb("earlier", [P, P])
        ones = sb("ones", [P, P])
        causal = sb("causal", [P, P])
        usel = sb("usel", [P, VW])
        iota8 = sb("iota8", [P, E])
        iota_t = sb("iota_t", [P, NT])
        iota_x = sb("iota_x", [P, NX + 4])
        wa = sb("wa", [P, 3 * C + E])
        wp = sb("wp", [P, C])
        bq = sb("bq", [P, 1])
        bq_s = sb("bq_s", [P, 1])
        bv = sb("bv", [P, C])
        sel = sb("sel", [P, TB, C])
        bgate = sb("bgate", [P, E])
        bp = sb("bp", [P, C])
        gain = sb("gain", [P, 1])
        gsign = sb("gsign", [P, 4])
        xn_row = sb("xn_row", [P, NT, XW])
        xn = xn_row[:, :, 0:C]
        xt4 = sb("xt4", [P, 4, XW])
        row_info = sb("row_info", [P, NX, 2])
        row_to = [sb(f"row_to{i}", [P, 1], I32) for i in range(4)]
        logit = sb("logit", [P, NT, E])
        prob = sb("prob", [P, NT, 2])
        pos = sb("pos", [P, 2, NT], I32)
        te = sb("te", [P, NX + 4], I32)
        gate_v, gate_p = sb("gate_v", [P, 1]), sb("gate_p", [P, NX])
        msum = sb("msum", [P, NQ, 4, MCOLS])

        weights = ExitStack()
        w12, wgs, w3s, b12, bgs, b3s = [weights.enter_context(nc.sbuf_tensor(name, shape, F32)) for name, shape in (
            ("w12", [P, E, 2 * F]), ("wgs", [P, E, 2, F]), ("w3s", [P, E, 2, C]),
            ("b12", [P, E, 2 * F]), ("bgs", [P, E, F]), ("b3s", [P, E, C]))]
        weights.close()
        xr = xn
        x_t = weights.enter_context(nc.sbuf_tensor("x_t", [P, NT, C], F32))
        qkf = x_t[:, :, :].rearrange("p n c -> p (n c)").rearrange("p (a s t) -> p a s t", a=2, s=2)
        early = weights.enter_context(ExitStack())
        xnb = [early.enter_context(nc.sbuf_tensor(f"xnb{i}", [P, TB, C], F32)) for i in range(2)]
        xnT = [early.enter_context(nc.sbuf_tensor(f"xnT{i}", [P, T], F32)) for i in range(2)]
        vb = [early.enter_context(nc.sbuf_tensor(f"vb{i}", [P, 4, TB, 4, VW], F32)) for i in range(2)]
        xnT_all = early.enter_context(nc.sbuf_tensor("xnT_all", [P, B, T], F32))
        early.close()
        parts = [weights.enter_context(nc.sbuf_tensor(f"parts{b}", [P, 2, 3, T], BF16)) for b in (0, 2)]
        weights.enter_context(nc.sbuf_tensor("rest_of_vb", [P, 2 * (TB * C + T + 4 * TB * 4 * VW) - 6 * T], F32))
        parts.append(weights.enter_context(nc.sbuf_tensor("parts3", [P, 2, 3, T], BF16)))
        weights.close()
        gat = sb("gat", [P, 2, NT, C])
        mrow_l, sums_l, fw_l = sb("mrow_l", [P, 1, H, TB]), sb("sums_l", [P, 2, 1, P]), sb("fw_l", [P, 3, P])
        yT_l = sb("yT_l", [P, T])
        sb("rest_of_weights", [P, E * (7 * F + 3 * C) - 2 * NT * C - T - 6 * P])

        xt = [xt4[:, i, :] for i in range(4)]

        bank = [ctx.enter_context(nc.psum_tensor(f"bank{i}", [P, 2, HALF], F32)) for i in range(4)]

        c_pool, c_vec = sem("constants_pool"), sem("constants_vec")
        w_in, w_ffn = sem("small_weights_in"), sem("ffn_weights_in")
        x_in, w_late = [sem("x_in0"), sem("x_in1")], sem("late_weights_in")
        xn_ready = [sem("xn_ready_vec"), sem("xn_ready_pool")]
        s_gain = sem("gain_sign")
        ln_v, ln_s = sem("ln_vector"), sem("ln_sqrt")
        xnb_ready, tr_done, xnT_ready = sem("xnb_ready"), sem("xn_transposed"), sem("xnT_ready")
        xnT_kept = sem("xnT_kept")
        q_mm, k_mm, v_mm = sem("q_mm"), sem("k_mm"), sem("v_mm")
        qk_f = sem("qk_float_ready")
        v_ev, lg_ev, k_mean, m_mm = sem("v_evacuated"), sem("logits_evacuated"), sem("k_mean"), sem("k_mean_mm")
        part_a, part_b = sem("part_rounded"), sem("second_part_rounded_vec")
        part_v, part_p = [[sem(f"{n}_{e}") for e in ("pool", "vec")] for n in ("part_rest", "last_part_rounded")]
        part_out = [sem(f"parts_stored{b}") for b in range(B)]
        v_out = [sem("v_stored0"), sem("v_stored1")]
        route, r_mm, r_exp = sem("route"), sem("route_mm"), sem("route_exp")
        z_out, row_end, xs_out = sem("xs_emptied"), sem("row_ends"), sem("xs_scattered")
        qk_in = [sem("quad_in0"), sem("quad_in1")]
        s_ready, u_ready, w_done, w_mask = sem("scores_ready"), sem("u_ready"), sem("w_done"), sem("w_masked")
        r_ready = [sem(f"r_ready{i}") for i in range(NW)]
        r_used, u_used = sem("r_used"), sem("u_used")
        acc_ev = sem("acc_evacuated")
        y_out, s_out = [sem("y_stored0"), sem("y_stored1")], [sem("sums_stored0"), sem("sums_stored1")]
        p_ready, p_used = sem("piece_ready"), {"V": sem("piece_used_vec"), "A": sem("piece_used_act")}
        fx = [sem(f"ffn_x_in{i}") for i in range(4)]
        fy = [sem(f"ffn_y_out{i}") for i in range(4)]
        f = {n: sem("ffn_" + n) for n in
             ("tx", "cx", "mx", "bx", "z", "tz", "cz", "mg", "bg", "sl", "ts", "cs", "my", "by", "wy")}
        rows_in = sem("row_info_in")
        m_row = sem("piece_sums_by_row")
        sums_in, fin_v, ms_t, rb_mm = sem("sums_in"), sem("scales_vec"), sem("ms_transposed"), sem("scales_by_row")
        sc_out, sc_in = sem("scales_stored"), [sem(f"scales_in{b}") for b in range(NE)]
        y_in, yn_ready, proj = [sem(f"y_in{b}") for b in range(B)], sem("yn_ready"), sem("proj")
        x_again, res_x, res_y = sem("x_in_again"), sem("x_and_bias"), sem("attention_added")
        B_POOL = 2
        res_p, res_v = sem("experts_added_pool"), sem("experts_added_vec")
        gathered = [sem(f"gathered{b}") for b in range(B)]
        res_out = sem("result_out")

        phase = ExitStack()

        def tmp(name, shape, dt=F32):
            return phase.enter_context(nc.sbuf_tensor(name, shape, dt))

        st = tmp("st", [P, TB, 6])
        mvb = tmp("mvb", [P, TB, 2])
        mv = tmp("mv", [P, NT, 2])
        lnw = tmp("lnw", [P, 5, NT])
        ksum = tmp("ksum", [P, B])
        k_off = tmp("k_off", [P, 2])
        rt = [tmp(f"rt{i}", [P, NT, E]) for i in range(6)]
        rs = tmp("rs", [P, 12, NT])
        rx = tmp("rx", [P, NX + 4, E])
        rxs = tmp("rxs", [P, NX + 4])
        rc = tmp("rc", [P, E, NT])
        rce = tmp("rce", [P, 4, E])
        phase.close()

        phase.enter_context(nc.sbuf_tensor("before_rest", [P, NU * 2 * HALF], F32))
        rest = [tmp(f"rest{i}", [P, 2, T]) for i in range(2)]
        tmp("before_parts1", [P, NW * 2 * HALF - 4 * T])
        parts.insert(1, tmp("parts1", [P, 2, 3, T], BF16))
        phase.close()

        U = [tmp(f"U{i}", [P, 2, HALF]) for i in range(NU)]
        W = [tmp(f"W{i}", [P, 2, HALF]) for i in range(NW)]
        yq = [tmp(f"yq{i}", [P, CH, HALF]) for i in range(2)]
        yb = [tmp(f"yb{i}", [P, C]) for i in range(4)]
        tmp("rest_of_parts", [P, 3 * T - 2 * CH * HALF - 4 * C])
        junk = [tmp(f"junk{i}", [P, HALF], BF16) for i in range(NPB)]
        QS = [tmp(f"QS{i}", [P, 2, T], BF16) for i in range(2)]
        KS = [tmp(f"KS{i}", [P, 4, T], BF16) for i in range(2)]
        VS = [tmp(f"VS{i}", [P, TB, 4, VW]) for i in range(2)]
        phase.close()

        xb = [tmp(f"xb{i}", [P, 2 * F]) for i in range(2)]
        xT = [tmp(f"xT{i}", [P, C]) for i in range(2)]
        zb = [tmp(f"zb{i}", [P, F]) for i in range(2)]
        tmp("rest_of_U1", [P, 2 * (2 * HALF) - 2 * (2 * F + C + F)])
        yT = [tmp(f"yT{i}", [P, T]) for i in range(NE)]
        scale = [tmp(f"scale{i}", [P, T]) for i in range(NE)]
        tmp("before_W1", [P, (NU - 1) * 2 * HALF - 2 * NE * T])
        zT = [tmp(f"zT{i}", [P, 2, P]) for i in range(2)]
        gb = [tmp(f"gb{i}", [P, F]) for i in range(2)]
        sg = [tmp(f"sg{i}", [P, F]) for i in range(2)]
        sT = [tmp(f"sT{i}", [P, 2, P]) for i in range(2)]
        mrow, sums, fw = tmp("mrow", [P, NE, H, TB]), tmp("sums", [P, 2, NE, P]), tmp("fw", [P, 3, NE * P])
        phase.close()

        x_v = x.rearrange("b (t p) c -> p (b t) c", p=P)
        out_v = out.rearrange("b (t p) c -> p (b t) c", p=P)
        flat = [bk[:, :, :].rearrange("p a n -> p (a n)") for bk in bank]
        row = lambda v: v.rearrange("(a n) -> a n", a=1)
        s_q = s_d.rearrange("k (q g) t -> q k g t", g=4)
        VG = C + E
        in_bank = HALF // VG
        v_banks = lambda par: [(t, min(in_bank, TB - t), (bank[par][:, 0, :], bank[par][:, 1, :], bank[2][:, par, :])[t // in_bank])
                               for t in range(0, TB, in_bank)]
        v_tiles = lambda at, n: at[:, 0:n * VG].rearrange("p (t c) -> p t c", c=VG)
        v_bias = bv[:, :].unsqueeze(1).to_broadcast([P, TB, C])
        qk_q = qk_d.rearrange("s (q hh r d) k t -> s q r (d k) hh t", hh=2, r=2, d=D)

        def rows_of(ap, n):
            return ap.to_broadcast([P, n])

        score = lambda n: bank[slot_of(n) // 2][:, slot_of(n) % 2, :]
        piece = lambda m: bank[2 + m % NPB][:, 1, :]

        def piece_sums(engine, bs, to, quads):
            for e in "VA":
                engine.wait_ge(p_used[e], pieces_done(NP * quads - 1, e))
            by_n = msum[:, :, :, :].rearrange("p (b q) g n -> p n b (q g)", b=B)
            for n in range(TB):
                if n == TB - 1:
                    engine.memset(to[:, :, :, n], 0.0).then_inc(m_row, 1)
                elif TB - 1 + n < MCOLS:
                    engine.tensor_tensor(to[:, :, :, n], by_n[:, n, bs, :], by_n[:, TB - 1 + n, bs, :], ALU.add).then_inc(m_row, 1)
                else:
                    engine.tensor_copy(to[:, :, :, n], by_n[:, n, bs, :]).then_inc(m_row, 1)

        rounds = [x for b in range(B + 1) for x in ((b, 0), (b - 1, 1)) if 0 <= x[0] < B and x[0] < B - 2 * x[1]]
        rounded = lambda b, n, s: 2 * rounds.index((b, n)) + 2 - s

        def take_off(engine, b, s, n):
            e, par = divmod(b, 2)
            if n == 0:
                engine.wait_ge(part_a, rounded(b, 0, s))
                if e:
                    engine.wait_ge(part_p[0], 2 * par + 2 - s)
                engine.tensor_tensor(rest[par][:, s, :], qkf[:, par, s, :], parts[b][:, s, 0, :], ALU.subtract).then_inc(part_v[e], 1)
            else:
                engine.wait_ge(part_b if e else part_a, 2 * par + 2 - s if e else rounded(b, 1, s))
                engine.wait_ge(part_v[e], 2 * par + 2 - s)
                engine.tensor_tensor(parts[b][:, s, 2, :], rest[par][:, s, :], parts[b][:, s, 1, :],
                                     ALU.subtract).then_inc(part_p[e], 1)

        def experts(engine, t):
            at = 4 * (t - 1) if not isinstance(t, int) or t else 0
            return nc.values_load_multi_w_load_instructions(
                te[0:1, at:at + 8] if isinstance(at, int) else te[0:1, bass.ds(at, 8)], engines=[engine],
                min_val=0, max_val=E - 1, skip_runtime_bounds_check_because="te is a minimum with E - 1")[1]

        block = ctx.enter_context(nc.Block())

        @block.sync
        def _(sp):
            for b in range(B):
                wait(sp, x_in[b % 2], b // 2 * 16)
                sp.dma_start(x_t[:, b * TB:(b + 1) * TB, :], x_v[:, b * TB:(b + 1) * TB, :]).then_inc(x_in[b % 2], 16)
            sp.wait_ge(c_pool, 13)
            empty_rows = xs_d.rearrange("(k four p) c -> p k four c", four=4, p=P)
            for k in range(4):
                sp.dma_start(empty_rows[:, :, k, :], xt4[:, k:k + 1, :].to_broadcast([P, NX // 4, XW])).then_inc(z_out, 16)
            with sp.Fori(0, B // 2) as i:
                for par in range(2):
                    sp.wait_ge(v_ev, i * 2 + par + 3)
                    for hq in range(4):
                        sp.dma_start(v_d[i * 8 + par * 4 + hq].rearrange("p t n -> p (t n)"),
                                     vb[par][:, hq].rearrange("p t g n -> p (t g n)")).then_inc(v_out[par], 16)

            def load_quad(q, par):
                for r in range(2):
                    rows = slice(64 * r, 64 * r + NK * D)
                    sp.dma_start(QS[par][rows, :, :], qk_q[0, q, r]).then_inc(qk_in[par], 16)
                    sp.dma_start(KS[par][rows, r::2, :], qk_q[1, q, r]).then_inc(qk_in[par], 16)
                sp.dma_start(VS[par][:, :, :, :].rearrange("p t g n -> p t (g n)"), v_d[q]).then_inc(qk_in[par], 16)

            def store_quad(q, i, par):
                sp.wait_ge(acc_ev, (q + 1) * CH)
                for k, at in enumerate((SUM_R, SUM_U)):
                    sp.dma_start(s_q[q, k], yq[par][at::32, :, :].rearrange("g c n -> g (c n)")).then_inc(s_out[par], 16)
                for g in range(4):
                    sp.dma_start(y_d[q * 4 + g], yq[par][32 * g:32 * g + D, :, :].rearrange("p c n -> p (c n)"),
                                 ).then_inc(y_out[par], 16)

            for b in range(B):
                of_b = parts[b]
                for n in range(3):
                    for s in (1, 0):
                        if n < 2:
                            wait(sp, *((part_a, rounded(b, n, s)) if n == 0 or b < B // 2 else (part_b, 2 * (b % 2) + 2 - s)))
                        else:
                            sp.wait_ge(part_p[b // 2], 2 * (b % 2) + 2 - s)
                        k, to, part = TERMS[2 - n if s else n]
                        some = of_b[:, 1, 0:to - k, :] if s else of_b[:, 0, part:part + 1, :].to_broadcast([P, to - k, T])
                        sp.dma_start(qk_d[s, b * P:(b + 1) * P, k:to, :], some).then_inc(part_out[b], 16)
                if b == 0:
                    for par in range(2):
                        sp.wait_ge(v_out[par], 64 * (B // 2) + 1)
                    sp.wait_ge(part_out[0], 96)
                    sp.wait_ge(c_pool, 17)
                    load_quad(0, 0)
                if b == 1:
                    load_quad(1, 1)
            def next_quad(i, par):
                store_quad(i * 2 + par, i, par)
                sp.wait_ge(u_used, i * (2 * NH) + (par + 1) * NH)
                load_quad(i * 2 + (par + 2), par)

            for par in range(2):
                next_quad(0, par)
            for b in range(B):
                sp.wait_ge(part_out[b], 96)
            for to, w in ((w12[:, :, 0:F], w1), (w12[:, :, F:2 * F], w2)):
                sp.dma_start(to, w.rearrange("e c n -> c e n")).then_inc(w_ffn, 16)
            for e in range(E):
                sp.dma_start(wgs[:, e, :, :], wg[e].rearrange("(k p) n -> p k n", p=P)).then_inc(w_ffn, 16)
                sp.dma_start(w3s[:, e, :, :], w3[e].rearrange("(k p) n -> p k n", p=P)).then_inc(w_ffn, 16)
            for to, v, n in ((b12[:, :, 0:F], b1, F), (b12[:, :, F:2 * F], b2, F), (bgs[:, :, :], bg, F), (b3s[:, :, :], b3, C)):
                sp.dma_start(to, v.rearrange("(a e) n -> a e n", a=1).to_broadcast([P, E, n])).then_inc(w_ffn, 16)
            with sp.Fori(1, MID - 1) as i:
                for par in range(2):
                    next_quad(i, par)
            sp.wait_ge(xs_out, 16 * TOPK * NT)
            sp.dma_start(row_info[:, :, :], xs_d.rearrange("(k p) c -> p k c", p=P)[:, :, C:XW]).then_inc(rows_in, 16)
            next_quad(MID - 1, 0)
            xs_t = xs_d.rearrange("(k p) c -> k p c", p=P)

            def ffn_sp(i, k):
                wait(sp, f["tx"], i - 3)
                sp.dma_start(xt[k][:, :], xs_t[i]).then_inc(fx[k], 16)

            for i in range(8):
                ffn_sp(i, i % 4)
            def load_y(b):
                sp.dma_start(yT[b][:, :], y_d[b * H:(b + 1) * H].rearrange("h d t -> (h d) t")).then_inc(y_in[b], 16)

            def ffn_tiles_sp(lo, hi):
                with sp.Fori(lo, hi) as t:
                    for k in range(4):
                        ffn_sp(t * 4 + k, k)

            sp.wait_ge(r_used, MID * 2 * NH)
            sp.wait_ge(u_used, MID * 2 * NH)
            for par in range(2):
                sp.wait_ge(s_out[par], 32 * (2 * NE) + par)
                sp.wait_ge(y_out[par], 64 * (2 * NE) + par)
            for k in range(2):
                sp.dma_start(sums[:, k, :, :], s_d[k, 0:NE * H].rearrange("(b h) (n t) -> (h n) b t", b=NE, t=P)).then_inc(sums_in, 16)
            store_quad(2 * MID - 1, MID - 1, 1)
            ffn_tiles_sp(2, 3)
            sp.dma_start(xr[:, :, :], x_v).then_inc(x_again, 16)
            ffn_tiles_sp(3, 4)
            for b in range(NE):
                load_y(b)
            ffn_tiles_sp(4, 7)
            sp.wait_ge(fin_v, 7 * NE)
            sp.dma_start(r_d.rearrange("b h n t -> (h n) b t"), fw[:, 0, :].rearrange("p (b t) -> p b t", t=P)).then_inc(sc_out, 16)
            ffn_tiles_sp(7, 8)
            sp.wait_ge(sc_out, 16)
            for b in range(NE):
                sp.dma_start(scale[b][:, :], r_d[b].rearrange("h (a n) t -> h a (n t)", a=1).to_broadcast([H, D, T]),
                             ).then_inc(sc_in[b], 16)
            ffn_tiles_sp(8, NX // 4)

            load_quad(NQ - 1, 1)
            for stored in fy:
                sp.wait_ge(stored, 16 * NX // 4)
            y_v = ys_d[0:TOPK * N].rearrange("(k t p) c -> p k t c", k=TOPK, p=P)
            for b in range(B):
                for k in range(TOPK):
                    tiles = slice(b * TB, (b + 1) * TB)
                    sp.dma_start(gat[:, k, tiles, :], y_v[:, k, tiles, :]).then_inc(gathered[b], 16)
            for par in range(2):
                sp.wait_ge(s_out[par], 32 * MID + par)
                sp.wait_ge(y_out[par], 64 * MID + par)
            h_in = 4 * (2 * MID - 4 * NE)
            for k in range(2):
                sp.dma_start(sums_l[0:h_in * TB, k, 0, :], s_d[k, NE * H:NE * H + h_in].rearrange("h (n t) -> (h n) t", t=P),
                             ).then_inc(sums_in, 16)
            sp.dma_start(yT_l[0:h_in * D, :], y_d[NE * H:NE * H + h_in].rearrange("h d t -> (h d) t")).then_inc(y_in[NE], 16)
            for par in range(2):
                sp.wait_ge(acc_ev, (2 * MID + par + 1) * CH)
                rows = slice((h_in + 4 * par) * TB, (h_in + 4 * par + 4) * TB)
                for k, at in enumerate((SUM_R, SUM_U)):
                    sp.dma_start(sums_l[rows, k, 0, :], yq[par][at::32, :, :].rearrange("g c (n t) -> g (c n) t", t=P),
                                 ).then_inc(sums_in, 16)
                for g in range(4):
                    h = h_in + 4 * par + g
                    sp.dma_start(yT_l[h * D:(h + 1) * D, :], yq[par][32 * g:32 * g + D, :, :].rearrange("p c n -> p (c n)"),
                                 ).then_inc(y_in[NE], 16)

            def store(lo, hi):
                sp.dma_start(out_v[:, lo:hi, :], xr[:, lo:hi, :]).then_inc(res_out, 16)

            sp.wait_ge(res_v, (B - B_POOL) * TOPK - 1)
            store(B_POOL * TB, NE * TB)
            for b in range(B_POOL):
                sp.wait_ge(res_p, TOPK * (b + 1))
                store(b * TB, (b + 1) * TB)
            for c in range(CH):
                sp.wait_ge(res_y, NE + c + 1)
                store(NE * TB + c * TB // CH, NE * TB + (c + 1) * TB // CH)
            sp.wait_ge(res_out, 16 * (NE + CH))

        @block.gpsimd
        def _(pool):
            pool.memset(ident[:, :], 0.0).then_inc(c_pool, 1)
            pool.memset(tri[:, :], 0.0).then_inc(c_pool, 1)
            pool.memset(ones[:, :], 1.0).then_inc(c_pool, 1)
            pool.memset(sel[:, :, :], 0.0).then_inc(c_pool, 1)
            pool.memset(xt4[:, :, :], 0.0).then_inc(c_pool, 1)
            pool.wait_ge(c_pool, 5)
            pool.iota(xt4[:, :, C], [[P, 4]], base=N * TOPK, channel_multiplier=1,
                      allow_small_or_imprecise_dtypes=True).then_inc(c_pool, 1)
            pool.affine_select(out=ident[:, :], in_=ident[:, :], compare_op=ALU.not_equal, fill=1.0, base=0,
                               pattern=[[-1, P]], channel_multiplier=1).then_inc(c_pool, 1)
            pool.affine_select(out=tri[:, :], in_=ones[:, :], compare_op=ALU.is_gt, fill=0.0, base=0,
                               pattern=[[1, P]], channel_multiplier=-1).then_inc(c_pool, 1)
            pool.affine_select(out=causal[:, :], in_=ones[:, :], compare_op=ALU.is_ge, fill=0.0, base=0,
                               pattern=[[1, P]], channel_multiplier=-1).then_inc(c_pool, 1)
            pool.affine_select(out=sel[:, :, :].rearrange("p a (m d) -> p a m d", d=D),
                               in_=sel[:, :, :].rearrange("p a (m d) -> p a m d", d=D), compare_op=ALU.not_equal, fill=1.0,
                               base=0, pattern=[[-1, TB], [-TB, H], [0, D]], channel_multiplier=1).then_inc(c_pool, 1)
            pool.iota(iota8[:, :], [[1, E]], base=-E, channel_multiplier=0,
                      allow_small_or_imprecise_dtypes=True).then_inc(c_pool, 1)
            pool.iota(iota_t[:, :], [[P, NT]], base=0, channel_multiplier=0,
                      allow_small_or_imprecise_dtypes=True).then_inc(c_pool, 1)
            pool.iota(iota_x[:, :], [[1, NX + 4]], base=-1, channel_multiplier=0,
                      allow_small_or_imprecise_dtypes=True).then_inc(c_pool, 1)
            pool.wait_ge(c_pool, 13)
            pool.wait_ge(ln_v, 3 * B + 7)
            with pool.Fori(0, B // 2) as i:
                at = bass.ds(i * 2 * TB + TB, TB)
                of_row = lambda k: lnw[:, k, at].unsqueeze(2).to_broadcast([P, TB, C])
                pool.tensor_tensor(xn[:, at, :], x_t[:, at, :], of_row(4), ALU.subtract).then_inc(xn_ready[1], 1)
                pool.wait_ge(xn_ready[1], i * 2 + 1)
                pool.tensor_tensor(xn[:, at, :], xn[:, at, :], of_row(3), ALU.mult).then_inc(xn_ready[1], 1)
            for par in range(2):
                pool.memset(QS[par][:, :, :], 0.0).then_inc(c_pool, 1)
                pool.memset(KS[par][:, :, :], 0.0).then_inc(c_pool, 1)
            for n in range(2):
                for b in range(2):
                    for s in (1, 0):
                        take_off(pool, b, s, n)

            pool.wait_ge(z_out, 16 * 4)
            pool.wait_ge(route, ROUTE_STEPS)
            for k in range(TOPK):
                wait(pool, xs_out, 16 * k * NT)
                pool.iota(xn_row[:, :, C], [[P, NT]], base=k * N, channel_multiplier=1,
                          allow_small_or_imprecise_dtypes=True).then_inc(row_end, 1)
                pool.tensor_copy(xn_row[:, :, C + 1], prob[:, :, k]).then_inc(row_end, 1)
                pool.wait_ge(row_end, 2 * k + 2)
                for t in range(NT):
                    pool.indirect_dma_start(xs_d, bass.IndirectOffsetOnAxis(pos[:, k, t:t + 1], 0),
                                            xn_row[:, t, :], None).then_inc(xs_out, 16)

            def attention_pool(i, first, drain, start=0):
                for x in range(start, 2 * NH):
                    if not drain and DIAG[x % NH // 2]:
                        pool.wait_ge(w_done, i * (4 * NH) + 2 * (x + 1))
                        pool.tensor_tensor(W[x % NW][:, :, 0:P], W[x % NW][:, :, 0:P],
                                           causal[:, :].unsqueeze(1).to_broadcast([P, 2, P]),
                                           ALU.mult).then_inc(w_mask, 1)
                    y = x - 1
                    if (y < start and first) or (y >= 0 and drain) or not by_pool(i, y):
                        continue
                    w = HALF - LOW[y % NH // 2]
                    if DIAG[y % NH // 2]:
                        pool.wait_ge(w_mask, i * (2 * ND) + masks_to(y))
                    else:
                        pool.wait_ge(w_done, i * (4 * NH) + 2 * (y + 1))
                    pool.tensor_tensor(W[y % NW][:, :, 0:w], W[y % NW][:, :, 0:w], W[y % NW][:, :, 0:w],
                                       ALU.mult).then_inc(r_ready[y % NW], 1)

            pool.wait_ge(w_mask, masks_to(POOL_FROM - 1))
            attention_pool(0, True, False, POOL_FROM)
            with pool.Fori(1, MID) as i:
                attention_pool(i, False, False)
            attention_pool(MID, False, True)

            pool.wait_ge(r_used, MID * 2 * NH)
            piece_sums(pool, slice(0, NE), mrow, 4 * NE)

            def x_and_bias(b):
                pool.wait_ge(x_again, 16)
                pool.wait_ge(w_late, 48)
                some = xr[:, b * TB:(b + 1) * TB, :]
                pool.tensor_tensor(some, some, bp[:, :].unsqueeze(1).to_broadcast([P, TB, C]), ALU.add).then_inc(res_x, 1)

            def times_scale(b):
                pool.wait_ge(y_in[b], 16)
                pool.wait_ge(sc_in[b], 16)
                pool.tensor_tensor(yT[b][:, :], yT[b][:, :], scale[b][:, :], ALU.mult).then_inc(yn_ready, 1)

            beside = [(4 + 2 * b, x_and_bias, b) for b in range(NE)] + [(10 + 2 * b, times_scale, b) for b in range(NE)]
            beside.append((16, x_and_bias, B - 1))
            done = 0
            for until, work, b in beside + [(NX // 4, None, 0)]:
                with pool.Fori(done, until) as t:
                    for k in range(4):
                        pool.wait_ge(f["wy"], (t * 4 + k + 1) * 2)
                        pool.tensor_tensor(gate_p[:, bass.ds(t * 4 + k, 1)], ones[:, 0:1], ones[:, 0:1], ALU.mult)
                        pool.indirect_dma_start(ys_d, bass.IndirectOffsetOnAxis(row_to[k][:, :], 0),
                                                yb[k][:, :], None).then_inc(fy[k], 16)
                if work:
                    work(b)
                done = until

            attention_pool(MID, True, False)
            attention_pool(MID + 1, False, True)

            pool.wait_ge(res_y, NE)
            for b in range(B_POOL):
                tiles = slice(b * TB, (b + 1) * TB)
                pool.wait_ge(gathered[b], 16 * TOPK)
                for k in range(TOPK):
                    wait(pool, res_p, b * TOPK + k)
                    pool.tensor_tensor(xr[:, tiles, :], xr[:, tiles, :], gat[:, k, tiles, :], ALU.add).then_inc(res_p, 1)

        @block.scalar
        def _(act):
            act.dma_start(wa[:, 0:3 * C], w_attn).then_inc(w_in, 16)
            act.dma_start(gain[:, :], rows_of(score_gain, 1)).then_inc(w_in, 16)
            act.dma_start(bq[:, :], b_attn[0:C].rearrange("(p a) -> p a", a=1)).then_inc(w_in, 16)
            act.dma_start(bv[:, :], rows_of(row(b_attn[2 * C:3 * C]), C)).then_inc(w_in, 16)
            act.dma_start(wa[:, 3 * C:], gate_w).then_inc(w_in, 16)
            act.dma_start(bgate[:, :], rows_of(row(gate_b), E)).then_inc(w_late, 16)
            act.dma_start(wp[:, :], w_proj).then_inc(w_late, 16)
            act.dma_start(bp[:, :], rows_of(row(b_proj), C)).then_inc(w_late, 16)
            act.wait_ge(ln_v, 3 * B + 1)
            act.activation(lnw[:, 1, :], lnw[:, 0, :], ACT.Sqrt).then_inc(ln_s, 1)
            act.wait_ge(w_in, 16 * 5)
            act.activation(gsign[:, 0:1], gain[:, :], ACT.Sign).then_inc(s_gain, 1)
            act.activation(gsign[:, 1:2], gain[:, :], ACT.Abs).then_inc(s_gain, 1)
            act.wait_ge(s_gain, 1)
            act.activation(bq_s[:, :], bq[:, :], ACT.Copy, scale=gsign[:, 0:1]).then_inc(s_gain, 1)
            act.wait_ge(s_gain, 3)
            with act.Fori(0, B // 2) as i:
                for par in range(2):
                    act.wait_ge(xn_ready[par], i * (1 + par) + (1 + par))
                    act.copy(xnb[par][:, :, :], xn[:, bass.ds(i * 2 * TB + par * TB, TB), :]).then_inc(xnb_ready, 1)
                for par in range(2):
                    act.wait_ge(tr_done, i * 2 + par + 1)
                    act.activation(xnT[par][:, :], flat[par], ACT.Identity,
                                   accum_out=ksum[:, bass.ds(i * 2 + par, 1)]).then_inc(xnT_ready, 1)
                for par in range(2):
                    act.wait_ge(xnT_ready, i * 2 + par + 1)
                    act.copy(xnT_all[:, bass.ds(i * 2 + par, 1), :].rearrange("p a t -> p (a t)"),
                             xnT[par][:, :]).then_inc(xnT_kept, 1)
            for b, n in rounds:
                par = b % 2
                if (b, n) == (B - 1, 0):
                    act.wait_ge(route, ROUTE_PLACES)
                    act.activation(rs[:, 5, :], rs[:, 4, :], ACT.Exp).then_inc(r_exp, 1)
                if n == 0:
                    act.wait_ge(m_mm, b + 1)
                    act.activation(k_off[:, par:par + 1], bank[2][:, 0, 0:1], ACT.Copy, scale=-1.0 / T).then_inc(k_mean, 1)
                    act.wait_ge(k_mm, b + 1)
                    act.wait_ge(k_mean, b + 1)
                    act.activation(qkf[:, par, 1, :], flat[0], ACT.Identity, bias=k_off[:, par:par + 1]).then_inc(qk_f, 1)
                    act.wait_ge(q_mm, b + 1)
                    act.activation(qkf[:, par, 0, :], flat[3], ACT.Identity,
                                   scale=gsign[:, 0:1], bias=bq_s[:, 0:1]).then_inc(qk_f, 1)
                    for stored in v_out:
                        act.wait_ge(stored, 64 * min(b, B // 2) + 1)
                for s in (1, 0):
                    if n == 0:
                        act.wait_ge(qk_f, 2 * b + 4 - s)
                    else:
                        act.wait_ge(part_v[b // 2], 2 * par + 2 - s)
                    act.copy(parts[b][:, s, n, :], rest[par][:, s, :] if n else qkf[:, par, s, :]).then_inc(part_a, 1)
            act.wait_ge(route, ROUTE_STEPS)

            def attention_act(i, first, drain, xs=range(2 * NH)):
                for x in xs:
                    par, h = divmod(x, NH)
                    if not drain:
                        w = HALF - LOW[h // 2]
                        wait(act, u_used, i * (2 * NH) + (x - NU + 1))
                        for r in range(2):
                            act.wait_ge(s_ready, i * (4 * NH) + (2 * x + r + 1))
                            act.activation(U[x % NU][:, r, 0:w], score(2 * x + r)[:, 0:w], ACT.Relu).then_inc(u_ready, 1)
                    for m, (at_h, e) in enumerate(PIECE_OF):
                        if not drain and at_h == h and e == "A":
                            q = i * 2 + par
                            act.wait_ge(p_ready, q * NP + (m + 1))
                            at = 0
                            for g, n, k, w, col in PIECES[m]:
                                last = act.activation(junk[m % NPB][:, at:at + w], piece(m)[:, at:at + w], ACT.Relu,
                                                      accum_out=msum_at(q, g, col))
                                at += w
                            last.then_inc(p_used["A"], 1)
                    y = x - RLAG
                    if not ((y < 0 and first) or (y >= 0 and drain)) and not by_pool(i, y):
                        w = HALF - LOW[y % NH // 2]
                        if DIAG[y % NH // 2]:
                            act.wait_ge(w_mask, i * (2 * ND) + masks_to(y))
                        else:
                            act.wait_ge(w_done, i * (4 * NH) + 2 * (y + 1))
                        act.activation(W[y % NW][:, :, 0:w], W[y % NW][:, :, 0:w], ACT.Square,
                                       ).then_inc(r_ready[y % NW], 1)
                    z = x - AVLAG
                    if z % NH in LAST and not ((z < 0 and first) or (z >= 0 and drain)):
                        q = i * 2 + z // NH
                        act.wait_ge(u_used, i * (2 * NH) + (z + 1))
                        if isinstance(q, int) and q == 0:
                            act.wait_ge(part_out[1], 96)
                        if not (isinstance(q, int) and q < 2):
                            act.wait_ge(y_out[z // NH % 2], 64 * (i + z // NH // 2) + z // NH % 2)
                            act.wait_ge(s_out[z // NH % 2], 32 * (i + z // NH // 2) + z // NH % 2)
                        act.copy(yq[z // NH % 2][:, STEPS[z % NH // 2][0], :], bank[3][:, 0, :]).then_inc(acc_ev, 1)

            def msum_at(q, g, col):
                return msum[:, q, g, col:col + 1] if isinstance(q, int) else msum[:, bass.ds(q, 1), g, col]

            attention_act(0, True, False)
            with act.Fori(1, MID) as i:
                attention_act(i, False, False)

            def ffn_act(i, par, lo, hi):
                o = 1 - par
                if lo >= 0 and hi > 0:
                    act.wait_ge(f["tx"], i + 1)
                    wait(act, f["mx"], i - 1)
                    act.copy(xT[par][:, :], bank[0][:, 0, 0:P]).then_inc(f["cx"], 1)
                if lo >= 2 and hi > -2:
                    act.wait_ge(f["tz"], i - 1)
                    wait(act, f["mg"], i - 3)
                    act.copy(zT[par][:, :, :].rearrange("p a n -> p (a n)"), bank[1][:, 0, 0:F]).then_inc(f["cz"], 1)
                if lo >= 3 and hi > -3:
                    act.wait_ge(f["bg"], i - 2)
                    wait(act, f["ts"], i - 4)
                    act.activation(sg[o][:, :], gb[o][:, :], ACT.Silu).then_inc(f["sl"], 1)
                if lo >= 4 and hi > -4:
                    act.wait_ge(f["ts"], i - 3)
                    wait(act, f["my"], i - 5)
                    act.copy(sT[par][:, :, :].rearrange("p a n -> p (a n)"), bank[2][:, 0, 0:F]).then_inc(f["cs"], 1)

            for i in range(8):
                if i < len(DRAIN):
                    attention_act(MID, False, True, DRAIN[i])
                ffn_act(i, i % 2, i, 1)
            with act.Fori(2, NX // 4) as t:
                for k in range(4):
                    ffn_act(t * 4 + k, k % 2, 9, 1)
            for i in range(NX, NX + 4):
                ffn_act(i, i % 2, 9, NX - i)
            act.wait_ge(proj, NE)
            attention_act(MID, True, False)
            attention_act(MID + 1, False, True)

        @block.tensor
        def _(pe):
            pe.wait_ge(c_pool, 13)
            pe.wait_ge(w_in, 16 * 5)
            with pe.Fori(0, B // 2) as i:
                for par in range(2):
                    pe.wait_ge(xnb_ready, i * 2 + par + 1)
                    pe.wait_ge(v_ev, i * 2 + par + 1)
                    for t in range(TB):
                        last = pe.transpose(flat[par][:, t * P:(t + 1) * P], xnb[par][:, t, :], ident[:, :])
                    last.then_inc(tr_done, 1)
                for par in range(2):
                    pe.wait_ge(xnT_ready, i * 2 + par + 1)
                    for t, n, at in v_banks(par):
                        for k in range(n):
                            last = pe.matmul(at[:, k * VG:(k + 1) * VG], xnT[par][:, (t + k) * P:(t + k + 1) * P],
                                             wa[:, 2 * C:3 * C + E], start=True, stop=True)
                    last.then_inc(v_mm, 1)
            def k_and_q(b):
                pe.wait_ge(xnT_kept, b + 1)
                for s, done in ((1, k_mm), (0, q_mm)):
                    pe.wait_ge(qk_f, b * 2 + 2 - s)
                    if s == 1:
                        pe.matmul(bank[2][:, 0, 0:1], wa[:, C:2 * C], ksum[:, bass.ds(b, 1)],
                                  start=True, stop=True).then_inc(m_mm, 1)
                    for c in range(CH):
                        last = pe.matmul(bank[0 if s else 3][:, c, :], wa[:, s * C:(s + 1) * C],
                                         xnT_all[:, bass.ds(b, 1), c * HALF:(c + 1) * HALF].rearrange("p a t -> p (a t)"),
                                         start=True, stop=True)
                    last.then_inc(done, 1)

            pe.wait_ge(v_ev, B + 2)
            pe.wait_ge(lg_ev, B * len(v_banks(0)))
            k_and_q(0)
            k_and_q(1)
            pe.wait_ge(route, ROUTE_M)
            m_all = rt[4][:, :, :].rearrange("p t e -> p (t e)")
            pe.matmul(bank[1][:, 0, 0:NT * E], tri[:, :], m_all, start=True, stop=True).then_inc(r_mm, 1)
            pe.matmul(bank[1][:, 1, 0:NT * E], ones[:, :], m_all, start=True, stop=True).then_inc(r_mm, 1)
            with pe.Fori(2, B) as b:
                k_and_q(b)

            def attention_pe(i, first, drain, xs=range(2 * NH)):
                for x in xs:
                    par, h = divmod(x, NH)

                    if not drain:
                        c, j = STEPS[h // 2]
                        lo, p = LOW[h // 2], h % 2
                        if h == 0:
                            pe.wait_ge(qk_in[par], (i + 1) * (16 * 5))
                        for r in range(2):
                            wait(pe, w_done, i * (4 * NH) + slot_free(2 * x + r))
                            pe.matmul(score(2 * x + r)[:, 0:HALF - lo], KS[par][:, 2 * p + r, P * j:P * (j + 1)],
                                      QS[par][:, p, HALF * c + lo:HALF * (c + 1)], start=True, stop=True).then_inc(s_ready, 1)
                    for m, (at_h, e) in enumerate(PIECE_OF):
                        if not drain and at_h == h:
                            before = PIECE_OF[m - NPB][1]
                            wait(pe, p_used[before], i * pieces_done(2 * NP - 1, before)
                                 + pieces_done(par * NP + m - NPB, before))
                            at = 0
                            for g, n, k, w, _ in PIECES[m]:
                                last = pe.matmul(piece(m)[:, at:at + w], QS[par][:, g // 2, P * n:P * (n + 1)],
                                                 KS[par][:, g, k:k + w], start=True, stop=True)
                                at += w
                            last.then_inc(p_ready, 1)
                    y, z = x - AVLAG, x - AVLAG - 1
                    has_r = not ((y < 0 and first) or (y >= 0 and drain))
                    has_u = not ((z < 0 and first) or (z >= 0 and drain))
                    if has_r:
                        pe.wait_ge(r_ready[y % NW], i * (2 * NH // NW) + (y // NW + 1))
                    if has_u and z % NH not in LAST:
                        average(z, U[z % NU], True).then_inc(u_used, 1)
                    if has_r:
                        if STEPS[y % NH // 2][1] == 0 and y % 2 == 0:
                            wait(pe, acc_ev, i * (2 * CH) + (y // NH * CH + STEPS[y % NH // 2][0]))
                        average(y, W[y % NW], False).then_inc(r_used, 1)
                        if y % NH in LAST:
                            average(y, U[y % NU], True).then_inc(u_used, 1)

            def average(y, src, of_u):
                c, j = STEPS[y % NH // 2]
                lo = LOW[y % NH // 2]
                for r in range(2):
                    g = y % 2 * 2 + r
                    last = pe.matmul(bank[3][32 * g:32 * g + VW, 0, lo:HALF],
                                     usel[:, :] if of_u else VS[y // NH % 2][:, j, g, :], src[:, r, 0:HALF - lo],
                                     start=(j == 0 and not of_u), stop=(y % NH // 2 in ENDS and of_u),
                                     skip_group_check=True)
                return last

            pe.wait_ge(route, ROUTE_STEPS)
            pe.wait_ge(qk_f, 2 * B + 2)
            attention_pe(0, True, False)
            with pe.Fori(1, MID) as i:
                attention_pe(i, False, False)

            for e in "VA":
                pe.wait_ge(p_used[e], MID * pieces_done(2 * NP - 1, e))
            pe.wait_ge(w_done, MID * 4 * NH)
            pe.wait_ge(w_ffn, 16 * (2 * E + 6))

            def ffn_pe(i, t, k, lo, hi, expert):
                par, o = k % 2, 1 - k % 2
                if hi > 0:
                    pe.wait_ge(fx[k], (t + 1) * 16)
                    wait(pe, f["cx"], i)
                    pe.transpose(bank[0][:, 0, 0:P], xt[k][:, 0:C], ident[:, :]).then_inc(f["tx"], 1)
                if lo >= 1 and hi > -1:
                    e = expert(1)
                    pe.wait_ge(f["cx"], i)
                    wait(pe, f["bx"], i - 1)
                    pe.matmul(bank[0][:, 1, :], xT[o][:, :], w12[:, bass.ds(e, 1), :].rearrange("p a n -> p (a n)"),
                              start=True, stop=True).then_inc(f["mx"], 1)
                if lo >= 2 and hi > -2:
                    pe.wait_ge(f["z"], i - 1)
                    wait(pe, f["cz"], i - 2)
                    for h in range(2):
                        last = pe.transpose(bank[1][:, 0, h * P:(h + 1) * P], zb[par][:, h * P:(h + 1) * P], ident[:, :])
                    last.then_inc(f["tz"], 1)
                if lo >= 3 and hi > -3:
                    e = expert(3)
                    pe.wait_ge(f["cz"], i - 2)
                    wait(pe, f["bg"], i - 3)
                    for h in range(2):
                        last = pe.matmul(bank[1][:, 1, 0:F], zT[o][:, h, :],
                                         wgs[:, bass.ds(e, 1), h, :].rearrange("p a n -> p (a n)"),
                                         start=(h == 0), stop=(h == 1))
                    last.then_inc(f["mg"], 1)
                if lo >= 4 and hi > -4:
                    pe.wait_ge(f["sl"], i - 3)
                    wait(pe, f["cs"], i - 4)
                    for h in range(2):
                        last = pe.transpose(bank[2][:, 0, h * P:(h + 1) * P], sg[par][:, h * P:(h + 1) * P], ident[:, :])
                    last.then_inc(f["ts"], 1)
                if lo >= 5:
                    e = expert(5)
                    pe.wait_ge(f["cs"], i - 4)
                    wait(pe, f["by"], i - 5)
                    for h in range(2):
                        last = pe.matmul(bank[2][:, 1, 0:C], sT[o][:, h, :],
                                         w3s[:, bass.ds(e, 1), h, :].rearrange("p a n -> p (a n)"),
                                         start=(h == 0), stop=(h == 1))
                    last.then_inc(f["my"], 1)

            es = experts(mybir.EngineType.PE, 0)
            for i in range(8):
                if i < len(DRAIN):
                    attention_pe(MID, False, True, DRAIN[i])
                ffn_pe(i, i // 4, i % 4, i, 1, lambda back: es[i - back + 1])
            def ffn_tiles_pe(lo, hi):
                with pe.Fori(lo, hi) as t:
                    es = experts(mybir.EngineType.PE, t)
                    for k in range(4):
                        ffn_pe(t * 4 + k, t, k, 9, 1, lambda back: es[k - back + 5])

            pe.wait_ge(m_row, TB)
            for b in range(NE):
                last = pe.transpose(bank[3][:, 1, b * P:(b + 1) * P], mrow[:, b, :, :].rearrange("p h n -> p (h n)"), ident[:, :])
            last.then_inc(ms_t, 1)
            done = 2
            for b in range(NE):
                until = 13 + 2 * b
                ffn_tiles_pe(done, until)
                done = until
                pe.wait_ge(yn_ready, b + 1)
                if b == 0:
                    pe.wait_ge(acc_ev, 2 * MID * CH)
                    pe.wait_ge(fin_v, 7 * NE)
                wait(pe, res_y, b)
                for t in range(TB):
                    last = pe.matmul(flat[3][:, t * C:(t + 1) * C], yT[b][:, t * P:(t + 1) * P], wp[:, :], start=True, stop=True)
                last.then_inc(proj, 1)
            ffn_tiles_pe(done, NX // 4)
            es = experts(mybir.EngineType.PE, NX // 4)
            for i in range(NX, NX + 5):
                ffn_pe(i, i // 4, i % 4, 9, NX - i, lambda back: es[min(i - NX - back + 5, 7)])

            pe.wait_ge(f["by"], NX)
            pe.wait_ge(res_y, NE)
            attention_pe(MID, True, False)
            attention_pe(MID + 1, False, True)

            pe.wait_ge(m_row, 2 * TB)
            pe.transpose(bank[0][:, 0, 0:P], mrow_l[:, 0, :, :].rearrange("p h n -> p (h n)"), ident[:, :]).then_inc(ms_t, 1)
            pe.wait_ge(fin_v, 7 * B)
            for c in range(CH):
                for n in range(c * TB // CH, (c + 1) * TB // CH):
                    last = pe.matmul(flat[1][:, n * P:(n + 1) * P], sel[:, n, :], fw_l[:, 0, :], start=True, stop=True)
                last.then_inc(rb_mm, 1)
            for c in range(CH):
                pe.wait_ge(yn_ready, NE + c + 1)
                for n in range(c * TB // CH, (c + 1) * TB // CH):
                    last = pe.matmul(flat[2][:, n * C:(n + 1) * C], yT_l[:, n * P:(n + 1) * P], wp[:, :], start=True, stop=True)
                last.then_inc(proj, 1)

        @block.vector
        def _(vec):
            vec.memset(usel[:, :], 0.0).then_inc(c_vec, 1)
            vec.memset(msum[:, :, :, :], 0.0).then_inc(c_vec, 1)
            for par in range(2):
                vec.memset(vb[par][:, :, :, :, :], 0.0).then_inc(c_vec, 1)
            vec.wait_ge(c_vec, 4)
            vec.memset(usel[:, SUM_U:SUM_U + 1], 1.0).then_inc(c_vec, 1)
            for par in range(2):
                vec.memset(vb[par][:, :, :, :, SUM_R], 1.0).then_inc(v_out[par], 1)
                vec.memset(gate_v[:, :], 0.0).then_inc(v_ev, 1)
                vec.wait_ge(v_ev, par + 1)
                vec.memset(rest[par][:, 0, 0:1], 0.0).then_inc(qk_f, 1)

            for n, stored in enumerate((y_out, s_out)):
                vec.memset(k_off[:, n:n + 1], 0.0).then_inc(stored[1], 1)

            with vec.Fori(0, B // 2) as i:
                for par in range(2):
                    first = i * 2 * TB + par * TB
                    vec.wait_ge(x_in[par], i * 16 + 16)
                    for t in range(TB):
                        last = vec.bn_stats(st[:, t, :], x_t[:, bass.ds(first + t, 1), :].rearrange("p a c -> p (a c)"))
                    last.then_inc(ln_v, 1)
                    vec.wait_ge(ln_v, i * 6 + 3 * par + 1)
                    vec.memset(gate_v[:, :], 0.0)
                    for t in range(TB):
                        last = vec.bn_aggr(mvb[:, t, :], st[:, t, :])
                    last.then_inc(ln_v, 1)
                    vec.wait_ge(ln_v, i * 6 + 3 * par + 2)
                    vec.tensor_copy(mv[:, bass.ds(first, TB), :], mvb[:, :, :]).then_inc(ln_v, 1)
            vec.wait_ge(ln_v, 3 * B)
            vec.tensor_scalar(lnw[:, 0, :], mv[:, :, 1], LN_EPS, None, ALU.add).then_inc(ln_v, 1)
            vec.wait_ge(ln_s, 1)
            vec.reciprocal(lnw[:, 2, :], lnw[:, 1, :]).then_inc(ln_v, 1)
            vec.wait_ge(ln_v, 3 * B + 2)
            vec.tensor_tensor(lnw[:, 3, :], lnw[:, 0, :], lnw[:, 2, :], ALU.mult).then_inc(ln_v, 1)
            vec.wait_ge(ln_v, 3 * B + 3)
            vec.tensor_tensor(lnw[:, 4, :], lnw[:, 3, :], lnw[:, 1, :], ALU.add).then_inc(ln_v, 1)
            vec.wait_ge(ln_v, 3 * B + 4)
            vec.reciprocal(lnw[:, 2, :], lnw[:, 4, :]).then_inc(ln_v, 1)
            vec.wait_ge(ln_v, 3 * B + 5)
            vec.tensor_scalar(lnw[:, 3, :], lnw[:, 2, :], 2.0, None, ALU.mult).then_inc(ln_v, 1)
            vec.wait_ge(ln_v, 3 * B + 6)
            vec.tensor_copy(lnw[:, 4, :], mv[:, :, 0]).then_inc(ln_v, 1)
            vec.wait_ge(ln_v, 3 * B + 7)
            with vec.Fori(0, B // 2) as i:
                for t in range(TB):
                    at = bass.ds(i * 2 * TB + t, 1)
                    last = vec.tensor_scalar(xn[:, at, :].rearrange("p a c -> p (a c)"),
                                             x_t[:, at, :].rearrange("p a c -> p (a c)"),
                                             lnw[:, 4, at], lnw[:, 3, at], ALU.subtract, ALU.mult)
                last.then_inc(xn_ready[0], 1)

            vec.wait_ge(w_late, 48)
            vec.wait_ge(w_in, 16 * 5)
            with vec.Fori(0, B // 2) as i:
                for par in range(2):
                    vec.wait_ge(v_mm, i * 2 + par + 1)
                    vec.wait_ge(v_out[par], i * 64 + 1)
                    heads = lambda ap, hq: ap[:, :, hq * 4 * D:(hq + 1) * 4 * D].rearrange("p t (g d) -> p t g d", d=D)
                    for t, n, at in v_banks(par):
                        vec.tensor_tensor(logit[:, bass.ds(i * 2 * TB + (par * TB + t), n), :], v_tiles(at, n)[:, :, C:VG],
                                          bgate[:, :].unsqueeze(1).to_broadcast([P, n, E]), ALU.add).then_inc(lg_ev, 1)
                        for hq in range(4):
                            last = vec.tensor_tensor(vb[par][:, hq, t:t + n, :, 0:D], heads(v_tiles(at, n), hq),
                                                     heads(v_bias[:, 0:n, :], hq), ALU.add)
                    last.then_inc(v_ev, 1)

            steps = [0]

            def chain(*instructions):
                steps[0] += 1
                instructions[-1].then_inc(route, 1)
                vec.wait_ge(route, steps[0])

            by_e = lambda v: v.unsqueeze(2).to_broadcast([P, NT, E])
            e_of = iota8[:, :].unsqueeze(1).to_broadcast([P, NT, E])
            vec.wait_ge(c_pool, 13)
            vec.wait_ge(lg_ev, B * len(v_banks(0)))
            chain(vec.tensor_reduce(rs[:, 0, :], logit[:, :, :], AX, ALU.max))
            chain(vec.tensor_tensor(rt[0][:, :, :], logit[:, :, :], by_e(rs[:, 0, :]), ALU.is_equal))
            chain(vec.tensor_tensor(rt[1][:, :, :], rt[0][:, :, :], e_of, ALU.mult))
            chain(vec.tensor_reduce(rs[:, 1, :], rt[1][:, :, :], AX, ALU.min))
            chain(vec.tensor_tensor(rt[2][:, :, :], e_of, by_e(rs[:, 1, :]), ALU.is_equal))
            chain(vec.scalar_tensor_tensor(rt[0][:, :, :], rt[2][:, :, :], -HUGE, logit[:, :, :], ALU.mult, ALU.add))
            chain(vec.tensor_reduce(rs[:, 2, :], rt[0][:, :, :], AX, ALU.max))
            chain(vec.tensor_tensor(rt[1][:, :, :], rt[0][:, :, :], by_e(rs[:, 2, :]), ALU.is_equal))
            chain(vec.tensor_tensor(rt[3][:, :, :], rt[1][:, :, :], e_of, ALU.mult))
            chain(vec.tensor_reduce(rs[:, 3, :], rt[3][:, :, :], AX, ALU.min))
            chain(vec.tensor_tensor(rt[5][:, :, :], e_of, by_e(rs[:, 3, :]), ALU.is_equal),
                  vec.tensor_tensor(rs[:, 4, :], rs[:, 2, :], rs[:, 0, :], ALU.subtract))
            chain(vec.tensor_tensor(rt[4][:, :, :], rt[2][:, :, :], rt[5][:, :, :], ALU.add))
            assert steps[0] == ROUTE_M, steps
            vec.wait_ge(r_mm, 2)
            total = bank[1][:, 1, 0:NT * E].rearrange("p (t e) -> p t e", e=E)
            chain(vec.tensor_copy(rt[0][:, :, :], total))
            a, b_ = rt[0], rt[1]
            k = 1
            while k < NT:
                chain(vec.tensor_copy(b_[:, 0:k, :], a[:, 0:k, :]),
                      vec.tensor_tensor(b_[:, k:, :], a[:, k:, :], a[:, 0:NT - k, :], ALU.add))
                a, b_, k = b_, a, 2 * k
            upto, free = a, b_
            rank = bank[1][:, 0, 0:NT * E].rearrange("p (t e) -> p t e", e=E)
            chain(vec.tensor_tensor(rc[:, :, :], upto[:, NT - 1, :].unsqueeze(2).to_broadcast([P, E, NT]),
                                    iota_t[:, :].unsqueeze(1).to_broadcast([P, E, NT]), ALU.is_gt),
                  vec.tensor_tensor(rt[3][:, :, :], rank, upto[:, :, :], ALU.add))
            chain(vec.tensor_reduce(rce[:, 0, :], rc[:, :, :], AX, ALU.add),
                  vec.tensor_tensor(free[:, :, :], rt[3][:, :, :], total, ALU.subtract))
            a, k = 0, 1
            for b_ in (1, 2, 3):
                chain(vec.tensor_copy(rce[:, b_, 0:k], rce[:, a, 0:k]),
                      vec.tensor_tensor(rce[:, b_, k:], rce[:, a, k:], rce[:, a, 0:E - k], ALU.add))
                a, k = b_, 2 * k
            chain(vec.tensor_tensor(rce[:, 1, :], rce[:, 3, :], rce[:, 0, :], ALU.subtract),
                  vec.tensor_tensor(rx[:, :, :], iota_x[:, :].unsqueeze(2).to_broadcast([P, NX + 4, E]),
                                    rce[:, 3, :].unsqueeze(1).to_broadcast([P, NX + 4, E]), ALU.is_ge))
            chain(vec.tensor_scalar(rce[:, 2, :], rce[:, 1, :], float(P), None, ALU.mult),
                  vec.tensor_reduce(rxs[:, :], rx[:, :, :], AX, ALU.add))
            chain(vec.tensor_tensor(rt[3][:, :, :], free[:, :, :],
                                    rce[:, 2, :].unsqueeze(1).to_broadcast([P, NT, E]), ALU.add),
                  vec.tensor_scalar(te[:, :], rxs[:, :], float(E - 1), None, ALU.min))
            chain(*[vec.tensor_tensor(to, rt[3][:, :, :], chosen[:, :, :], ALU.mult)
                    for to, chosen in ((rt[0][:, :, :], rt[2]), (rt[1][:, :, :], rt[5]))])
            chain(*[vec.tensor_reduce(rs[:, 7 + k, :], rt[k][:, :, :], AX, ALU.add) for k in range(TOPK)])
            chain(vec.tensor_copy(pos[:, :, :], rs[:, 7:9, :]))
            assert steps[0] == ROUTE_PLACES, steps
            def parts_of(b):
                for s in (1, 0):
                    take_off(vec, b, s, 0)
                for s in (1, 0):
                    vec.wait_ge(part_v[1], 2 * (b % 2) + 2 - s)
                    vec.tensor_copy(parts[b][:, s, 1, :], rest[b % 2][:, s, :]).then_inc(part_b, 1)
                for s in (1, 0):
                    take_off(vec, b, s, 1)

            parts_of(2)
            vec.wait_ge(r_exp, 1)
            chain(vec.tensor_scalar(rs[:, 6, :], rs[:, 5, :], 1.0, None, ALU.add))
            chain(vec.reciprocal(prob[:, :, 0], rs[:, 6, :]))
            chain(vec.tensor_tensor(prob[:, :, 1], rs[:, 5, :], prob[:, :, 0], ALU.mult))
            assert steps[0] == ROUTE_STEPS, steps
            parts_of(3)
            vec.wait_ge(part_p[0], 4)

            def attention_vec(i, masks=0):
                def mask(x):
                    if 0 <= x < masks and DIAG[x % NH // 2]:
                        vec.wait_ge(w_done, i * (4 * NH) + 2 * (x + 1))
                        vec.tensor_tensor(W[x % NW][:, :, 0:P], W[x % NW][:, :, 0:P],
                                          causal[:, :].unsqueeze(1).to_broadcast([P, 2, P]), ALU.mult).then_inc(w_mask, 1)

                for x in range(2 * NH):
                    par, h = divmod(x, NH)
                    for m, (at_h, e) in enumerate(PIECE_OF):
                        if at_h == h and e == "V":
                            q = i * 2 + par
                            vec.wait_ge(p_ready, q * NP + (m + 1))
                            at = 0
                            for g, n, k, w, col in PIECES[m]:
                                to = msum[:, q, g, col:col + 1] if isinstance(q, int) else msum[:, bass.ds(q, 1), g, col]
                                last = vec.tensor_scalar(junk[m % NPB][:, at:at + w], piece(m)[:, at:at + w], 0.0, None,
                                                         ALU.max, ALU.add, accum_out=to)
                                at += w
                            last.then_inc(p_used["V"], 1)
                    w = HALF - LOW[h // 2]
                    wait(vec, r_used, i * (2 * NH) + (x - NW + 1))
                    for r in range(2):
                        vec.wait_ge(u_ready, i * (4 * NH) + (2 * x + r + 1))
                        vec.scalar_tensor_tensor(W[x % NW][:, r, 0:w], score(2 * x + r)[:, 0:w], 0.0,
                                                 U[x % NU][:, r, 0:w], ALU.max, ALU.mult).then_inc(w_done, 1)
                    mask(x - 1)
                mask(2 * NH - 1)

            attention_vec(0, POOL_FROM)
            with vec.Fori(1, MID) as i:
                attention_vec(i)

            vec.wait_ge(s_gain, 2)
            vec.reciprocal(gsign[:, 2:3], gsign[:, 1:2]).then_inc(s_gain, 1)
            vec.wait_ge(s_gain, 4)
            vec.tensor_tensor(gsign[:, 3:4], gsign[:, 2:3], gsign[:, 2:3], ALU.mult).then_inc(s_gain, 1)
            vec.wait_ge(s_gain, 5)
            vec.wait_ge(rows_in, 16)
            vec.wait_ge(w_ffn, 16 * (2 * E + 6))

            def ffn_vec(i, t, k, lo, hi, expert):
                par, o = k % 2, 1 - k % 2
                at_6 = bass.ds(i - 6, 1) if not isinstance(i, int) else slice(i - 6, i - 5)
                if lo >= 1 and hi > -1:
                    e = expert(1)
                    vec.wait_ge(f["mx"], i)
                    vec.tensor_tensor(xb[o][:, :], bank[0][:, 1, :], b12[:, bass.ds(e, 1), :].rearrange("p a n -> p (a n)"),
                                      ALU.add).then_inc(f["bx"], 1)
                    vec.wait_ge(f["bx"], i)
                    wait(vec, f["tz"], i - 2)
                    vec.tensor_tensor(zb[o][:, :], xb[o][:, 0:F], xb[o][:, F:2 * F], ALU.mult).then_inc(f["z"], 1)
                if lo >= 3 and hi > -3:
                    e = expert(3)
                    vec.wait_ge(f["mg"], i - 2)
                    wait(vec, f["sl"], i - 4)
                    vec.tensor_tensor(gb[o][:, :], bank[1][:, 1, 0:F], bgs[:, bass.ds(e, 1), :].rearrange("p a n -> p (a n)"),
                                      ALU.add).then_inc(f["bg"], 1)
                if lo >= 6:
                    vec.wait_ge(f["by"], i - 5)
                    vec.tensor_scalar(yb[k - 2][:, :], yb[k - 2][:, :], row_info[:, at_6, 1:2].rearrange("p a n -> p (a n)"), None,
                                      ALU.mult).then_inc(f["wy"], 1)
                    vec.tensor_copy(row_to[k - 2][:, :], row_info[:, at_6, 0:1].rearrange("p a n -> p (a n)")).then_inc(f["wy"], 1)
                if lo >= 5 and hi > -5:
                    e = expert(5)
                    vec.wait_ge(f["my"], i - 4)
                    wait(vec, fy[k - 1], (t + (k - 9) // 4 + 1) * 16)
                    vec.tensor_tensor(yb[k - 1][:, :], bank[2][:, 1, 0:C], b3s[:, bass.ds(e, 1), :].rearrange("p a n -> p (a n)"),
                                      ALU.add).then_inc(f["by"], 1)

            es = experts(mybir.EngineType.DVE, 0)
            for i in range(8):
                ffn_vec(i, i // 4, i % 4, i, 1, lambda back: es[i - back + 1])
            def ffn_tiles_vec(lo, hi):
                with vec.Fori(lo, hi) as t:
                    es = experts(mybir.EngineType.DVE, t)
                    for k in range(4):
                        ffn_vec(t * 4 + k, t, k, 9, 1, lambda back: es[k - back + 5])

            def scales(at, ms, sums, fw):
                vec.tensor_tensor(fw[:, 1, :], sums[:, 1, :], ms, ALU.add).then_inc(fin_v, 1)
                vec.wait_ge(fin_v, at + 1)
                vec.tensor_scalar(fw[:, 2, :], fw[:, 1, :], 2.0 / T, SMALL, ALU.mult, ALU.add).then_inc(fin_v, 1)
                vec.wait_ge(fin_v, at + 2)
                vec.scalar_tensor_tensor(fw[:, 1, :], fw[:, 2, :], gsign[:, 3:4], fw[:, 2, :], ALU.mult, ALU.mult).then_inc(fin_v, 1)
                vec.wait_ge(fin_v, at + 3)
                vec.tensor_tensor(fw[:, 2, :], fw[:, 1, :], fw[:, 1, :], ALU.mult).then_inc(fin_v, 1)
                vec.wait_ge(fin_v, at + 4)
                vec.scalar_tensor_tensor(fw[:, 1, :], fw[:, 2, :], SMALL, sums[:, 0, :], ALU.mult, ALU.add).then_inc(fin_v, 1)
                vec.wait_ge(fin_v, at + 5)
                vec.tensor_scalar(fw[:, 2, :], fw[:, 1, :], TINY, None, ALU.max).then_inc(fin_v, 1)
                vec.wait_ge(fin_v, at + 6)
                vec.reciprocal(fw[:, 0, :], fw[:, 2, :]).then_inc(fin_v, 1)

            es = experts(mybir.EngineType.DVE, 2)
            for k in range(4):
                ffn_vec(8 + k, 2, k, 9, 1, lambda back: es[k - back + 5])
            done = 3
            for b in range(NE):
                until = 4 + b
                ffn_tiles_vec(done, until)
                done = until
                vec.wait_ge(sums_in, 16 * 2)
                vec.wait_ge(ms_t, 1)
                scales(7 * b, bank[3][:, 1, b * P:(b + 1) * P], sums[:, :, b, :], fw[:, :, b * P:(b + 1) * P])
            for b in range(NE):
                until = 14 + 2 * b
                ffn_tiles_vec(done, until)
                done = until
                vec.wait_ge(proj, b + 1)
                vec.wait_ge(res_x, b + 1)
                some = xr[:, b * TB:(b + 1) * TB, :]
                vec.tensor_tensor(some, flat[3].rearrange("p (t c) -> p t c", c=C), some, ALU.add).then_inc(res_y, 1)
            es = experts(mybir.EngineType.DVE, NX // 4)
            for i in range(NX, NX + 6):
                ffn_vec(i, i // 4, i % 4, 9, NX - i, lambda back: es[min(i - NX - back + 5, 7)])

            attention_vec(MID)

            piece_sums(vec, slice(NE, B), mrow_l, NQ)
            for k in range(TOPK):
                for b in range(B_POOL, B):
                    vec.wait_ge(res_x, B)
                    vec.wait_ge(gathered[b], 16 * TOPK)
                    wait(vec, res_v, (B - B_POOL) * k)
                    tiles = slice(b * TB, (b + 1) * TB)
                    vec.tensor_tensor(xr[:, tiles, :], xr[:, tiles, :], gat[:, k, tiles, :], ALU.add).then_inc(res_v, 1)
            vec.wait_ge(sums_in, 16 * (2 + 2 + 4))
            vec.wait_ge(ms_t, 2)
            scales(7 * NE, bank[0][:, 0, 0:P], sums_l[:, :, 0, :], fw_l)
            vec.wait_ge(y_in[NE], 16 * 9)
            vec.wait_ge(res_v, (B - B_POOL) * TOPK)
            for c in range(CH):
                vec.wait_ge(rb_mm, c + 1)
                half = slice(c * HALF, (c + 1) * HALF)
                vec.tensor_tensor(yT_l[:, half], yT_l[:, half], flat[1][:, half], ALU.mult).then_inc(yn_ready, 1)
            for c in range(CH):
                vec.wait_ge(proj, NE + c + 1)
                some = xr[:, NE * TB + c * TB // CH:NE * TB + (c + 1) * TB // CH, :]
                vec.tensor_tensor(some, bank[2][:, c, :].rearrange("p (t c) -> p t c", c=C), some, ALU.add).then_inc(res_y, 1)


_INS = ["L0_attn_x", "L0_attn_W_attn", "L0_attn_b_attn", "L0_attn_W_proj", "L0_attn_b_proj", "L0_attn_score_gain",
        "L0_ffn_gate_w", "L0_ffn_gate_b", "L0_ffn_w1", "L0_ffn_b1", "L0_ffn_w2", "L0_ffn_b2", "L0_ffn_wg",
        "L0_ffn_bg", "L0_ffn_w3", "L0_ffn_b3"]


def kernel(**inputs):
    import numpy as np
    import concourse.bacc as bacc
    from concourse.bass_utils import run_bass_kernel_spmd

    nc = bacc.Bacc("TRN2", target_bir_lowering=False, num_devices=1)
    arrays, args = {}, []
    for name in _INS:
        a = np.ascontiguousarray(inputs[name])
        if a.size == 1:
            a = a.reshape(1, 1)
        arrays["in_" + name] = a
        args.append(nc.dram_tensor("in_" + name, a.shape, mybir.dt.from_np(a.dtype), kind="ExternalInput").ap())
    shape = np.asarray(inputs["L0_attn_x"]).shape
    args.append(nc.dram_tensor("out", shape, F32, kind="ExternalOutput").ap())
    layer_kernel(nc, *args)
    r = run_bass_kernel_spmd(nc, [arrays], core_ids=[0])
    return r.results[0]["out"]
```
